# Optimizing a Trainium2 kernel written in Bass

```python
import numpy as np
import jax
import jax.numpy as jnp

def _softmax(x, axis=-1):
    return jax.nn.softmax(x, axis=axis)

def _gelu(x):
    return jax.nn.gelu(x, approximate=True)

def _silu(x):
    return jax.nn.silu(x)

def _sigmoid(x):
    return jax.nn.sigmoid(x)

def _layernorm(x, axis=-1, eps=1e-05):
    m = jnp.mean(x, axis=axis, keepdims=True)
    v = jnp.var(x, axis=axis, keepdims=True)
    return (x - m) / jnp.sqrt(v + eps)

def _scatter_add(tgt, idx, src, axis=0):
    return tgt.at[idx].add(src)

def _segment_sum(src, seg, n):
    return jax.ops.segment_sum(src, seg, n)
kernel_name = 'mk_adaln_attn_ffn_d2_seqx_r8_929da6'

def setup_inputs(seed: int=0):
    np.random.seed(seed)
    _w = jnp.asarray

    def _rec_inputs():
        import jax
        import jax.numpy as jnp
        _rk = jax.random.key(seed)
        x = -0.000125 + 0.9999 * jax.random.normal(jax.random.fold_in(_rk, 1), (4, 256, 256), jnp.float32)
        _lenS = 256 - jax.random.randint(jax.random.fold_in(_rk, 7), (4,), 0, max(1, 256 // 4) + 1, jnp.int32)
        _lenS2 = 256 - jax.random.randint(jax.random.fold_in(_rk, 8), (4,), 0, max(1, 256 // 4) + 1, jnp.int32)
        fside_BxSxS_0 = -1.52775e-05 + 0.999936 * jax.random.normal(jax.random.fold_in(_rk, 11), (4, 256, 256), jnp.float32)
        cond_512 = -5.03954e-05 + 1.00559 * jax.random.normal(jax.random.fold_in(_rk, 12), (4, 64), jnp.float32)
        return (x, fside_BxSxS_0, cond_512)
    x, fside_BxSxS_0, cond_512 = _rec_inputs()

    def _L0_cond_setup():
        import jax, jax.numpy as jnp
        from jax import lax
        import numpy as np
        B, T, C, TD = (8, 256, 256, 64)

        def _bi_wkv(r, k, v, w, u, time_emb):
            tf = jax.nn.sigmoid(jnp.sum(time_emb, axis=-1))[:, None, None]
            decay = jnp.exp(-jnp.exp(w.astype(jnp.float32)))[None, :] * (0.5 + 0.5 * tf[:, :, 0])
            kf = k.astype(jnp.float32)
            vf = v.astype(jnp.float32)
            ek = jnp.exp(jnp.minimum(kf, 30.0))
            ekv = ek * vf

            def step(carry, x):
                a, b = carry
                ekv_t, ek_t = x
                a = a * decay + ekv_t
                b = b * decay + ek_t
                return ((a, b), (a, b))
            ekv_t = jnp.swapaxes(ekv, 0, 1)
            ek_t = jnp.swapaxes(ek, 0, 1)
            init = (jnp.zeros_like(decay), jnp.zeros_like(decay))
            _, (nf, df) = lax.scan(step, init, (ekv_t, ek_t))
            _, (nb, db) = lax.scan(step, init, (ekv_t, ek_t), reverse=True)
            nf = jnp.swapaxes(nf, 0, 1)
            df = jnp.swapaxes(df, 0, 1)
            nb = jnp.swapaxes(nb, 0, 1)
            db = jnp.swapaxes(db, 0, 1)
            euk = jnp.exp(jnp.minimum(u.astype(jnp.float32)[None, None, :] + kf, 30.0))
            num = nf + nb - ekv + euk * vf
            den = df + db - ek + euk
            base = jax.nn.sigmoid(r.astype(jnp.float32)) * (num / jnp.maximum(den, 1e-08))
            out = base * (0.8 + 0.2 * tf)
            return out.astype(r.dtype)
        key = jax.random.key(seed)
        ks = jax.random.split(key, 6)
        return {'r': jax.random.normal(ks[0], (B, T, C), dtype=jnp.float32), 'k': jax.random.normal(ks[1], (B, T, C), dtype=jnp.float32), 'v': jax.random.normal(ks[2], (B, T, C), dtype=jnp.float32), 'w': jax.random.normal(ks[3], (C,), dtype=jnp.float32), 'u': jax.random.normal(ks[4], (C,), dtype=jnp.float32), 'time_emb': jax.random.normal(ks[5], (B, TD), dtype=jnp.float32)}
    _L0_cond_all = _L0_cond_setup()
    _L0_cond_in = {k: v for k, v in _L0_cond_all.items() if k in ('w', 'u')}
    del _L0_cond_all

    def _L0_attn_setup():
        import jax, jax.numpy as jnp
        import numpy as np
        B, T, D, N = (2, 128, 256, 16)
        G, C, K = (1, 4, 128)
        DHD = 2
        HD = D // N

        def _rmsnorm_noscale(x, eps=1e-06):
            var = jnp.mean(x * x, axis=-1, keepdims=True)
            return x * jax.lax.rsqrt(var + eps)

        def _cross_head_proj(inputs, qw1, qw2, kw1, kw2, qdd, kdd):
            h_q = jnp.einsum('bnts,btin->btsi', inputs, qw1)
            out = inputs + jnp.einsum('btsi,btin->bnts', h_q, qw2)
            h_k = jnp.einsum('bnts,bsin->btsi', inputs, kw1)
            out = out + jnp.einsum('btsi,bsin->bnts', h_k, kw2)
            out = out + inputs * jnp.transpose(qdd, (0, 2, 1))[:, :, :, None]
            out = out + inputs * jnp.transpose(kdd, (0, 2, 1))[:, :, None, :]
            return out
        key = jax.random.key(seed)
        ks = jax.random.split(key, 6)
        x = jax.random.normal(ks[0], (B, T, D), dtype=jnp.float32)
        w_qkv = jax.random.normal(ks[1], (D, 3 * D), dtype=jnp.float32) * 0.02
        w_o = jax.random.normal(ks[2], (D, D), dtype=jnp.float32) * 0.02
        dw1 = jax.random.normal(ks[3], (D, G, C, K), dtype=jnp.float32) * 0.02
        qkw = jax.random.normal(ks[4], (G, C, K, 2 * DHD, N), dtype=jnp.float32) * 0.02
        dd_w = jax.random.normal(ks[5], (D, G, 4 * N), dtype=jnp.float32) * 0.02
        return {'x': x, 'w_qkv': w_qkv, 'w_o': w_o, 'dw1': dw1, 'qkw': qkw, 'dd_w': dd_w}
    _L0_attn_all = _L0_attn_setup()
    _L0_attn_in = {k: v for k, v in _L0_attn_all.items() if k in ('w_qkv', 'w_o', 'dw1', 'qkw', 'dd_w')}
    del _L0_attn_all

    def _L0_cond2_setup():
        import jax, jax.numpy as jnp
        from jax import lax
        import numpy as np
        B, T, C, TD = (8, 256, 256, 64)

        def _bi_wkv(r, k, v, w, u, time_emb):
            tf = jax.nn.sigmoid(jnp.sum(time_emb, axis=-1))[:, None, None]
            decay = jnp.exp(-jnp.exp(w.astype(jnp.float32)))[None, :] * (0.5 + 0.5 * tf[:, :, 0])
            kf = k.astype(jnp.float32)
            vf = v.astype(jnp.float32)
            ek = jnp.exp(jnp.minimum(kf, 30.0))
            ekv = ek * vf

            def step(carry, x):
                a, b = carry
                ekv_t, ek_t = x
                a = a * decay + ekv_t
                b = b * decay + ek_t
                return ((a, b), (a, b))
            ekv_t = jnp.swapaxes(ekv, 0, 1)
            ek_t = jnp.swapaxes(ek, 0, 1)
            init = (jnp.zeros_like(decay), jnp.zeros_like(decay))
            _, (nf, df) = lax.scan(step, init, (ekv_t, ek_t))
            _, (nb, db) = lax.scan(step, init, (ekv_t, ek_t), reverse=True)
            nf = jnp.swapaxes(nf, 0, 1)
            df = jnp.swapaxes(df, 0, 1)
            nb = jnp.swapaxes(nb, 0, 1)
            db = jnp.swapaxes(db, 0, 1)
            euk = jnp.exp(jnp.minimum(u.astype(jnp.float32)[None, None, :] + kf, 30.0))
            num = nf + nb - ekv + euk * vf
            den = df + db - ek + euk
            base = jax.nn.sigmoid(r.astype(jnp.float32)) * (num / jnp.maximum(den, 1e-08))
            out = base * (0.8 + 0.2 * tf)
            return out.astype(r.dtype)
        key = jax.random.key(seed)
        ks = jax.random.split(key, 6)
        return {'r': jax.random.normal(ks[0], (B, T, C), dtype=jnp.float32), 'k': jax.random.normal(ks[1], (B, T, C), dtype=jnp.float32), 'v': jax.random.normal(ks[2], (B, T, C), dtype=jnp.float32), 'w': jax.random.normal(ks[3], (C,), dtype=jnp.float32), 'u': jax.random.normal(ks[4], (C,), dtype=jnp.float32), 'time_emb': jax.random.normal(ks[5], (B, TD), dtype=jnp.float32)}
    _L0_cond2_all = _L0_cond2_setup()
    _L0_cond2_in = {k: v for k, v in _L0_cond2_all.items() if k in ('w', 'u')}
    del _L0_cond2_all

    def _L0_ffn_setup():
        import jax, jax.numpy as jnp
        import numpy as np
        B, S, H = (2, 256, 256)
        E, K = (16, 4)
        I_MOE, I_SH = (176, 704)
        key = jax.random.key(seed)
        ks = jax.random.split(key, 9)

        def w(k, shape, fan_in):
            return jax.random.normal(k, shape, jnp.float32) * fan_in ** (-0.5)
        return {'hidden_states': jax.random.normal(ks[0], (B, S, H), jnp.float32), 'router_w': w(ks[1], (E, H), H), 'w_gate': w(ks[2], (E, H, I_MOE), H), 'w_up': w(ks[3], (E, H, I_MOE), H), 'w_down': w(ks[4], (E, I_MOE, H), I_MOE), 'sh_gate': w(ks[5], (H, I_SH), H), 'sh_up': w(ks[6], (H, I_SH), H), 'sh_down': w(ks[7], (I_SH, H), I_SH), 'sh_gate_w': w(ks[8], (H, 1), H)}
    _L0_ffn_all = _L0_ffn_setup()
    _L0_ffn_in = {k: v for k, v in _L0_ffn_all.items() if k in ('router_w', 'w_gate', 'w_up', 'w_down', 'sh_gate', 'sh_up', 'sh_down', 'sh_gate_w')}
    del _L0_ffn_all

    def _L1_cond_setup():
        import jax, jax.numpy as jnp
        from jax import lax
        import numpy as np
        B, T, C, TD = (8, 256, 256, 64)

        def _bi_wkv(r, k, v, w, u, time_emb):
            tf = jax.nn.sigmoid(jnp.sum(time_emb, axis=-1))[:, None, None]
            decay = jnp.exp(-jnp.exp(w.astype(jnp.float32)))[None, :] * (0.5 + 0.5 * tf[:, :, 0])
            kf = k.astype(jnp.float32)
            vf = v.astype(jnp.float32)
            ek = jnp.exp(jnp.minimum(kf, 30.0))
            ekv = ek * vf

            def step(carry, x):
                a, b = carry
                ekv_t, ek_t = x
                a = a * decay + ekv_t
                b = b * decay + ek_t
                return ((a, b), (a, b))
            ekv_t = jnp.swapaxes(ekv, 0, 1)
            ek_t = jnp.swapaxes(ek, 0, 1)
            init = (jnp.zeros_like(decay), jnp.zeros_like(decay))
            _, (nf, df) = lax.scan(step, init, (ekv_t, ek_t))
            _, (nb, db) = lax.scan(step, init, (ekv_t, ek_t), reverse=True)
            nf = jnp.swapaxes(nf, 0, 1)
            df = jnp.swapaxes(df, 0, 1)
            nb = jnp.swapaxes(nb, 0, 1)
            db = jnp.swapaxes(db, 0, 1)
            euk = jnp.exp(jnp.minimum(u.astype(jnp.float32)[None, None, :] + kf, 30.0))
            num = nf + nb - ekv + euk * vf
            den = df + db - ek + euk
            base = jax.nn.sigmoid(r.astype(jnp.float32)) * (num / jnp.maximum(den, 1e-08))
            out = base * (0.8 + 0.2 * tf)
            return out.astype(r.dtype)
        key = jax.random.key(seed)
        ks = jax.random.split(key, 6)
        return {'r': jax.random.normal(ks[0], (B, T, C), dtype=jnp.float32), 'k': jax.random.normal(ks[1], (B, T, C), dtype=jnp.float32), 'v': jax.random.normal(ks[2], (B, T, C), dtype=jnp.float32), 'w': jax.random.normal(ks[3], (C,), dtype=jnp.float32), 'u': jax.random.normal(ks[4], (C,), dtype=jnp.float32), 'time_emb': jax.random.normal(ks[5], (B, TD), dtype=jnp.float32)}
    _L1_cond_all = _L1_cond_setup()
    _L1_cond_in = {k: v for k, v in _L1_cond_all.items() if k in ('w', 'u')}
    del _L1_cond_all

    def _L1_attn_setup():
        import jax, jax.numpy as jnp
        import numpy as np
        DIM = 256
        N_HEADS = 32
        N_KV_HEADS = 8
        ROPE_THETA = 10000.0

        def _rope(x, theta):
            B, N, H, D = x.shape
            freq = theta ** (-(jnp.arange(D // 2, dtype=jnp.float32) * (2.0 / D)))
            phase = jnp.arange(N, dtype=jnp.float32)[:, None] * freq[None, :]
            c = jnp.cos(phase)[None, :, None, :]
            s = jnp.sin(phase)[None, :, None, :]
            x0, x1 = (x[..., 0::2], x[..., 1::2])
            return jnp.stack([x0 * c - x1 * s, x0 * s + x1 * c], axis=-1).reshape(B, N, H, D)
        key = jax.random.key(seed)
        k0, k1, k2, k3, k4 = jax.random.split(key, 5)
        B, N = (2, 128)
        kv_dim = DIM // (N_HEADS // N_KV_HEADS)
        return {'x': jax.random.normal(k0, (B, N, DIM), jnp.float32), 'wq': jax.random.normal(k1, (DIM, DIM), jnp.float32) * 0.02, 'wk': jax.random.normal(k2, (DIM, kv_dim), jnp.float32) * 0.02, 'wv': jax.random.normal(k3, (DIM, kv_dim), jnp.float32) * 0.02, 'wo': jax.random.normal(k4, (DIM, DIM), jnp.float32) * 0.02}
    _L1_attn_all = _L1_attn_setup()
    _L1_attn_in = {k: v for k, v in _L1_attn_all.items() if k in ('wq', 'wk', 'wv', 'wo')}
    del _L1_attn_all

    def _L1_cond2_setup():
        import jax, jax.numpy as jnp
        from jax import lax
        import numpy as np
        B, T, C, TD = (8, 256, 256, 64)

        def _bi_wkv(r, k, v, w, u, time_emb):
            tf = jax.nn.sigmoid(jnp.sum(time_emb, axis=-1))[:, None, None]
            decay = jnp.exp(-jnp.exp(w.astype(jnp.float32)))[None, :] * (0.5 + 0.5 * tf[:, :, 0])
            kf = k.astype(jnp.float32)
            vf = v.astype(jnp.float32)
            ek = jnp.exp(jnp.minimum(kf, 30.0))
            ekv = ek * vf

            def step(carry, x):
                a, b = carry
                ekv_t, ek_t = x
                a = a * decay + ekv_t
                b = b * decay + ek_t
                return ((a, b), (a, b))
            ekv_t = jnp.swapaxes(ekv, 0, 1)
            ek_t = jnp.swapaxes(ek, 0, 1)
            init = (jnp.zeros_like(decay), jnp.zeros_like(decay))
            _, (nf, df) = lax.scan(step, init, (ekv_t, ek_t))
            _, (nb, db) = lax.scan(step, init, (ekv_t, ek_t), reverse=True)
            nf = jnp.swapaxes(nf, 0, 1)
            df = jnp.swapaxes(df, 0, 1)
            nb = jnp.swapaxes(nb, 0, 1)
            db = jnp.swapaxes(db, 0, 1)
            euk = jnp.exp(jnp.minimum(u.astype(jnp.float32)[None, None, :] + kf, 30.0))
            num = nf + nb - ekv + euk * vf
            den = df + db - ek + euk
            base = jax.nn.sigmoid(r.astype(jnp.float32)) * (num / jnp.maximum(den, 1e-08))
            out = base * (0.8 + 0.2 * tf)
            return out.astype(r.dtype)
        key = jax.random.key(seed)
        ks = jax.random.split(key, 6)
        return {'r': jax.random.normal(ks[0], (B, T, C), dtype=jnp.float32), 'k': jax.random.normal(ks[1], (B, T, C), dtype=jnp.float32), 'v': jax.random.normal(ks[2], (B, T, C), dtype=jnp.float32), 'w': jax.random.normal(ks[3], (C,), dtype=jnp.float32), 'u': jax.random.normal(ks[4], (C,), dtype=jnp.float32), 'time_emb': jax.random.normal(ks[5], (B, TD), dtype=jnp.float32)}
    _L1_cond2_all = _L1_cond2_setup()
    _L1_cond2_in = {k: v for k, v in _L1_cond2_all.items() if k in ('w', 'u')}
    del _L1_cond2_all

    def _L1_ffn_setup():
        import jax, jax.numpy as jnp
        import numpy as np
        B, S, D = (4, 128, 256)
        H = 512
        NE = 8
        TOPK = 2
        key = jax.random.key(seed)
        ks = jax.random.split(key, 9)
        s = lambda fan_in: 1.0 / np.sqrt(fan_in)
        return {'x': jax.random.normal(ks[0], (B, S, D), dtype=jnp.float32), 'W1': jax.random.normal(ks[1], (NE, D, H), dtype=jnp.float32) * s(D), 'b1': jnp.zeros((NE, H), dtype=jnp.float32), 'W2': jax.random.normal(ks[2], (NE, H, H), dtype=jnp.float32) * s(H), 'b2': jnp.zeros((NE, H), dtype=jnp.float32), 'W3': jax.random.normal(ks[3], (NE, H, D), dtype=jnp.float32) * s(H), 'b3': jnp.zeros((NE, D), dtype=jnp.float32), 'Wg': jax.random.normal(ks[4], (D, NE), dtype=jnp.float32) * s(D), 'bg': jnp.zeros((NE,), dtype=jnp.float32)}
    _L1_ffn_all = _L1_ffn_setup()
    _L1_ffn_in = {k: v for k, v in _L1_ffn_all.items() if k in ('W1', 'b1', 'W2', 'b2', 'W3', 'b3', 'Wg', 'bg')}
    del _L1_ffn_all
    return {'x': x, 'fside_BxSxS_0': fside_BxSxS_0, 'cond_512': cond_512, 'L0_cond_w': _L0_cond_in['w'], 'L0_cond_u': _L0_cond_in['u'], 'L0_attn_w_qkv': _L0_attn_in['w_qkv'], 'L0_attn_w_o': _L0_attn_in['w_o'], 'L0_attn_dw1': _L0_attn_in['dw1'], 'L0_attn_qkw': _L0_attn_in['qkw'], 'L0_attn_dd_w': _L0_attn_in['dd_w'], 'L0_cond2_w': _L0_cond2_in['w'], 'L0_cond2_u': _L0_cond2_in['u'], 'L0_ffn_router_w': _L0_ffn_in['router_w'], 'L0_ffn_w_gate': _L0_ffn_in['w_gate'], 'L0_ffn_w_up': _L0_ffn_in['w_up'], 'L0_ffn_w_down': _L0_ffn_in['w_down'], 'L0_ffn_sh_gate': _L0_ffn_in['sh_gate'], 'L0_ffn_sh_up': _L0_ffn_in['sh_up'], 'L0_ffn_sh_down': _L0_ffn_in['sh_down'], 'L0_ffn_sh_gate_w': _L0_ffn_in['sh_gate_w'], 'L1_cond_w': _L1_cond_in['w'], 'L1_cond_u': _L1_cond_in['u'], 'L1_attn_wq': _L1_attn_in['wq'], 'L1_attn_wk': _L1_attn_in['wk'], 'L1_attn_wv': _L1_attn_in['wv'], 'L1_attn_wo': _L1_attn_in['wo'], 'L1_cond2_w': _L1_cond2_in['w'], 'L1_cond2_u': _L1_cond2_in['u'], 'L1_ffn_W1': _L1_ffn_in['W1'], 'L1_ffn_b1': _L1_ffn_in['b1'], 'L1_ffn_W2': _L1_ffn_in['W2'], 'L1_ffn_b2': _L1_ffn_in['b2'], 'L1_ffn_W3': _L1_ffn_in['W3'], 'L1_ffn_b3': _L1_ffn_in['b3'], 'L1_ffn_Wg': _L1_ffn_in['Wg'], 'L1_ffn_bg': _L1_ffn_in['bg']}

def reference(x, fside_BxSxS_0, cond_512, L0_cond_w, L0_cond_u, L0_attn_w_qkv, L0_attn_w_o, L0_attn_dw1, L0_attn_qkw, L0_attn_dd_w, L0_cond2_w, L0_cond2_u, L0_ffn_router_w, L0_ffn_w_gate, L0_ffn_w_up, L0_ffn_w_down, L0_ffn_sh_gate, L0_ffn_sh_up, L0_ffn_sh_down, L0_ffn_sh_gate_w, L1_cond_w, L1_cond_u, L1_attn_wq, L1_attn_wk, L1_attn_wv, L1_attn_wo, L1_cond2_w, L1_cond2_u, L1_ffn_W1, L1_ffn_b1, L1_ffn_W2, L1_ffn_b2, L1_ffn_W3, L1_ffn_b3, L1_ffn_Wg, L1_ffn_bg):
    import jax
    import jax.numpy as jnp

    def _L0_cond_ref(r, k, v, w, u, time_emb):
        import jax, jax.numpy as jnp
        from jax import lax
        import numpy as np
        B, T, C, TD = (8, 256, 256, 64)

        def _bi_wkv(r, k, v, w, u, time_emb):
            tf = jax.nn.sigmoid(jnp.sum(time_emb, axis=-1))[:, None, None]
            decay = jnp.exp(-jnp.exp(w.astype(jnp.float32)))[None, :] * (0.5 + 0.5 * tf[:, :, 0])
            kf = k.astype(jnp.float32)
            vf = v.astype(jnp.float32)
            ek = jnp.exp(jnp.minimum(kf, 30.0))
            ekv = ek * vf

            def step(carry, x):
                a, b = carry
                ekv_t, ek_t = x
                a = a * decay + ekv_t
                b = b * decay + ek_t
                return ((a, b), (a, b))
            ekv_t = jnp.swapaxes(ekv, 0, 1)
            ek_t = jnp.swapaxes(ek, 0, 1)
            init = (jnp.zeros_like(decay), jnp.zeros_like(decay))
            _, (nf, df) = lax.scan(step, init, (ekv_t, ek_t))
            _, (nb, db) = lax.scan(step, init, (ekv_t, ek_t), reverse=True)
            nf = jnp.swapaxes(nf, 0, 1)
            df = jnp.swapaxes(df, 0, 1)
            nb = jnp.swapaxes(nb, 0, 1)
            db = jnp.swapaxes(db, 0, 1)
            euk = jnp.exp(jnp.minimum(u.astype(jnp.float32)[None, None, :] + kf, 30.0))
            num = nf + nb - ekv + euk * vf
            den = df + db - ek + euk
            base = jax.nn.sigmoid(r.astype(jnp.float32)) * (num / jnp.maximum(den, 1e-08))
            out = base * (0.8 + 0.2 * tf)
            return out.astype(r.dtype)
        return _bi_wkv(r, k, v, w, u, time_emb)

    def _L0_attn_ref(x, w_qkv, w_o, dw1, qkw, dd_w):
        import jax, jax.numpy as jnp
        import numpy as np
        B, T, D, N = (2, 128, 256, 16)
        G, C, K = (1, 4, 128)
        DHD = 2
        HD = D // N

        def _rmsnorm_noscale(x, eps=1e-06):
            var = jnp.mean(x * x, axis=-1, keepdims=True)
            return x * jax.lax.rsqrt(var + eps)

        def _cross_head_proj(inputs, qw1, qw2, kw1, kw2, qdd, kdd):
            h_q = jnp.einsum('bnts,btin->btsi', inputs, qw1)
            out = inputs + jnp.einsum('btsi,btin->bnts', h_q, qw2)
            h_k = jnp.einsum('bnts,bsin->btsi', inputs, kw1)
            out = out + jnp.einsum('btsi,bsin->bnts', h_k, kw2)
            out = out + inputs * jnp.transpose(qdd, (0, 2, 1))[:, :, :, None]
            out = out + inputs * jnp.transpose(kdd, (0, 2, 1))[:, :, None, :]
            return out
        b, t, d = x.shape
        qkv = x @ w_qkv
        q, k, v = jnp.split(qkv, 3, axis=-1)
        q = q.reshape(b, t, N, HD).transpose(0, 2, 1, 3) * HD ** (-0.5)
        k = k.reshape(b, t, N, HD).transpose(0, 2, 1, 3)
        v = v.reshape(b, t, N, HD).transpose(0, 2, 1, 3)
        dw_hidden = jax.nn.gelu(jnp.einsum('btd,dgck->btgck', x, dw1))
        w = jnp.einsum('btgck,gckim->btgcim', dw_hidden, qkw)
        w1, w2 = jnp.split(w, 2, axis=-2)
        w1 = _rmsnorm_noscale(w1)
        pre_qw1, pre_kw1, post_qw1, post_kw1 = (w1[:, :, 0, c] for c in range(4))
        pre_qw2, pre_kw2, post_qw2, post_kw2 = (w2[:, :, 0, c] for c in range(4))
        dd = jnp.tanh(jnp.einsum('btd,dgm->btgm', x, dd_w))[:, :, 0]
        pre_qdd, pre_kdd, post_qdd, post_kdd = jnp.split(dd, 4, axis=-1)
        logits = jnp.einsum('bnth,bnsh->bnts', q, k)
        logits = _cross_head_proj(logits, pre_qw1, pre_qw2, pre_kw1, pre_kw2, pre_qdd, pre_kdd)
        mask = jnp.tril(jnp.ones((t, t), dtype=bool))
        logits = jnp.where(mask, logits, jnp.finfo(jnp.float32).min)
        probs = jax.nn.softmax(logits, axis=-1)
        probs = _cross_head_proj(probs, post_qw1, post_qw2, post_kw1, post_kw2, post_qdd, post_kdd)
        o = jnp.einsum('bnts,bnsh->bnth', probs, v)
        o = o.transpose(0, 2, 1, 3).reshape(b, t, d)
        return o @ w_o.T

    def _L0_cond2_ref(r, k, v, w, u, time_emb):
        import jax, jax.numpy as jnp
        from jax import lax
        import numpy as np
        B, T, C, TD = (8, 256, 256, 64)

        def _bi_wkv(r, k, v, w, u, time_emb):
            tf = jax.nn.sigmoid(jnp.sum(time_emb, axis=-1))[:, None, None]
            decay = jnp.exp(-jnp.exp(w.astype(jnp.float32)))[None, :] * (0.5 + 0.5 * tf[:, :, 0])
            kf = k.astype(jnp.float32)
            vf = v.astype(jnp.float32)
            ek = jnp.exp(jnp.minimum(kf, 30.0))
            ekv = ek * vf

            def step(carry, x):
                a, b = carry
                ekv_t, ek_t = x
                a = a * decay + ekv_t
                b = b * decay + ek_t
                return ((a, b), (a, b))
            ekv_t = jnp.swapaxes(ekv, 0, 1)
            ek_t = jnp.swapaxes(ek, 0, 1)
            init = (jnp.zeros_like(decay), jnp.zeros_like(decay))
            _, (nf, df) = lax.scan(step, init, (ekv_t, ek_t))
            _, (nb, db) = lax.scan(step, init, (ekv_t, ek_t), reverse=True)
            nf = jnp.swapaxes(nf, 0, 1)
            df = jnp.swapaxes(df, 0, 1)
            nb = jnp.swapaxes(nb, 0, 1)
            db = jnp.swapaxes(db, 0, 1)
            euk = jnp.exp(jnp.minimum(u.astype(jnp.float32)[None, None, :] + kf, 30.0))
            num = nf + nb - ekv + euk * vf
            den = df + db - ek + euk
            base = jax.nn.sigmoid(r.astype(jnp.float32)) * (num / jnp.maximum(den, 1e-08))
            out = base * (0.8 + 0.2 * tf)
            return out.astype(r.dtype)
        return _bi_wkv(r, k, v, w, u, time_emb)

    def _L0_ffn_ref(hidden_states, router_w, w_gate, w_up, w_down, sh_gate, sh_up, sh_down, sh_gate_w):
        import jax, jax.numpy as jnp
        import numpy as np
        B, S, H = (2, 256, 256)
        E, K = (16, 4)
        I_MOE, I_SH = (176, 704)
        orig = hidden_states.shape
        h = hidden_states.reshape(-1, orig[-1])
        N = h.shape[0]
        logits = h @ router_w.T
        probs = jax.nn.softmax(logits.astype(jnp.float32), axis=-1)
        top_vals, top_idx = jax.lax.top_k(probs, K)
        top_vals = top_vals / jnp.maximum(top_vals.sum(-1, keepdims=True), 1e-09)
        top_vals = top_vals.astype(h.dtype)
        comb = jnp.zeros((N, E), h.dtype).at[jnp.arange(N)[:, None], top_idx].add(top_vals)
        g = jnp.einsum('nh,ehi->eni', h, w_gate)
        u = jnp.einsum('nh,ehi->eni', h, w_up)
        y = jnp.einsum('eni,eih->enh', jax.nn.silu(g) * u, w_down)
        routed = jnp.einsum('enh,ne->nh', y, comb)
        shared = jax.nn.silu(h @ sh_gate) * (h @ sh_up) @ sh_down
        sg = jax.nn.sigmoid(h @ sh_gate_w)
        return (routed + sg * shared).reshape(orig)

    def _L1_cond_ref(r, k, v, w, u, time_emb):
        import jax, jax.numpy as jnp
        from jax import lax
        import numpy as np
        B, T, C, TD = (8, 256, 256, 64)

        def _bi_wkv(r, k, v, w, u, time_emb):
            tf = jax.nn.sigmoid(jnp.sum(time_emb, axis=-1))[:, None, None]
            decay = jnp.exp(-jnp.exp(w.astype(jnp.float32)))[None, :] * (0.5 + 0.5 * tf[:, :, 0])
            kf = k.astype(jnp.float32)
            vf = v.astype(jnp.float32)
            ek = jnp.exp(jnp.minimum(kf, 30.0))
            ekv = ek * vf

            def step(carry, x):
                a, b = carry
                ekv_t, ek_t = x
                a = a * decay + ekv_t
                b = b * decay + ek_t
                return ((a, b), (a, b))
            ekv_t = jnp.swapaxes(ekv, 0, 1)
            ek_t = jnp.swapaxes(ek, 0, 1)
            init = (jnp.zeros_like(decay), jnp.zeros_like(decay))
            _, (nf, df) = lax.scan(step, init, (ekv_t, ek_t))
            _, (nb, db) = lax.scan(step, init, (ekv_t, ek_t), reverse=True)
            nf = jnp.swapaxes(nf, 0, 1)
            df = jnp.swapaxes(df, 0, 1)
            nb = jnp.swapaxes(nb, 0, 1)
            db = jnp.swapaxes(db, 0, 1)
            euk = jnp.exp(jnp.minimum(u.astype(jnp.float32)[None, None, :] + kf, 30.0))
            num = nf + nb - ekv + euk * vf
            den = df + db - ek + euk
            base = jax.nn.sigmoid(r.astype(jnp.float32)) * (num / jnp.maximum(den, 1e-08))
            out = base * (0.8 + 0.2 * tf)
            return out.astype(r.dtype)
        return _bi_wkv(r, k, v, w, u, time_emb)

    def _L1_attn_ref(x, wq, wk, wv, wo):
        import jax, jax.numpy as jnp
        import numpy as np
        DIM = 256
        N_HEADS = 32
        N_KV_HEADS = 8
        ROPE_THETA = 10000.0

        def _rope(x, theta):
            B, N, H, D = x.shape
            freq = theta ** (-(jnp.arange(D // 2, dtype=jnp.float32) * (2.0 / D)))
            phase = jnp.arange(N, dtype=jnp.float32)[:, None] * freq[None, :]
            c = jnp.cos(phase)[None, :, None, :]
            s = jnp.sin(phase)[None, :, None, :]
            x0, x1 = (x[..., 0::2], x[..., 1::2])
            return jnp.stack([x0 * c - x1 * s, x0 * s + x1 * c], axis=-1).reshape(B, N, H, D)
        B, N, D = x.shape
        H, J = (N_HEADS, N_KV_HEADS)
        hd = D // H
        q = (x @ wq).reshape(B, N, H, hd)
        k = (x @ wk).reshape(B, N, J, hd)
        v = (x @ wv).reshape(B, N, J, hd)
        q = _rope(q, ROPE_THETA)
        k = _rope(k, ROPE_THETA)
        rep = H // J
        k = jnp.repeat(k, rep, axis=2)
        v = jnp.repeat(v, rep, axis=2)
        q = q.transpose(0, 2, 1, 3)
        k = k.transpose(0, 2, 1, 3)
        v = v.transpose(0, 2, 1, 3)
        scores = jnp.einsum('bhqd,bhkd->bhqk', q, k) / jnp.sqrt(jnp.float32(hd))
        causal = jnp.tril(jnp.ones((N, N), dtype=bool))
        scores = jnp.where(causal[None, None], scores, -jnp.inf)
        weight = jax.nn.softmax(scores, axis=-1)
        out = jnp.einsum('bhqk,bhkd->bhqd', weight, v)
        out = out.transpose(0, 2, 1, 3).reshape(B, N, D)
        return out @ wo

    def _L1_cond2_ref(r, k, v, w, u, time_emb):
        import jax, jax.numpy as jnp
        from jax import lax
        import numpy as np
        B, T, C, TD = (8, 256, 256, 64)

        def _bi_wkv(r, k, v, w, u, time_emb):
            tf = jax.nn.sigmoid(jnp.sum(time_emb, axis=-1))[:, None, None]
            decay = jnp.exp(-jnp.exp(w.astype(jnp.float32)))[None, :] * (0.5 + 0.5 * tf[:, :, 0])
            kf = k.astype(jnp.float32)
            vf = v.astype(jnp.float32)
            ek = jnp.exp(jnp.minimum(kf, 30.0))
            ekv = ek * vf

            def step(carry, x):
                a, b = carry
                ekv_t, ek_t = x
                a = a * decay + ekv_t
                b = b * decay + ek_t
                return ((a, b), (a, b))
            ekv_t = jnp.swapaxes(ekv, 0, 1)
            ek_t = jnp.swapaxes(ek, 0, 1)
            init = (jnp.zeros_like(decay), jnp.zeros_like(decay))
            _, (nf, df) = lax.scan(step, init, (ekv_t, ek_t))
            _, (nb, db) = lax.scan(step, init, (ekv_t, ek_t), reverse=True)
            nf = jnp.swapaxes(nf, 0, 1)
            df = jnp.swapaxes(df, 0, 1)
            nb = jnp.swapaxes(nb, 0, 1)
            db = jnp.swapaxes(db, 0, 1)
            euk = jnp.exp(jnp.minimum(u.astype(jnp.float32)[None, None, :] + kf, 30.0))
            num = nf + nb - ekv + euk * vf
            den = df + db - ek + euk
            base = jax.nn.sigmoid(r.astype(jnp.float32)) * (num / jnp.maximum(den, 1e-08))
            out = base * (0.8 + 0.2 * tf)
            return out.astype(r.dtype)
        return _bi_wkv(r, k, v, w, u, time_emb)

    def _L1_ffn_ref(x, W1, b1, W2, b2, W3, b3, Wg, bg):
        import jax, jax.numpy as jnp
        import numpy as np
        B, S, D = (4, 128, 256)
        H = 512
        NE = 8
        TOPK = 2
        gate_logits = jnp.einsum('bsd,dn->bsn', x, Wg) + bg
        gate_weights = jax.nn.softmax(gate_logits, axis=-1)
        topv, topi = jax.lax.top_k(gate_weights, TOPK)
        h = jax.nn.gelu(jnp.einsum('bsd,ndh->nbsh', x, W1) + b1[:, None, None, :], approximate=False)
        h = jax.nn.gelu(jnp.einsum('nbsh,nhf->nbsf', h, W2) + b2[:, None, None, :], approximate=False)
        eo = jnp.einsum('nbsf,nfd->nbsd', h, W3) + b3[:, None, None, :]
        comb = jnp.sum(jax.nn.one_hot(topi, NE, dtype=x.dtype) * topv[..., None], axis=-2)
        out = jnp.einsum('nbsd,bsn->bsd', eo, comb)
        return out
    x = x + _L0_attn_ref(_L0_cond_ref(x, fside_BxSxS_0, fside_BxSxS_0, L0_cond_w, L0_cond_u, cond_512), L0_attn_w_qkv, L0_attn_w_o, L0_attn_dw1, L0_attn_qkw, L0_attn_dd_w)
    x = x + _L0_ffn_ref(_L0_cond2_ref(x, fside_BxSxS_0, fside_BxSxS_0, L0_cond2_w, L0_cond2_u, cond_512), L0_ffn_router_w, L0_ffn_w_gate, L0_ffn_w_up, L0_ffn_w_down, L0_ffn_sh_gate, L0_ffn_sh_up, L0_ffn_sh_down, L0_ffn_sh_gate_w)
    x = x + _L1_attn_ref(_L1_cond_ref(x, fside_BxSxS_0, fside_BxSxS_0, L1_cond_w, L1_cond_u, cond_512), L1_attn_wq, L1_attn_wk, L1_attn_wv, L1_attn_wo)
    x = x + _L1_ffn_ref(_L1_cond2_ref(x, fside_BxSxS_0, fside_BxSxS_0, L1_cond2_w, L1_cond2_u, cond_512), L1_ffn_W1, L1_ffn_b1, L1_ffn_W2, L1_ffn_b2, L1_ffn_W3, L1_ffn_b3, L1_ffn_Wg, L1_ffn_bg)
    return x

_drawn_inputs = setup_inputs


def setup_inputs(seed=0):
    import zlib

    import numpy as np

    out = dict(_drawn_inputs(seed))
    spreads = {'L1_ffn_b1': (0.0, 0.743),
     'L1_ffn_b2': (0.0, 0.46),
     'L1_ffn_b3': (0.0, 0.1),
     'L1_ffn_bg': (0.0, 0.445)}
    factors = {'cond_512': 4.591,
     'L0_cond_w': 4.345,
     'L0_cond_u': 8.0,
     'L0_attn_dw1': 8.0,
     'L0_attn_qkw': 8.0,
     'L0_attn_dd_w': 8.0,
     'L0_ffn_sh_gate_w': 5.401,
     'L1_cond_w': 13.063,
     'L1_cond_u': 25.718,
     'L1_attn_wq': 33.468,
     'L1_attn_wk': 35.526,
     'L1_cond2_u': 4.25}
    for name, (base, spread) in spreads.items():
        noise = np.random.default_rng([zlib.crc32(name.encode()), seed]).standard_normal(out[name].shape)
        drawn = base * np.exp(spread * noise) if base else spread * noise
        out[name] = jnp.asarray(drawn.astype(out[name].dtype))
    for name, factor in factors.items():
        out[name] = (out[name] * factor).astype(out[name].dtype)
    return out
```

```python
from contextlib import ExitStack, contextmanager

import concourse.bass as bass
from concourse import mybir
import numpy as np

F32 = mybir.dt.float32
BF16 = mybir.dt.bfloat16
U32 = mybir.dt.uint32
ALU = mybir.AluOpType
ACT = mybir.ActivationFunctionType
X = mybir.AxisListType.X

P = 128
B, T, C = 4, 256, 256
NT = B * T
CT = C // P
TT = T // P
BANK = 512
N0, HD0 = 16, 16
N1, J1, HD1 = 32, 8, 8
REP = N1 // J1
E0, K0, I0 = 16, 4, 176
SH0 = 704 // I0
EX0 = E0 + SH0
E1, K1, H1 = 8, 2, 512
TAU = NT // P
COND_PRE, COND_PER = 7, 15
OWN0, OWN1, OWN3 = 64, 49, 9
COND_DVE = COND_PRE + 4 * COND_PER
PROJ0, EVA0, EVD0, TAIL0 = 21, 13, 10, 9
CAUSAL = [(0, 0), (1, 0), (1, 1)]
MASKED = -1.0e30


class Steps:

    def __init__(self, eng, own):
        self.eng, self.own, self.n, self.term = eng, own, 0, 0
        self.last = None

    def __call__(self, ins):
        ins.then_inc(self.own, 1)
        self.n += 1
        self.last = (self.own, self.term + self.n)

    def tell(self, ins, sem, value):
        ins.then_inc(sem, 1)
        self.last = (sem, value)

    def settle(self):
        self.eng.wait_ge(*self.last)

    @contextmanager
    def loop(self, count, per):
        before = self.n
        with self.eng.Fori(0, count) as it:
            self.term, self.n = it * per + before, 0
            yield it
            assert self.n == per, f"{self.own}: {self.n} steps in a turn"
        self.term, self.n, self.last = 0, before + count * per, None


def spread(ap, axis, n):
    shape = list(ap.shape)
    return ap.unsqueeze(axis).broadcast_to(shape[:axis] + [n] + shape[axis:])


def build(nc, d, out, phases=5):
    ctx = ExitStack()
    with ctx:
        def sb(name, *shape, dt=F32):
            return ctx.enter_context(nc.sbuf_tensor(name, [P, *shape], dt))

        def sem(name):
            return ctx.enter_context(nc.semaphore(name))

        xT = sb("xT", CT, NT)
        fac = sb("fac", 4, CT, NT)
        hT = sb("hT", CT, NT)
        dec = sb("dec", 4 * CT, B)
        oscale = sb("oscale", B)
        wu = sb("wu", 2, 4, CT)
        small = sb("small", 64)
        ident = sb("ident", P)
        causal = sb("causal", P, dt=BF16)
        identb = sb("identb", P, dt=BF16)
        zerob = sb("zerob", BANK, dt=BF16)
        notfirst = sb("notfirst", T)
        condv = sb("condv", B, 64)
        sig = sb("sig", CT, T)
        xc = sb("xc", CT, T)
        arena = sb("arena", 34 * 1024)
        at = [0]

        def cut(*shape, dt=F32):
            n = int(np.prod(shape))
            a = arena[:, at[0]:at[0] + n]
            at[0] += n
            assert at[0] <= 34 * 1024
            if len(shape) > 1:
                names = "abcdef"[:len(shape)]
                a = a.rearrange(f"p ({' '.join(names)}) -> p {' '.join(names)}",
                                **dict(zip(names, shape)))
            return a

        kT, ek, ekv = cut(CT * NT), cut(CT * NT), cut(CT * NT)
        decays, euk, euv = cut(CT * NT), cut(CT * NT), cut(CT * NT)
        num, den, back = cut(CT * NT), cut(CT * NT), cut(CT * NT)
        at[0] = 0
        wqkv, dw1, qkw, ddw, wo0 = cut(CT, 3 * C), cut(CT, 512), cut(4, 64), cut(CT, 64), cut(CT, C)
        qk, v0 = cut(TT, 2, C), cut(TT, C)
        dd, mixw, sq, ms = cut(TT, 64), cut(TT, 4, 4, N0), cut(TT * 4, 2, N0), cut(TT * 4, 2)
        hid = cut(4, T)
        qs, ks = cut(TT, N0, 2, HD0), cut(TT, N0, 2, HD0)
        qw, kw = cut(TT, 2, C), cut(TT, 2, C)
        vs, vk = cut(TT, N0, 2, HD0), cut(TT, 2, C)
        qsT, ksT, qkT = cut(4, T), cut(4, T), cut(2 * CT, T)
        qT, kTb = qkT[:, 0:CT], qkT[:, CT:]
        qwT, kwT = cut(2 * CT, T), cut(2 * CT, T)
        rankq, rankkT = cut(2, 384), cut(2, 384)
        diag_pre, diag_post = cut(4, TT * 2, P), cut(4, TT * 2, P)
        logit, prob, probT = cut(2, 384), cut(2, 384), cut(2, 384)
        nmax, rsum, rinv = cut(2, 2), cut(2, 2), cut(2, 2)
        mixq, mixk = cut(2, 384), cut(2 * 384)
        mixqT, mixkT = cut(2, 384), cut(2, 384)
        o_tok, o_tmp, oT = cut(TT, C), cut(TT, C), cut(CT, T)
        at[0] = 0
        wr0 = cut(CT, E0 + 1)
        iota = cut(E0)
        lg0, pr0, mx0 = cut(TAU, E0 + 1), cut(TAU, E0), cut(TAU)
        top0, idf0, comb0, oh0 = cut(TAU, 8), cut(TAU, 8), cut(TAU, EX0), cut(TAU, E0)
        wgu, wd = cut(2, CT, 2 * I0), cut(2, 2, C)
        act0, mid0, midT = cut(2, I0), cut(2, I0), cut(2, 2, 512)
        w1qkv, wo1, cosk, sink, rmask = cut(CT, 384), cut(CT, C), cut(TT, 4), cut(TT, 4), cut(REP)
        raw1, rot1, rtmp, v1 = cut(TT, 320), cut(TT, 320), cut(TT, 160), cut(TT, 64)
        krep, q1T, kz = cut(TT, C), cut(CT, T), cut(REP, CT, T)
        prob1, prob1T, nmax1 = cut(2, 384), cut(2, 384), cut(2, 2)
        rsum1, rinv1 = cut(N1, 2), cut(N1, 2)
        o1, o1T = cut(TT, C), cut(CT, T)
        at[0] = 0
        wg1, bg1, sel1 = cut(CT, E1), cut(E1), cut(E1, P)
        lg1, pr1, top1, idf1, comb1 = cut(TAU, E1), cut(TAU, E1), cut(TAU, 8), cut(TAU, 8), cut(TAU, E1)
        oh1, mx1, combT = cut(TAU, E1), cut(TAU), cut(NT)
        iota1 = cut(E1)
        b1, b2, b3, biases = cut(E1, 4), cut(E1, 4), cut(E1, 2), cut(2, 2, 4)
        weight = cut(E1, NT)
        w1e, w2e, w3e = cut(2, CT, H1), cut(2, 4, H1), cut(2, 4, C)
        h1, h2, scaled = cut(2, 4, 512), cut(2, 4, 512), cut(2, 512)
        idx0 = sb("idx0", TAU, 8, dt=U32)

        ps = ctx.enter_context(nc.psum_tensor("ps", [P, 8, BANK], F32))

        ld = {n: sem(f"loaded_{n}") for n in ("cond", "attn0", "moe0", "attn1", "moe1")}
        dve_own, act_own, pool_own = sem("dve_own"), sem("act_own"), sem("pool_own")
        c_dve, c_act, c_pool = sem("cond_dve"), sem("cond_act"), sem("cond_pool")
        sig_ready, xc_ready = sem("sig_ready"), sem("xc_ready")
        projected, evac_a, evac_d = sem("projected"), sem("evacuated_act"), sem("evacuated_dve")
        mix_ready, norm_in, norm_out = sem("mix_ready"), sem("norm_in"), sem("norm_out")
        s_ready, s_read = sem("scores_ready"), sem("scores_read")
        lmax, p_exp, p_norm = sem("logits_max"), sem("probs_exp"), sem("probs_normed")
        h_done = sem("mixed_queries")
        t_ready, t_read, pv_done = sem("probsT_ready"), sem("probsT_read"), sem("pv_done")
        dg_pre, dg_post = sem("diag_pre_ready"), sem("diag_post_ready")
        tail_pe, tail_dve, tail_act = sem("tail_pe"), sem("tail_dve"), sem("tail_act")
        x_done = sem("residual_done")
        h_ready, route_pe, route_dve, route_act = sem("h_ready"), sem("route_pe"), sem("route_dve"), sem("route_act")
        gu_ready, silu_done, mid_done = sem("gate_up_ready"), sem("silu_done"), sem("mid_done")
        midT_ready, midT_done = sem("midT_ready"), sem("midT_done")
        w_in = [sem("expert_weights_0"), sem("expert_weights_1")]
        down_done = sem("down_done")
        y_ready = sem("y_ready")
        w1_in = [sem("expert1_weights_0"), sem("expert1_weights_1")]
        l_ready, l_read = sem("hidden_ready"), sem("hidden_read")
        y1_ready, y1_read = sem("y1_ready"), sem("y1_read")
        stacked, values_ready = sem("stacks_ready"), sem("values_ready")
        proj1_pe, attn1_dve, q1T_ready = sem("attn1_pe"), sem("attn1_dve"), sem("q1T_ready")
        s1_ready, lmax1, p1_exp = sem("scores1_ready"), sem("logits1_max"), sem("probs1_exp")
        t1_ready, t1_read, pv1_done = sem("probs1T_ready"), sem("probs1T_read"), sem("pv1_done")
        bias_ready = sem("bias_ready")
        wb_read, zeroed = sem("weight_rows_read"), sem("zeroed")
        wb_ready, stored = sem("weight_rows_ready"), sem("stored")

        block = ctx.enter_context(nc.Block())

        def turned(u):
            tt, kind = divmod(u, 5)
            return (qsT, ksT, qwT, kwT, qkT)[kind][:, :, tt * P:(tt + 1) * P]

        def turned_bank(u):
            return ps[:, u % 8].rearrange("p (g t) -> p g t", g=4)

        def turn_mid(act, i, u):
            half, q = (u // 4) % 2, u % 4
            act.wait_ge(midT_ready, i * 2 * TAU + u + 1)
            dst = midT[:, half, :, q * P:(q + 1) * P]
            act.activation(dst[:, 0], ps[:, 2 + u % 2, 0:P], ACT.Copy)
            act.activation(dst[0:I0 - P, 1], ps[0:I0 - P, 2 + u % 2, P:2 * P], ACT.Copy).then_inc(midT_done, 1)

        def store(sp):
            need = {1: 0, 2: B, 3: B + 1, 4: 2 * B + 1, 5: 2 * B + 2}[phases]
            if need:
                sp.wait_ge(x_done, need)
            sp.dma_start(out, xT[:]).then_inc(stored, 16)
            sp.wait_ge(stored, 16)

        @block.sync
        def _(sp):
            def load(dst, src, s):
                sp.dma_start(dst, src).then_inc(s, 16)

            load(condv[:], d["cond"].partition_broadcast(P), ld["cond"])
            load(wu[:], d["wu"], ld["cond"])
            load(kT, d["fT"], ld["cond"])
            load(notfirst[:], d["notfirst"], ld["cond"])
            load(xT[:], d["xT"], ld["cond"])
            load(ident[:], d["ident"], ld["cond"])
            load(identb[:], d["identb"], ld["cond"])
            load(causal[:], d["causal"], ld["cond"])
            sp.wait_ge(c_dve, COND_DVE)
            for dst, n in ((wqkv, "wqkv"), (dw1, "dw1"), (qkw, "qkw"), (ddw, "ddw"), (wo0, "wo0")):
                load(dst, d[n], ld["attn0"])
            if phases < 2:
                sp.wait_ge(ld["attn0"], 80)
                return store(sp)
            sp.wait_ge(x_done, B)
            load(wr0, d["wr0"], ld["moe0"])
            load(iota, d["iota"].partition_broadcast(P), ld["moe0"])
            for dst, n in ((w1qkv, "w1qkv"), (wo1, "wo1"), (cosk, "cosk"), (sink, "sink"), (rmask, "rmask")):
                load(dst, d[n], ld["attn1"])

            def expert0(e, slot):
                load(wgu[:, slot], d["wgu"][bass.ds(e, 1)].rearrange("o p k n -> (o p) k n"), w_in[slot])
                load(wd[:, slot, 0], d["wd"][bass.ds(e, 1), 0:P].rearrange("o p n -> (o p) n"), w_in[slot])
                load(wd[0:I0 - P, slot, 1], d["wd"][bass.ds(e, 1), P:I0].rearrange("o p n -> (o p) n"), w_in[slot])

            if phases >= 3:
                expert0(0, 0)
                expert0(1, 1)
                with sp.Fori(1, EX0 // 2) as i:
                    for slot in range(2):
                        sp.wait_ge(down_done, 4 * i + 2 * slot - 2)
                        expert0(2 * i + slot, slot)
            if phases < 4:
                sp.wait_ge(ld["moe0"], 32)
                sp.wait_ge(ld["attn1"], 80)
                return store(sp)
            if phases >= 5:
                sp.wait_ge(x_done, 2 * B + 1)
                load(wg1, d["wg1"], ld["moe1"])
                load(bg1, d["bg1"].partition_broadcast(P), ld["moe1"])
                load(iota1, d["iota"][:, 0:E1].partition_broadcast(P), ld["moe1"])
                load(sel1, d["sel1"], ld["moe1"])
                load(b1, d["b1"], ld["moe1"])
                load(b2, d["b2"], ld["moe1"])
                load(b3, d["b3"], ld["moe1"])

                def expert1(e, slot):
                    for dst, n in ((w1e, "w1"), (w2e, "w2"), (w3e, "w3")):
                        load(dst[:, slot], d[n][bass.ds(e, 1)].rearrange("o p k n -> (o p) k n"), w1_in[slot])

                expert1(0, 0)
                expert1(1, 1)
                with sp.Fori(1, E1 // 2) as i:
                    for slot in range(2):
                        sp.wait_ge(y1_ready, 8 * i + 4 * slot - 4)
                        expert1(2 * i + slot, slot)
            store(sp)

        @block.gpsimd
        def _(pool):
            st = Steps(pool, pool_own)
            st(pool.memset(small[:, 40:42], -0.5))
            pool.memset(zerob[:], 0.0).then_inc(zeroed, 1)
            pool.wait_ge(ld["cond"], 16 * 8)
            pool.wait_ge(c_dve, 4)
            with st.loop(4, 0) as i:
                pool.wait_ge(c_dve, i * COND_PER + 4)
                pool.tensor_tensor(decays.rearrange("p (g t) -> p g t", t=T), spread(notfirst[:], 1, CT * B),
                                   spread(dec[:, bass.ds(i * CT, CT)].rearrange("p a b -> p (a b)"), 2, T),
                                   ALU.mult).then_inc(c_pool, 1)
            if phases < 2:
                return
            with st.loop(B, 0) as b:
                pool.wait_ge(norm_in, b + 1)
                pool.tensor_tensor(ms, ms, spread(small[:, 40:42], 1, TT * 4), ALU.pow).then_inc(norm_out, 1)
                pool.wait_ge(mix_ready, b + 1)

                def diagonals(ring, n, row, i0):
                    w = mixw[:, :, row, i0:i0 + 2, n]
                    return pool.tensor_tensor(ring[:, n % 4].rearrange("p (s i) j -> p s i j", i=2),
                                              spread(spread(ident[:], 1, 2), 1, TT),
                                              spread(w, 3, P), ALU.mult)

                for n in range(N0):
                    if n >= 4:
                        pool.wait_ge(s_ready, b * N0 + n - 3)
                    diagonals(diag_pre, n, 1, 2).then_inc(dg_pre, 1)
                    if n >= 4:
                        pool.wait_ge(pv_done, b * N0 + n - 3)
                    diagonals(diag_post, n, 3, 0).then_inc(dg_post, 1)

        @block.scalar
        def _(act):
            st = Steps(act, act_own)
            act.wait_ge(ld["cond"], 16 * 8)
            st(act.activation(small[:, 16:24], wu[:, 0].rearrange("p i c -> p (i c)"), ACT.Exp))
            st.settle()
            act.activation(small[:, 24:32], small[:, 16:24], ACT.Exp, scale=-1.0).then_inc(c_act, 1)
            act.wait_ge(c_dve, 1)
            act.activation(small[:, 4:8], small[:, 0:4], ACT.Sigmoid).then_inc(c_act, 1)
            act.wait_ge(c_dve, 5)
            act.activation(ek, ek, ACT.Exp).then_inc(c_act, 1)
            with st.loop(4, 0) as i:
                act.wait_ge(c_dve, i * COND_PER + 9)
                act.activation(euk, euk, ACT.Exp).then_inc(c_act, 1)

            def sigmoid_batch(b):
                act.wait_ge(ld["cond"], 16 * 8)
                act.activation(sig[:], xT[:, :, bass.ds(b * T, T)], ACT.Sigmoid).then_inc(sig_ready, 1)

            if phases < 2:
                return
            act.wait_ge(c_dve, COND_DVE)
            with st.loop(B, 0) as b:
                sigmoid_batch(b)
                for tt in range(TT):
                    act.wait_ge(projected, b * PROJ0 + 2 * tt + 2)
                    act.activation(v0[:, tt], ps[:, 1 + 2 * tt, 0:C], ACT.Copy).then_inc(evac_a, 1)
                    act.activation(dd[:, tt], ps[:, 1 + 2 * tt, C:C + 64], ACT.Tanh).then_inc(evac_a, 1)
                for h in range(2):
                    act.wait_ge(projected, b * PROJ0 + 5 + h)
                    act.activation(hid[:, 2 * h:2 * h + 2].rearrange("p c t -> p (c t)"), ps[:, 4 + h],
                                   ACT.Gelu_apprx_tanh).then_inc(evac_a, 1)
                for u in range(0, 10, 2):
                    act.wait_ge(projected, b * PROJ0 + 8 + u)
                    act.activation(turned(u), turned_bank(u), ACT.Copy).then_inc(evac_a, 1)
                act.wait_ge(projected, b * PROJ0 + 19)
                act.activation(rankq[:, 1], ps[:, 3, 0:384], ACT.Copy).then_inc(evac_a, 1)
                act.wait_ge(projected, b * PROJ0 + 21)
                act.activation(rankkT[:, 1], ps[:, 5, 0:384], ACT.Copy).then_inc(evac_a, 1)

                def exps(n):
                    s = n % 2
                    act.wait_ge(lmax, b * N0 + n + 1)
                    if n >= 2:
                        act.wait_ge(h_done, b * N0 + n - 1)
                    act.activation(prob[:, s, 0:P], logit[:, s, 0:P], ACT.Exp, bias=nmax[:, s, 0:1],
                                   accum_out=rsum[:, s, 0:1])
                    act.activation(prob[:, s, P:], logit[:, s, P:], ACT.Exp, bias=nmax[:, s, 1:2],
                                   accum_out=rsum[:, s, 1:2]).then_inc(p_exp, 1)

                def turn_out(n):
                    act.wait_ge(t_ready, b * N0 + n + 1)
                    if n >= 2:
                        act.wait_ge(pv_done, b * N0 + n - 1)
                    act.activation(probT[:, n % 2], ps[:, 2 + n % 2, 0:384], ACT.Copy).then_inc(t_read, 1)

                for k in range(N0 + 1):
                    if k < N0:
                        exps(k)
                    if k >= 1:
                        turn_out(k - 1)
                act.wait_ge(pv_done, b * N0 + N0)
                act.activation(mixk[:, 0:256], ps[:, 6, 0:256], ACT.Copy).then_inc(tail_act, 1)
                act.activation(mixk[:, 256:768], ps[:, 7], ACT.Copy).then_inc(tail_act, 1)
                for i in range(2):
                    act.wait_ge(tail_pe, b * TAIL0 + 3 + i)
                    act.activation(mixkT[:, i], ps[:, 2 + i, 0:384], ACT.Copy).then_inc(tail_act, 1)
            if phases < 3:
                return
            act.wait_ge(x_done, B)
            act.activation(hT[:], xT[:], ACT.Sigmoid).then_inc(route_act, 1)
            act.wait_ge(route_dve, 2)
            act.activation(pr0, pr0, ACT.Exp).then_inc(route_act, 1)
            act.activation(comb0[:, :, E0], lg0[:, :, E0], ACT.Sigmoid).then_inc(route_act, 1)
            with st.loop(EX0 // 2, 0) as i:
                for u in range(2 * TAU):
                    act.wait_ge(gu_ready, i * 2 * TAU + u + 1)
                    if u >= 2:
                        act.wait_ge(mid_done, i * 2 * TAU + u - 1)
                    act.activation(act0[:, u % 2], ps[:, u % 2, 0:I0], ACT.Silu).then_inc(silu_done, 1)
                    if u >= 1:
                        turn_mid(act, i, u - 1)
                turn_mid(act, i, 2 * TAU - 1)
            if phases < 4:
                return
            act.wait_ge(x_done, B + 1)
            with st.loop(B, 0) as b:
                sigmoid_batch(b)
                act.wait_ge(proj1_pe, b * 6 + 3)
                act.activation(q1T.rearrange("p a t -> p (a t)"), ps[:, 2], ACT.Copy).then_inc(q1T_ready, 1)

                def exps1(n):
                    s = n % 2
                    act.wait_ge(lmax1, b * N1 + n + 1)
                    if n >= 2:
                        act.wait_ge(t1_ready, b * N1 + n - 1)
                    act.activation(prob1[:, s, 0:P], ps[:, 4 + s, 0:P], ACT.Exp, bias=nmax1[:, s, 0:1],
                                   scale=HD1 ** -0.5, accum_out=rsum1[:, n, 0:1])
                    act.activation(prob1[:, s, P:], ps[:, 4 + s, P:384], ACT.Exp, bias=nmax1[:, s, 1:2],
                                   scale=HD1 ** -0.5, accum_out=rsum1[:, n, 1:2]).then_inc(p1_exp, 1)

                for n in range(N1):
                    exps1(n)
            if phases < 5:
                return
            act.wait_ge(x_done, 2 * B + 1)
            act.activation(hT[:], xT[:], ACT.Sigmoid).then_inc(route_act, 1)
            act.wait_ge(route_dve, 3)
            act.wait_ge(ld["moe1"], 7 * 16)
            act.activation(pr1, pr1, ACT.Exp).then_inc(route_act, 1)
            with st.loop(E1 // 2, 0) as i:
                act.wait_ge(bias_ready, i + 1)
                for slot in range(2):
                    for half in range(2):
                        for m in range(4):
                            k = slot * 16 + half * 4 + m
                            act.wait_ge(l_ready, i * 32 + k + 1)
                            act.activation(h1[:, half, m], ps[:, k % 4], ACT.Gelu,
                                           bias=biases[:, 0, slot, m:m + 1]).then_inc(l_read, 1)
                    for half in range(2):
                        for m in range(4):
                            k = slot * 16 + 8 + half * 4 + m
                            act.wait_ge(l_ready, i * 32 + k + 1)
                            act.activation(h2[:, half, m], ps[:, k % 4], ACT.Gelu,
                                           bias=biases[:, 1, slot, m:m + 1]).then_inc(l_read, 1)

        @block.vector
        def _(dve):
            st = Steps(dve, dve_own)

            cs = Steps(dve, c_dve)
            dve.wait_ge(ld["cond"], 16 * 8)
            cs(dve.tensor_reduce(small[:, 0:4], condv[:], X, ALU.add))
            dve.wait_ge(c_act, 2)
            cs(dve.tensor_scalar(small[:, 8:12], small[:, 4:8], 0.5, 0.5, ALU.mult, ALU.add))
            cs(dve.tensor_scalar(oscale[:], small[:, 4:8], 0.2, 0.8, ALU.mult, ALU.add))
            cs.settle()
            cs(dve.tensor_tensor(dec[:], spread(small[:, 24:32], 2, B), spread(small[:, 8:12], 1, 4 * CT), ALU.mult))
            cs(dve.tensor_scalar(ek, kT, 30.0, None, ALU.min))
            dve.wait_ge(c_act, 3)
            cs(dve.tensor_tensor(ekv, ek, kT, ALU.mult))
            cs(dve.memset(back[:, CT * NT - 1:], 0.0))
            with cs.loop(4, COND_PER) as i:
                dve.wait_ge(c_dve, i * COND_PER + COND_PRE)
                for c in range(CT):
                    cols = slice(c * NT, (c + 1) * NT)
                    cs(dve.tensor_scalar(euk[:, cols], kT[:, cols], wu[:, 1, bass.ds(i, 1), c], 30.0,
                                         ALU.add, ALU.min))
                dve.wait_ge(c_pool, i + 1)
                end = CT * NT - 1
                cs(dve.tensor_tensor_scan(num, decays, ekv, 0.0, ALU.mult, ALU.add))
                cs(dve.tensor_tensor_scan(back[:, end - 1::-1], ekv[:, end:0:-1], decays[:, end:0:-1], 0.0,
                                          ALU.add, ALU.mult))
                cs.settle()
                cs(dve.tensor_tensor(num, num, back, ALU.add))
                cs(dve.tensor_tensor_scan(den, decays, ek, 0.0, ALU.mult, ALU.add))
                cs.settle()
                cs(dve.tensor_tensor_scan(back[:, end - 1::-1], ek[:, end:0:-1], decays[:, end:0:-1], 0.0,
                                          ALU.add, ALU.mult))
                cs.settle()
                cs(dve.tensor_tensor(den, den, back, ALU.add))
                dve.wait_ge(c_act, i + 4)
                cs(dve.tensor_tensor(euv, euk, kT, ALU.mult))
                cs.settle()
                cs(dve.tensor_tensor(num, num, euv, ALU.add))
                cs(dve.tensor_tensor(den, den, euk, ALU.add))
                cs.settle()
                cs(dve.tensor_scalar(den, den, 1e-8, None, ALU.max))
                cs.settle()
                cs(dve.reciprocal(den, den))
                cs.settle()
                cs(dve.tensor_tensor(num, num, den, ALU.mult))
                cs.settle()
                cs(dve.tensor_tensor(fac[:, bass.ds(i, 1)].rearrange("p i c (b t) -> p (i c) b t", t=T),
                                     num.rearrange("p (c b t) -> p c b t", b=B, t=T),
                                     spread(spread(oscale[:], 2, T), 1, CT), ALU.mult))
            if phases < 2:
                dve.wait_ge(c_dve, COND_DVE)
                dve.wait_ge(ld["attn0"], 80)
                return
            dve.wait_ge(c_dve, COND_DVE)

            def condition_batch(b, which, before):
                dve.wait_ge(sig_ready, before + b + 1)
                st.tell(dve.tensor_tensor(xc[:], sig[:], fac[:, which, :, bass.ds(b * T, T)], ALU.mult),
                        xc_ready, before + b + 1)

            with st.loop(B, OWN0) as b:
                condition_batch(b, 0, 0)
                for tt in range(TT):
                    dve.wait_ge(projected, b * PROJ0 + 2 * tt + 1)
                    st(dve.tensor_scalar(qk[:, tt, 0], ps[:, 2 * tt, 0:C], HD0 ** -0.5, None, ALU.mult))
                    st.tell(dve.tensor_copy(qk[:, tt, 1], ps[:, 2 * tt, C:]), evac_d, b * EVD0 + tt + 1)
                dve.wait_ge(projected, b * PROJ0 + 7)
                flat = mixw.rearrange("p t c i m -> p (t c) i m")
                st.tell(dve.tensor_copy(mixw.rearrange("p t c i m -> p (t c i m)"), ps[:, 6]), evac_d, b * EVD0 + 3)
                st.settle()
                st(dve.tensor_tensor(sq, flat[:, :, 0:2], flat[:, :, 0:2], ALU.mult))
                st.settle()
                st(dve.tensor_reduce(ms, sq, X, ALU.add))
                st.settle()
                st.tell(dve.tensor_scalar(ms, ms, 1.0 / N0, 1e-6, ALU.mult, ALU.add), norm_in, b + 1)
                dve.wait_ge(norm_out, b + 1)
                st.tell(dve.tensor_tensor(flat[:, :, 0:2], flat[:, :, 0:2], spread(ms, 3, N0), ALU.mult),
                        mix_ready, b + 1)
                st.settle()
                dve.wait_ge(evac_a, b * EVA0 + 4)

                def heads(ap):
                    return ap.rearrange("p (n h) -> p n h", h=HD0)

                for tt in range(TT):
                    q, k = heads(qk[:, tt, 0]), heads(qk[:, tt, 1])
                    st(dve.scalar_tensor_tensor(qs[:, tt, :, 0], spread(dd[:, tt, 0:16], 2, HD0), 1.0, q,
                                                ALU.add, ALU.mult))
                    st(dve.tensor_copy(qs[:, tt, :, 1], q))
                    st(dve.tensor_copy(ks[:, tt, :, 0], k))
                    st(dve.tensor_tensor(ks[:, tt, :, 1], k, spread(dd[:, tt, 16:32], 2, HD0), ALU.mult))
                    st(dve.tensor_tensor(qw[:, tt].rearrange("p i (n h) -> p i n h", h=HD0), spread(q, 1, 2),
                                         spread(mixw[:, tt, 0, 0:2], 3, HD0), ALU.mult))
                    st.tell(dve.tensor_tensor(kw[:, tt].rearrange("p i (n h) -> p i n h", h=HD0), spread(k, 1, 2),
                                              spread(mixw[:, tt, 1, 0:2], 3, HD0), ALU.mult),
                            stacked, b * TT + tt + 1)
                for tt in range(TT):
                    v = heads(v0[:, tt])
                    st(dve.tensor_copy(vs[:, tt, :, 0], v))
                    st(dve.tensor_tensor(vs[:, tt, :, 1], v, spread(dd[:, tt, 48:64], 2, HD0), ALU.mult))
                    ins = dve.tensor_tensor(vk[:, tt].rearrange("p i (n h) -> p i n h", h=HD0), spread(v, 1, 2),
                                            spread(mixw[:, tt, 3, 2:4], 3, HD0), ALU.mult)
                    if tt:
                        st.tell(ins, values_ready, b + 1)
                    else:
                        st(ins)
                for u in range(1, 10, 2):
                    dve.wait_ge(projected, b * PROJ0 + 8 + u)
                    st.tell(dve.tensor_copy(turned(u), turned_bank(u)), evac_d, b * EVD0 + 4 + u // 2)
                dve.wait_ge(projected, b * PROJ0 + 18)
                st.tell(dve.tensor_copy(rankq[:, 0], ps[:, 2, 0:384]), evac_d, b * EVD0 + 9)
                dve.wait_ge(projected, b * PROJ0 + 20)
                st.tell(dve.tensor_copy(rankkT[:, 0], ps[:, 4, 0:384]), evac_d, b * EVD0 + 10)
                st.settle()
                dve.wait_ge(evac_a, b * EVA0 + 12)
                tiles = (slice(0, P), slice(P, 384))

                def logits(n):
                    s = n % 2
                    dve.wait_ge(s_ready, b * N0 + n + 1)
                    if n >= 2:
                        dve.wait_ge(p_exp, b * N0 + n - 1)
                    for tt in range(TT):
                        ins = dve.scalar_tensor_tensor(logit[:, s, tiles[tt]], rankq[:, 0, tiles[tt]],
                                                       mixw[:, tt, 0, 2, n:n + 1], ps[:, s, tiles[tt]],
                                                       ALU.mult, ALU.add)
                    st.tell(ins, s_read, b * N0 + n + 1)
                    st.settle()
                    for tt in range(TT):
                        ins = dve.scalar_tensor_tensor(logit[:, s, tiles[tt]], rankq[:, 1, tiles[tt]],
                                                       mixw[:, tt, 0, 3, n:n + 1], logit[:, s, tiles[tt]],
                                                       ALU.mult, ALU.add)
                    st(ins)
                    st.settle()
                    for tt in range(TT):
                        ins = dve.tensor_reduce(nmax[:, s, tt:tt + 1], logit[:, s, tiles[tt]], X, ALU.max, negate=True)
                    st.tell(ins, lmax, b * N0 + n + 1)

                def normalise(n):
                    s = n % 2
                    dve.wait_ge(p_exp, b * N0 + n + 1)
                    st(dve.reciprocal(rinv[:, s], rsum[:, s]))
                    st.settle()
                    for tt in range(TT):
                        ins = dve.tensor_scalar(prob[:, s, tiles[tt]], prob[:, s, tiles[tt]], rinv[:, s, tt:tt + 1],
                                                None, ALU.mult)
                    st.tell(ins, p_norm, b * N0 + n + 1)
                    st.settle()
                    for i in range(2):
                        for tt in range(TT):
                            w = mixw[:, tt, 2, i, n:n + 1]
                            dst = mixq[:, i, tiles[tt]]
                            if n == 0:
                                ins = dve.tensor_scalar(dst, prob[:, s, tiles[tt]], w, None, ALU.mult)
                            else:
                                ins = dve.scalar_tensor_tensor(dst, prob[:, s, tiles[tt]], w, dst, ALU.mult, ALU.add)
                    st.tell(ins, h_done, b * N0 + n + 1)

                for k in range(N0 + 1):
                    if k < N0:
                        logits(k)
                    if k >= 1:
                        normalise(k - 1)

                for i in range(2):
                    dve.wait_ge(tail_pe, b * TAIL0 + 1 + i)
                    st.tell(dve.tensor_copy(mixqT[:, i], ps[:, i, 0:384]), tail_dve, b * 4 + 1 + i)
                dve.wait_ge(tail_pe, b * TAIL0 + 7)
                for tt in range(TT):
                    o = heads(o_tok[:, tt])
                    own = ps[:, 4 + tt].rearrange("p (n e h) -> p e n h", e=2, h=HD0)
                    st(dve.scalar_tensor_tensor(o, spread(dd[:, tt, 32:48], 2, HD0), 1.0, own[:, 0],
                                                ALU.add, ALU.mult))
                    for i in range(2):
                        if i:
                            st.settle()
                        st(dve.tensor_tensor(heads(o_tmp[:, tt]), heads(ps[:, tt, i * C:(i + 1) * C]),
                                             spread(mixw[:, tt, 2, 2 + i], 2, HD0), ALU.mult))
                        st.settle()
                        st(dve.tensor_tensor(o_tok[:, tt], o_tok[:, tt], o_tmp[:, tt], ALU.add))
                    st.settle()
                    st(dve.tensor_tensor(o, o, own[:, 1], ALU.add))
                    st.settle()
                    ins = dve.tensor_tensor(o_tok[:, tt], o_tok[:, tt], ps[:, 2, tt * C:(tt + 1) * C], ALU.add)
                    if tt:
                        st.tell(ins, tail_dve, b * 4 + 3)
                    else:
                        st(ins)
                dve.wait_ge(tail_pe, b * TAIL0 + 8)
                st.tell(dve.tensor_copy(oT.rearrange("p a t -> p (a t)"), ps[:, 3]), tail_dve, b * 4 + 4)
                dve.wait_ge(tail_pe, b * TAIL0 + 9)
                here = xT[:, :, bass.ds(b * T, T)]
                st.tell(dve.tensor_tensor(here, here, ps[:, 4].rearrange("p (m t) -> p m t", m=CT), ALU.add),
                        x_done, b + 1)
            if phases < 3:
                return

            def condition_all(which, act_done, done):
                dve.wait_ge(route_act, act_done)
                st.tell(dve.tensor_tensor(hT[:], hT[:], fac[:, which], ALU.mult), h_ready, done)

            def softmax_rows(lg, pr, mx, told, act_done):
                n = pr.shape[2]
                st(dve.tensor_reduce(mx, lg[:, :, 0:n], X, ALU.max))
                st.settle()
                st.tell(dve.tensor_tensor(pr, lg[:, :, 0:n], spread(mx, 2, n), ALU.subtract), route_dve, told)
                dve.wait_ge(route_act, act_done)
                st(dve.tensor_reduce(mx, pr, X, ALU.add))
                st.settle()
                st(dve.reciprocal(mx, mx))
                st.settle()
                st(dve.tensor_tensor(pr, pr, spread(mx, 2, n), ALU.mult))
                st.settle()

            def choose(pr, top, idf, comb, oh, ia, kk):
                n = pr.shape[2]
                for tau in range(TAU):
                    st(dve.max(top[:, tau], pr[:, tau]))
                st.settle()
                for tau in range(TAU):
                    st(dve.max_index(idx0[:, tau], top[:, tau], pr[:, tau]))
                st.settle()
                st(dve.tensor_copy(idf, idx0[:]))
                st.settle()

            def weigh(top, idf, comb, oh, ia, kk):
                n = oh.shape[2]
                for k in range(kk):
                    st(dve.tensor_tensor(oh, spread(ia, 1, TAU), spread(idf[:, :, k], 2, n), ALU.is_equal))
                    st.settle()
                    st(dve.tensor_tensor(comb if k == 0 else oh, oh, spread(top[:, :, k], 2, n), ALU.mult))
                    st.settle()
                    if k:
                        st(dve.tensor_tensor(comb, comb, oh, ALU.add))
                        st.settle()

            condition_all(1, 1, 1)
            dve.wait_ge(ld["moe0"], 32)
            dve.wait_ge(route_pe, 1)
            st.tell(dve.tensor_copy(lg0, ps[:, 0].rearrange("p (a n) -> p a n", n=64)[:, :, 0:E0 + 1]), route_dve, 1)
            st.settle()
            softmax_rows(lg0, pr0, mx0, 2, 2)
            choose(pr0, top0, idf0, comb0, oh0, iota, K0)
            st(dve.tensor_reduce(mx0, top0[:, :, 0:K0], X, ALU.add))
            st.settle()
            st(dve.tensor_scalar(mx0, mx0, 1e-9, None, ALU.max))
            st.settle()
            st(dve.reciprocal(mx0, mx0))
            st.settle()
            st(dve.tensor_tensor(top0, top0, spread(mx0, 2, 8), ALU.mult))
            st.settle()
            weigh(top0, idf0, comb0[:, :, 0:E0], oh0, iota, K0)
            dve.wait_ge(route_act, 3)
            st(dve.tensor_copy(comb0[:, :, E0 + 1:], spread(comb0[:, :, E0], 2, SH0 - 1)))
            st.settle()
            with st.loop(EX0 // 2, 0) as i:
                for u in range(2 * TAU):
                    slot, tau = divmod(u, TAU)
                    dve.wait_ge(silu_done, i * 2 * TAU + u + 1)
                    if u >= 2:
                        dve.wait_ge(midT_ready, i * 2 * TAU + u - 1)
                    dve.scalar_tensor_tensor(mid0[:, u % 2], ps[:, u % 2, I0:2 * I0],
                                             comb0[:, tau, bass.ds(2 * i + slot, 1)], act0[:, u % 2],
                                             ALU.mult, ALU.mult).then_inc(mid_done, 1)
            dve.wait_ge(y_ready, 1)
            for m in range(CT):
                here = xT[:, m].rearrange("p (a t) -> p a t", a=2)
                ins = dve.tensor_tensor(here, here, ps[:, 4 + 2 * m:6 + 2 * m], ALU.add)
                if m:
                    st.tell(ins, x_done, B + 1)
            if phases < 4:
                return

            with st.loop(B, OWN1) as b:
                condition_batch(b, 2, B)
                dve.wait_ge(ld["attn1"], 80)
                for tt in range(TT):
                    dve.wait_ge(proj1_pe, b * 6 + tt + 1)
                    st(dve.tensor_copy(raw1[:, tt], ps[:, tt, 0:320]))
                    st(dve.tensor_copy(v1[:, tt], ps[:, tt, 320:384]))
                st.settle()
                x0, x1 = (raw1.rearrange("p t (g d e) -> p t g d e", d=4, e=2)[:, :, :, :, e] for e in range(2))
                r0, r1 = (rot1.rearrange("p t (g d e) -> p t g d e", d=4, e=2)[:, :, :, :, e] for e in range(2))
                tmp = rtmp.rearrange("p t (g d) -> p t g d", d=4)
                for tt in range(TT):
                    c, s = spread(cosk[:, tt], 1, 40), spread(sink[:, tt], 1, 40)
                    st(dve.tensor_tensor(tmp[:, tt], x1[:, tt], s, ALU.mult))
                    st(dve.tensor_tensor(r0[:, tt], x0[:, tt], c, ALU.mult))
                    st.settle()
                    st(dve.tensor_tensor(r0[:, tt], r0[:, tt], tmp[:, tt], ALU.subtract))
                    st.settle()
                    st(dve.tensor_tensor(tmp[:, tt], x1[:, tt], c, ALU.mult))
                    st(dve.tensor_tensor(r1[:, tt], x0[:, tt], s, ALU.mult))
                    st.settle()
                    st(dve.tensor_tensor(r1[:, tt], r1[:, tt], tmp[:, tt], ALU.add))
                    st.settle()
                for tt in range(TT):
                    ins = dve.tensor_copy(krep[:, tt].rearrange("p (j r d) -> p j r d", r=REP, d=HD1),
                                          spread(rot1[:, tt, C:].rearrange("p (j d) -> p j d", d=HD1), 2, REP))
                st.tell(ins, attn1_dve, b * 4 + 1)
                dve.wait_ge(proj1_pe, b * 6 + 4)
                for r in range(REP):
                    ins = dve.tensor_scalar(kz[:, r].rearrange("p a t -> p (a t)"), ps[:, 3], rmask[:, r:r + 1],
                                            None, ALU.mult)
                st.tell(ins, attn1_dve, b * 4 + 2)

                def maxima(n):
                    s = n % 2
                    dve.wait_ge(s1_ready, b * N1 + n + 1)
                    for tt in range(TT):
                        ins = dve.tensor_reduce(nmax1[:, s, tt:tt + 1], ps[:, 4 + s, tt * P:P + 2 * tt * P], X,
                                                ALU.max, negate=True)
                    st(ins)
                    st.settle()
                    st.tell(dve.tensor_scalar(nmax1[:, s], nmax1[:, s], HD1 ** -0.5, None, ALU.mult),
                            lmax1, b * N1 + n + 1)

                def turn_out(n):
                    dve.wait_ge(t1_ready, b * N1 + n + 1)
                    if n >= 2:
                        dve.wait_ge(pv1_done, b * N1 + n - 1)
                    st.tell(dve.tensor_copy(prob1T[:, n % 2], ps[:, n % 2, 0:384]), t1_read, b * N1 + n + 1)

                for k in range(N1 + 1):
                    if k < N1:
                        maxima(k)
                    if k >= 1:
                        turn_out(k - 1)
                dve.wait_ge(pv1_done, b * N1 + N1)
                st(dve.reciprocal(rinv1, rsum1))
                st.settle()
                for tt in range(TT):
                    ins = dve.tensor_tensor(o1[:, tt].rearrange("p (n h) -> p n h", h=HD1),
                                            ps[:, 6 + tt, 0:C].rearrange("p (n h) -> p n h", h=HD1),
                                            spread(rinv1[:, :, tt], 2, HD1), ALU.mult)
                st.tell(ins, attn1_dve, b * 4 + 3)
                dve.wait_ge(proj1_pe, b * 6 + 5)
                st.tell(dve.tensor_copy(o1T.rearrange("p a t -> p (a t)"), ps[:, 0]), attn1_dve, b * 4 + 4)
                dve.wait_ge(proj1_pe, b * 6 + 6)
                here = xT[:, :, bass.ds(b * T, T)]
                st.tell(dve.tensor_tensor(here, here, ps[:, 2].rearrange("p (m t) -> p m t", m=CT), ALU.add),
                        x_done, B + b + 2)
            if phases < 5:
                return

            condition_all(3, 4, 2)
            dve.wait_ge(ld["moe1"], 7 * 16)
            dve.wait_ge(route_pe, 2)
            st(dve.tensor_tensor(lg1, ps[:, 0].rearrange("p (a n) -> p a n", n=64)[:, :, 0:E1], spread(bg1, 1, TAU),
                                 ALU.add))
            st.settle()
            softmax_rows(lg1, pr1, mx1, 3, 5)
            choose(pr1, top1, idf1, comb1, oh1, iota1, K1)
            weigh(top1, idf1, comb1, oh1, iota1, K1)
            st.tell(dve.tensor_copy(oh1, comb1), route_dve, 4)
            dve.wait_ge(route_pe, 3)
            st.tell(dve.tensor_copy(combT[0:E1, :].rearrange("p (a t) -> p a t", a=2), ps[0:E1, 1:3]), route_dve, 5)
            for e in range(E1):
                for half in range(2):
                    j = 2 * e + half
                    dve.wait_ge(wb_ready, j + 1)
                    st.tell(dve.tensor_copy(weight[:, e, half * 512:(half + 1) * 512], ps[:, 4 + j % 4]),
                            wb_read, j + 1)
            st.settle()
            with st.loop(E1 // 2, OWN3) as i:
                st(dve.tensor_scalar(biases[:, 0], b1[:, bass.ds(2 * i, 2)], 1.0, None, ALU.mult))
                st.tell(dve.tensor_scalar(biases[:, 1], b2[:, bass.ds(2 * i, 2)], 1.0, None, ALU.mult),
                        bias_ready, i + 1)
                for slot in range(2):
                    for half in range(2):
                        for m in range(CT):
                            y = i * 8 + slot * 4 + half * 2 + m
                            cols = slice(half * 512, (half + 1) * 512)
                            dve.wait_ge(y1_ready, y + 1)
                            st.tell(dve.scalar_tensor_tensor(scaled[:, m], ps[:, 4 + 2 * half + m],
                                                             b3[:, bass.ds(2 * i + slot, 1), m], weight[:, bass.ds(2 * i + slot, 1), cols].rearrange("p o t -> p (o t)"),
                                                             ALU.add, ALU.mult), y1_read, y + 1)
                            st.settle()
                            st(dve.tensor_tensor(xT[:, m, cols], xT[:, m, cols], scaled[:, m], ALU.add))
                            st.settle()
            dve.tensor_copy(small[:, 0:1], xT[:, 0, 0:1]).then_inc(x_done, 1)

        @block.tensor
        def _(pe):
            if phases < 2:
                return

            def mm(o, l, r, start=True, stop=True, shared=False):
                return pe.matmul(o, l, r, start=start, stop=stop, skip_group_check=shared)

            pe.wait_ge(ld["cond"], 16 * 8)
            pe.wait_ge(ld["attn0"], 80)
            with pe.Fori(0, B) as b:
                pe.wait_ge(xc_ready, b + 1)
                for tt in range(TT):
                    tok = slice(tt * P, (tt + 1) * P)
                    for o, w in ((ps[:, 2 * tt], wqkv[:, :, 0:2 * C]), (ps[:, 2 * tt + 1, 0:C], wqkv[:, :, 2 * C:]),
                                 (ps[:, 2 * tt + 1, C:C + 64], ddw)):
                        for k in range(CT):
                            ins = mm(o, xc[:, k, tok], w[:, k], k == 0, k == CT - 1)
                        if w is not ddw and w.shape[2] == C:
                            continue
                        ins.then_inc(projected, 1)
                for c in range(4):
                    for k in range(CT):
                        ins = mm(ps[:, 4 + c // 2, (c % 2) * T:(c % 2 + 1) * T], dw1[:, k, c * P:(c + 1) * P],
                                 xc[:, k], k == 0, k == CT - 1)
                    if c % 2:
                        ins.then_inc(projected, 1)
                pe.wait_ge(evac_a, b * EVA0 + 6)
                for tt in range(TT):
                    for c in range(4):
                        ins = mm(ps[:, 6, tt * 256 + c * 64:tt * 256 + (c + 1) * 64], hid[:, c, tt * P:(tt + 1) * P],
                                 qkw[:, c])
                ins.then_inc(projected, 1)
                for u in range(10):
                    tt, kind = divmod(u, 5)
                    if kind == 0:
                        pe.wait_ge(stacked, b * TT + tt + 1)
                    if u == 8:
                        pe.wait_ge(evac_a, b * EVA0 + 7)
                    if u == 9:
                        pe.wait_ge(evac_d, b * EVD0 + 4)
                    src = (qs[:, tt].rearrange("p n e h -> p (n e h)"), ks[:, tt].rearrange("p n e h -> p (n e h)"),
                           qw[:, tt].rearrange("p i c -> p (i c)"), kw[:, tt].rearrange("p i c -> p (i c)"),
                           qk[:, tt].rearrange("p i c -> p (i c)"))[kind]
                    for g in range(4):
                        ins = pe.transpose(ps[:, u % 8, g * P:(g + 1) * P], src[:, g * P:(g + 1) * P], ident[:])
                    ins.then_inc(projected, 1)
                pe.wait_ge(evac_a, b * EVA0 + 11)
                pe.wait_ge(evac_d, b * EVD0 + 8)
                for i in range(2):
                    for tt in range(TT):
                        for k in range(CT):
                            ins = mm(ps[:, 2 + i, tt * P:P + tt * 2 * P], qwT[:, 2 * i + k, tt * P:(tt + 1) * P],
                                     kTb[:, k, 0:(tt + 1) * P], k == 0, k == CT - 1)
                    ins.then_inc(projected, 1)
                for i in range(2):
                    for s in range(TT):
                        for k in range(CT):
                            ins = mm(ps[:, 4 + i, s * 256:s * 256 + (2 - s) * P], kwT[:, 2 * i + k, s * P:(s + 1) * P],
                                     qT[:, k, s * P:], k == 0, k == CT - 1)
                    ins.then_inc(projected, 1)
                pe.wait_ge(evac_a, b * EVA0 + 13)
                pe.wait_ge(evac_d, b * EVD0 + 10)

                def scores(n):
                    pe.wait_ge(dg_pre, b * N0 + n + 1)
                    if n >= 2:
                        pe.wait_ge(s_read, b * N0 + n - 1)
                    rows, g = slice(32 * (n % 4), 32 * (n % 4) + 32), n // 4
                    o = ps[:, n % 2]
                    mm(o[:, 0:P], qsT[rows, g, 0:P], ksT[rows, g, 0:P], True, False, True)
                    mm(o[:, P:384], qsT[rows, g, P:], ksT[rows, g], False, False, True)
                    for blk in (0, 2):
                        mm(o[:, blk * P:(blk + 1) * P], identb[:], causal[:], False, False, True)
                    for blk, (tt, s) in enumerate(CAUSAL):
                        for i in range(2):
                            ins = mm(o[:, blk * P:(blk + 1) * P], rankkT[:, i, blk * P:(blk + 1) * P],
                                     diag_pre[:, n % 4, 2 * s + i], False, blk == 2 and i == 1, True)
                    ins.then_inc(s_ready, 1)

                def turn(n):
                    pe.wait_ge(p_norm, b * N0 + n + 1)
                    if n >= 2:
                        pe.wait_ge(t_read, b * N0 + n - 1)
                    for blk in range(3):
                        ins = pe.transpose(ps[:, 2 + n % 2, blk * P:(blk + 1) * P],
                                           prob[:, n % 2, blk * P:(blk + 1) * P], ident[:])
                    ins.then_inc(t_ready, 1)

                def values(n):
                    pe.wait_ge(t_read, b * N0 + n + 1)
                    pe.wait_ge(dg_post, b * N0 + n + 1)
                    if n == 0:
                        pe.wait_ge(values_ready, b + 1)
                    pT = probT[:, n % 2]
                    vals = vs.rearrange("p t n e h -> p t n (e h)")
                    mm(ps[:, 4, 32 * n:32 * n + 32], pT[:, 0:P], vals[:, 0, n])
                    mm(ps[:, 5, 32 * n:32 * n + 32], pT[:, P:2 * P], vals[:, 0, n], True, False)
                    mm(ps[:, 5, 32 * n:32 * n + 32], pT[:, 2 * P:], vals[:, 1, n], False, True)
                    d0 = diag_post[:, n % 4, 0:2].rearrange("p i j -> p (i j)")
                    d1 = diag_post[:, n % 4, 2:4].rearrange("p i j -> p (i j)")
                    last = n == N0 - 1
                    mm(ps[:, 6, 0:256], pT[:, 0:P], d0, n == 0, last, True)
                    mm(ps[:, 7, 0:256], pT[:, P:2 * P], d0, n == 0, last, True)
                    mm(ps[:, 7, 256:512], pT[:, 2 * P:], d1, False, last, True).then_inc(pv_done, 1)

                for k in range(N0 + 2):
                    if k < N0:
                        scores(k)
                    if 1 <= k <= N0:
                        turn(k - 1)
                    if k >= 2:
                        values(k - 2)

                pe.wait_ge(h_done, b * N0 + N0)
                pe.wait_ge(s_read, b * N0 + N0)
                for i in range(2):
                    for blk in range(3):
                        ins = pe.transpose(ps[:, i, blk * P:(blk + 1) * P], mixq[:, i, blk * P:(blk + 1) * P], ident[:])
                    ins.then_inc(tail_pe, 1)
                pe.wait_ge(tail_act, b * 4 + 2)
                for i in range(2):
                    for blk in range(3):
                        src = (0, 256, 512)[blk] + i * P
                        ins = pe.transpose(ps[:, 2 + i, blk * P:(blk + 1) * P], mixk[:, src:src + P], ident[:])
                    ins.then_inc(tail_pe, 1)
                pe.wait_ge(tail_dve, b * 4 + 2)
                for tt in range(TT):
                    for i in range(2):
                        for s in range(tt + 1):
                            blk = tt + s
                            ins = mm(ps[:, tt, i * C:(i + 1) * C], mixqT[:, i, blk * P:(blk + 1) * P], v0[:, s],
                                     s == 0, s == tt)
                    ins.then_inc(tail_pe, 1)
                pe.wait_ge(tail_act, b * 4 + 4)
                for tt in range(TT):
                    terms = [(i, s) for i in range(2) for s in range(tt + 1)]
                    for j, (i, s) in enumerate(terms):
                        blk = tt + s
                        ins = mm(ps[:, 2, tt * C:(tt + 1) * C], mixkT[:, i, blk * P:(blk + 1) * P], vk[:, s, i],
                                 j == 0, j == len(terms) - 1)
                ins.then_inc(tail_pe, 1)
                pe.wait_ge(tail_dve, b * 4 + 3)
                for k in range(CT):
                    for tt in range(TT):
                        ins = pe.transpose(ps[:, 3, (k * TT + tt) * P:(k * TT + tt + 1) * P],
                                           o_tok[:, tt, k * P:(k + 1) * P], ident[:])
                ins.then_inc(tail_pe, 1)
                pe.wait_ge(tail_dve, b * 4 + 4)
                for m in range(CT):
                    for k in range(CT):
                        ins = mm(ps[:, 4, m * T:(m + 1) * T], wo0[:, k, m * P:(m + 1) * P], oT[:, k], k == 0, k == CT - 1)
                ins.then_inc(tail_pe, 1)
            if phases < 3:
                return

            def route(w, n, h_done_, banks):
                pe.wait_ge(h_ready, h_done_)
                for tau in range(TAU):
                    for k in range(CT):
                        ins = mm(ps[:, 0, tau * 64:tau * 64 + n], hT[:, k, tau * P:(tau + 1) * P], w[:, k],
                                 k == 0, k == CT - 1)
                ins.then_inc(route_pe, 1)

            pe.wait_ge(ld["moe0"], 32)
            route(wr0, E0 + 1, 1, None)
            pe.wait_ge(route_dve, 1)
            pe.wait_ge(zeroed, 1)
            for m in range(4):
                mm(ps[:, 4 + m], zerob[:, 0:P], zerob[:], True, False, True)
            with pe.Fori(0, EX0 // 2) as i:
                for u in range(2 * TAU + 3):
                    if u < 2 * TAU:
                        slot, tau = divmod(u, TAU)
                        if tau == 0:
                            pe.wait_ge(w_in[slot], 48 * i + 48)
                        if u >= 2:
                            pe.wait_ge(mid_done, i * 2 * TAU + u - 1)
                        for k in range(CT):
                            ins = mm(ps[:, u % 2, 0:2 * I0], hT[:, k, tau * P:(tau + 1) * P], wgu[:, slot, k],
                                     k == 0, k == CT - 1)
                        ins.then_inc(gu_ready, 1)
                    if 1 <= u <= 2 * TAU:
                        v = u - 1
                        pe.wait_ge(mid_done, i * 2 * TAU + v + 1)
                        if v >= 2:
                            pe.wait_ge(midT_done, i * 2 * TAU + v - 1)
                        pe.transpose(ps[:, 2 + v % 2, 0:P], mid0[:, v % 2, 0:P], ident[:])
                        pe.transpose(ps[0:I0 - P, 2 + v % 2, P:2 * P], mid0[:, v % 2, P:I0], ident[:])\
                            .then_inc(midT_ready, 1)
                    if u in (6, 10, 14, 18):
                        n = (u - 6) // 4
                        slot, half = divmod(n, 2)
                        pe.wait_ge(midT_done, i * 2 * TAU + 4 * n + 4)
                        for m in range(CT):
                            mm(ps[:, 4 + 2 * m + half], wd[:, slot, 0, m * P:(m + 1) * P], midT[:, half, 0],
                               False, False, True)
                            ins = mm(ps[:, 4 + 2 * m + half], wd[0:I0 - P, slot, 1, m * P:(m + 1) * P],
                                     midT[0:I0 - P, half, 1], False, False, True)
                        ins.then_inc(down_done, 1)
            for m in range(4):
                ins = mm(ps[:, 4 + m], zerob[:, 0:P], zerob[:], False, True, True)
            ins.then_inc(y_ready, 1)
            if phases < 4:
                return

            pe.wait_ge(ld["attn1"], 80)
            with pe.Fori(0, B) as b:
                pe.wait_ge(xc_ready, B + b + 1)
                for tt in range(TT):
                    for k in range(CT):
                        ins = mm(ps[:, tt, 0:384], xc[:, k, tt * P:(tt + 1) * P], w1qkv[:, k], k == 0, k == CT - 1)
                    ins.then_inc(proj1_pe, 1)
                pe.wait_ge(attn1_dve, b * 4 + 1)
                for src, bank in ((rot1, 2), (krep, 3)):
                    for k in range(CT):
                        for tt in range(TT):
                            ins = pe.transpose(ps[:, bank, (k * TT + tt) * P:(k * TT + tt + 1) * P],
                                               src[:, tt, k * P:(k + 1) * P], ident[:])
                    ins.then_inc(proj1_pe, 1)
                pe.wait_ge(attn1_dve, b * 4 + 2)
                pe.wait_ge(q1T_ready, b + 1)

                def scores(n):
                    m, r = divmod(n, REP)
                    rows, k = slice(32 * (m % 4), 32 * (m % 4) + 32), m // 4
                    if n >= 2:
                        pe.wait_ge(p1_exp, b * N1 + n - 1)
                    o = ps[:, 4 + n % 2]
                    mm(o[:, 0:P], q1T[rows, k, 0:P], kz[rows, r, k, 0:P], True, False, True)
                    mm(o[:, P:384], q1T[rows, k, P:], kz[rows, r, k], False, False, True)
                    mm(o[:, 0:P], identb[:], causal[:], False, False, True)
                    mm(o[:, 256:384], identb[:], causal[:], False, True, True).then_inc(s1_ready, 1)

                def turn(n):
                    pe.wait_ge(p1_exp, b * N1 + n + 1)
                    if n >= 2:
                        pe.wait_ge(t1_read, b * N1 + n - 1)
                    for blk in range(3):
                        ins = pe.transpose(ps[:, n % 2, blk * P:(blk + 1) * P],
                                           prob1[:, n % 2, blk * P:(blk + 1) * P], ident[:])
                    ins.then_inc(t1_ready, 1)

                def values(n):
                    j = n // REP
                    pe.wait_ge(t1_read, b * N1 + n + 1)
                    pT, cols, vj = prob1T[:, n % 2], slice(n * HD1, (n + 1) * HD1), slice(j * HD1, (j + 1) * HD1)
                    mm(ps[:, 6, cols], pT[:, 0:P], v1[:, 0, vj])
                    mm(ps[:, 7, cols], pT[:, P:2 * P], v1[:, 0, vj], True, False)
                    mm(ps[:, 7, cols], pT[:, 2 * P:], v1[:, 1, vj], False, True).then_inc(pv1_done, 1)

                for k in range(N1 + 2):
                    if k < N1:
                        scores(k)
                    if 1 <= k <= N1:
                        turn(k - 1)
                    if k >= 2:
                        values(k - 2)
                pe.wait_ge(attn1_dve, b * 4 + 3)
                for k in range(CT):
                    for tt in range(TT):
                        ins = pe.transpose(ps[:, 0, (k * TT + tt) * P:(k * TT + tt + 1) * P],
                                           o1[:, tt, k * P:(k + 1) * P], ident[:])
                ins.then_inc(proj1_pe, 1)
                pe.wait_ge(attn1_dve, b * 4 + 4)
                for m in range(CT):
                    for k in range(CT):
                        ins = mm(ps[:, 2, m * T:(m + 1) * T], wo1[:, k, m * P:(m + 1) * P], o1T[:, k], k == 0, k == CT - 1)
                ins.then_inc(proj1_pe, 1)
            if phases < 5:
                return

            pe.wait_ge(ld["moe1"], 7 * 16)
            route(wg1, E1, 2, None)
            pe.wait_ge(route_dve, 4)
            for tau in range(TAU):
                ins = pe.transpose(ps[0:E1, 1 + tau // 4, (tau % 4) * P:(tau % 4 + 1) * P], oh1[:, tau], ident[:])
            ins.then_inc(route_pe, 1)
            pe.wait_ge(route_dve, 5)
            for e in range(E1):
                for half in range(2):
                    j = 2 * e + half
                    if j >= 4:
                        pe.wait_ge(wb_read, j - 3)
                    mm(ps[:, 4 + j % 4], sel1[0:E1, e], combT[0:E1, half * 512:(half + 1) * 512]).then_inc(wb_ready, 1)
            pe.wait_ge(wb_read, 2 * E1)
            with pe.Fori(0, E1 // 2) as i:
                for slot in range(2):
                    pe.wait_ge(w1_in[slot], 48 * i + 48)
                    if slot:
                        pe.wait_ge(y1_read, i * 8 + slot * 4)

                    def layer(k0, w, src, nk, width):
                        for half in range(2):
                            for m in range(4):
                                k = k0 + half * 4 + m
                                if k >= 4:
                                    pe.wait_ge(l_read, i * 32 + k - 3)
                                for c in range(nk):
                                    ins = mm(ps[:, k % 4], w[:, slot, c, m * P:(m + 1) * P], src(half, c),
                                             c == 0, c == nk - 1)
                                ins.then_inc(l_ready, 1)
                    layer(slot * 16, w1e, lambda half, c: hT[:, c, half * 512:(half + 1) * 512], CT, H1)
                    pe.wait_ge(l_read, i * 32 + slot * 16 + 8)
                    layer(slot * 16 + 8, w2e, lambda half, c: h1[:, half, c], 4, H1)
                    pe.wait_ge(l_read, i * 32 + slot * 16 + 16)
                    for half in range(2):
                        for m in range(CT):
                            for c in range(4):
                                ins = mm(ps[:, 4 + 2 * half + m], w3e[:, slot, c, m * P:(m + 1) * P], h2[:, half, c],
                                         c == 0, c == 3)
                            ins.then_inc(y1_ready, 1)


INPUTS = ["x", "fside_BxSxS_0", "cond_512"]


def kernel(**inp):
    from concourse import bacc
    from concourse.bass_utils import run_bass_kernel_spmd
    import ml_dtypes

    a = {k: np.asarray(v) for k, v in inp.items()}

    def tiles(w):
        return np.ascontiguousarray(w.reshape(-1, P, w.shape[-1]).transpose(1, 0, 2))

    def stack(w):
        return np.ascontiguousarray(w.reshape(w.shape[0], -1, P, w.shape[-1]).transpose(0, 2, 1, 3))

    def column(v):
        return np.ascontiguousarray(v.reshape(v.shape[0], -1, P).transpose(2, 0, 1))

    w = np.stack([a[n + "_w"] for n in ("L0_cond", "L0_cond2", "L1_cond", "L1_cond2")])
    u = np.stack([a[n + "_u"] for n in ("L0_cond", "L0_cond2", "L1_cond", "L1_cond2")])

    def cut(w):
        return w.reshape(C, SH0, I0).transpose(1, 0, 2)

    gate = np.concatenate([a["L0_ffn_w_gate"], cut(a["L0_ffn_sh_gate"])])
    up = np.concatenate([a["L0_ffn_w_up"], cut(a["L0_ffn_sh_up"])])
    down = np.concatenate([a["L0_ffn_w_down"], a["L0_ffn_sh_down"].reshape(SH0, I0, C)])
    f4 = np.float32
    freq = 10000.0 ** (-(np.arange(HD1 // 2, dtype=f4) * f4(2.0 / HD1)))
    phase = (np.arange(T, dtype=f4)[:, None] * freq.astype(f4)[None, :]).astype(f4)
    s_after_t = np.arange(P)[None, :] > np.arange(P)[:, None]
    arrays = {
        "xT": tiles(a["x"].reshape(NT, C).T), "fT": tiles(a["fside_BxSxS_0"].reshape(NT, C).T).reshape(P, CT * NT),
        "cond": a["cond_512"], "wu": np.ascontiguousarray(np.stack([column(w), column(u)], 1)),
        "notfirst": np.tile((np.arange(T) > 0).astype(f4), (P, 1)),
        "ident": np.eye(P, dtype=f4), "identb": np.eye(P).astype(ml_dtypes.bfloat16),
        "causal": np.where(s_after_t, MASKED, 0.0).astype(ml_dtypes.bfloat16),
        "wqkv": tiles(a["L0_attn_w_qkv"]), "dw1": tiles(a["L0_attn_dw1"].reshape(C, 512)),
        "qkw": np.ascontiguousarray(a["L0_attn_qkw"][0].reshape(4, P, 64).transpose(1, 0, 2)),
        "ddw": tiles(a["L0_attn_dd_w"][:, 0]), "wo0": tiles(a["L0_attn_w_o"].T),
        "wr0": tiles(np.concatenate([a["L0_ffn_router_w"].T, a["L0_ffn_sh_gate_w"]], 1)),
        "iota": np.arange(E0, dtype=f4)[None],
        "wgu": stack(np.concatenate([gate, up], 2)), "wd": np.ascontiguousarray(down),
        "w1qkv": tiles(np.concatenate([a["L1_attn_wq"], a["L1_attn_wk"], a["L1_attn_wv"]], 1)),
        "wo1": tiles(a["L1_attn_wo"]),
        "cosk": tiles(np.cos(phase)), "sink": tiles(np.sin(phase)),
        "rmask": (np.arange(P)[:, None] // HD1 % REP == np.arange(REP)[None, :]).astype(f4),
        "wg1": tiles(a["L1_ffn_Wg"]), "bg1": a["L1_ffn_bg"][None],
        "sel1": np.ascontiguousarray(np.broadcast_to(np.eye(P, E1, dtype=f4)[:, :, None], (P, E1, P))),
        "b1": column(a["L1_ffn_b1"]), "b2": column(a["L1_ffn_b2"]), "b3": column(a["L1_ffn_b3"]),
        "w1": stack(a["L1_ffn_W1"]), "w2": stack(a["L1_ffn_W2"]), "w3": stack(a["L1_ffn_W3"]),
    }
    nc = bacc.Bacc("TRN2", target_bir_lowering=False, num_devices=1)
    d = {k: nc.dram_tensor("in_" + k, v.shape, mybir.dt.from_np(v.dtype), kind="ExternalInput").ap()
         for k, v in arrays.items()}
    out = nc.dram_tensor("out", (P, CT, NT), F32, kind="ExternalOutput").ap()
    build(nc, d, out)
    got = run_bass_kernel_spmd(nc, [{"in_" + k: v for k, v in arrays.items()}], core_ids=[0])
    xT = got.results[0]["out"]
    return np.ascontiguousarray(xT.transpose(1, 0, 2).reshape(C, NT).T).reshape(B, T, C)
```

```python
from contextlib import ExitStack, contextmanager

import concourse.bass as bass
from concourse import mybir
import numpy as np

F32 = mybir.dt.float32
BF16 = mybir.dt.bfloat16
U32 = mybir.dt.uint32
ALU = mybir.AluOpType
ACT = mybir.ActivationFunctionType
X = mybir.AxisListType.X

P = 128
B, T, C = 4, 256, 256
NT = B * T
CT = C // P
TT = T // P
BANK = 512
N0, HD0 = 16, 16
N1, J1, HD1 = 32, 8, 8
REP = N1 // J1
E0, K0, I0 = 16, 4, 176
SH0 = 704 // I0
EX0 = E0 + SH0
E1, K1, H1 = 8, 2, 512
ARENA = 31700
TAU = NT // P
SLICE_OWN = 14
OWN0, OWN1, OWN3 = 76, 54, 9
PROJ0, EVA0, EVD0, TAIL0 = 21, 13, 10, 9
SLICE_EXP = (1, 10)
SLICE_SUMS = (7, 15)
CAUSAL = [(0, 0), (1, 0), (1, 1)]
MASKED = -1.0e30


class Steps:

    def __init__(self, eng, own):
        self.eng, self.own, self.n, self.term = eng, own, 0, 0
        self.last = None

    def __call__(self, ins):
        ins.then_inc(self.own, 1)
        self.n += 1
        self.last = (self.own, self.term + self.n)

    def tell(self, ins, sem, value):
        ins.then_inc(sem, 1)
        self.last = (sem, value)

    def settle(self):
        self.eng.wait_ge(*self.last)

    @contextmanager
    def loop(self, count, per):
        before = self.n
        with self.eng.Fori(0, count) as it:
            self.term, self.n = it * per + before, 0
            yield it
            assert self.n == per, f"{self.own}: {self.n} steps in a turn"
        self.term, self.n, self.last = 0, before + count * per, None


def spread(ap, axis, n):
    shape = list(ap.shape)
    return ap.unsqueeze(axis).broadcast_to(shape[:axis] + [n] + shape[axis:])


def build(nc, d, out, phases=5):
    ctx = ExitStack()
    with ctx:
        def sb(name, *shape, dt=F32):
            return ctx.enter_context(nc.sbuf_tensor(name, [P, *shape], dt))

        def sem(name):
            return ctx.enter_context(nc.semaphore(name))

        xT = sb("xT", CT, NT)
        fac = sb("fac", 4, CT, NT)
        kT, ek, ekv = sb("kT", CT, NT), sb("ek", CT, NT), sb("ekv", CT, NT)
        euk, euv, num, den, backn, backd = (sb(n, CT, T) for n in ("euk", "euv", "num", "den", "backn", "backd"))
        dec = sb("dec", 4 * CT, B)
        oscale = sb("oscale", B)
        wu = sb("wu", 2, 4, CT)
        small = sb("small", 64)
        ident = sb("ident", P)
        causal = sb("causal", P, dt=BF16)
        identb = sb("identb", P, dt=BF16)
        zerob = sb("zerob", BANK, dt=BF16)
        condv = sb("condv", B, 64)
        sig = sb("sig", CT, T)
        xc = sb("xc", CT, T)
        arena = sb("arena", ARENA)
        at = [0]

        def cut(*shape, dt=F32):
            n = int(np.prod(shape))
            a = arena[:, at[0]:at[0] + n]
            at[0] += n
            assert at[0] <= ARENA
            if len(shape) > 1:
                names = "abcdef"[:len(shape)]
                a = a.rearrange(f"p ({' '.join(names)}) -> p {' '.join(names)}",
                                **dict(zip(names, shape)))
            return a

        at[0] = 0
        wqkv, dw1, qkw, ddw, wo0 = cut(CT, 3 * C), cut(CT, 512), cut(4, 64), cut(CT, 64), cut(CT, C)
        qk, v0 = cut(TT, 2, C), cut(TT, C)
        dd, mixw, sq, ms = cut(TT, 64), cut(TT, 4, 4, N0), cut(TT * 4, 2, N0), cut(TT * 4, 2)
        hid = cut(4, T)
        qs_at = at[0]
        qs, ks = cut(TT, N0, 2, HD0), cut(TT, N0, 2, HD0)
        owT = arena[:, qs_at:qs_at + 4 * T].rearrange("p (g t) -> p g t", g=4)
        qw, kw = cut(TT, 2, C), cut(TT, 2, C)
        vs, vk = cut(TT, N0, 2, HD0), cut(TT, 2, C)
        qsT, ksT, qkT = cut(4, T), cut(4, T), cut(2 * CT, T)
        qT, kTb = qkT[:, 0:CT], qkT[:, CT:]
        qwT, kwT = cut(2 * CT, T), cut(2 * CT, T)
        rankq, rankkT = cut(2, 384), cut(2, 384)
        diag_pre, diag_post = cut(4, TT * 2, P), cut(4, TT * 2, P)
        logit, prob, probT = cut(2, 384), cut(3, 384), cut(2, 384)
        nmax, rsum, rinv = cut(2, 2), cut(2, 2), cut(2, 2)
        mixq, mixk = cut(2, 384), cut(2 * 384)
        mixqT, mixkT = cut(2, 384), cut(2, 384)
        o_tok, o_tmp, oT = cut(TT, C), cut(TT, C), cut(CT, T)
        at[0] = 0
        hT = cut(CT, NT)
        hT_words = at[0]
        wr0 = cut(CT, E0 + 1)
        iota = cut(E0)
        lg0, pr0, mx0 = cut(TAU, E0 + 1), cut(TAU, E0), cut(TAU)
        top0, idf0, comb0, oh0 = cut(TAU, 8), cut(TAU, 8), cut(TAU, EX0), cut(TAU, E0)
        wgu, wd = cut(2, CT, 2 * I0), cut(2, 2, C)
        act0, mid0, midT = cut(2, I0), cut(2, I0), cut(2, 2, 512)
        w1qkv, wo1, cosk, sink, rmask = cut(CT, 384), cut(CT, C), cut(TT, 4), cut(TT, 4), cut(P // HD1)
        raw1, rot1, rtmp, v1 = cut(TT, 320), cut(TT, 320), cut(TT, 160), cut(TT, 64)
        krep, q1T, k1T, kz = cut(TT, C), cut(CT, T), cut(CT, T), cut(4, T)
        vz = cut(TT, J1, REP, 32)
        prob1, prob1T, nmax1 = cut(4, 384), cut(2, 384), cut(4, 2)
        rsum1, rinv1 = cut(N1, 2), cut(N1, 2)
        rrep, rT, o1T = cut(TT, C), cut(CT, T), cut(CT, T)
        at[0] = hT_words
        wg1, bg1, sel1 = cut(CT, E1), cut(E1), cut(E1, P)
        lg1, pr1, top1, idf1, comb1 = cut(TAU, E1), cut(TAU, E1), cut(TAU, 8), cut(TAU, 8), cut(TAU, E1)
        oh1, mx1, combT = cut(TAU, E1), cut(TAU), cut(NT)
        iota1 = cut(E1)
        b1, b2, b3, biases = cut(E1, 4), cut(E1, 4), cut(E1, 2), cut(2, 2, 4)
        weight = cut(E1, NT)
        w1e, w2e, w3e = cut(2, CT, H1), cut(2, 4, H1), cut(2, 4, C)
        h1, h2, scaled = cut(2, 4, 512), cut(2, 4, 512), cut(2, 512)
        idx0 = sb("idx0", TAU, 8, dt=U32)

        ps = ctx.enter_context(nc.psum_tensor("ps", [P, 8, BANK], F32))

        ld = {n: sem(f"loaded_{n}") for n in ("cond", "x", "attn0", "moe0", "attn1", "moe1")}
        dve_own, act_own, pool_own = sem("dve_own"), sem("act_own"), sem("pool_own")
        c_dve, c_act = sem("cond_dve"), sem("cond_act")
        euk_in, euk_out = sem("euk_in"), sem("euk_out")
        sums_in, sums_out = sem("cond_sums_in"), sem("cond_sums_out")
        sig_ready, xc_ready = sem("sig_ready"), sem("xc_ready")
        projected, evac_a, evac_d = sem("projected"), sem("evacuated_act"), sem("evacuated_dve")
        mix_ready, norm_in, norm_out = sem("mix_ready"), sem("norm_in"), sem("norm_out")
        s_ready, s_read = sem("scores_ready"), sem("scores_read")
        lmax, p_exp, p_norm, r_ready = sem("logits_max"), sem("probs_exp"), sem("probs_normed"), sem("rinv_ready")
        h_done = sem("mixed_queries")
        t_ready, t_read, pv_done = sem("probsT_ready"), sem("probsT_read"), sem("pv_done")
        dg_pre, dg_post = sem("diag_pre_ready"), sem("diag_post_ready")
        tail_pe, tail_dve, tail_act = sem("tail_pe"), sem("tail_dve"), sem("tail_act")
        x_done = sem("residual_done")
        h_ready, route_pe, route_dve, route_act = sem("h_ready"), sem("route_pe"), sem("route_dve"), sem("route_act")
        gu_ready, silu_done, mid_done = sem("gate_up_ready"), sem("silu_done"), sem("mid_done")
        midT_ready, midT_done = sem("midT_ready"), sem("midT_done")
        w_in = [sem("expert_weights_0"), sem("expert_weights_1")]
        down_done = sem("down_done")
        y_ready = sem("y_ready")
        w1_in = [sem("expert1_weights_0"), sem("expert1_weights_1")]
        l_ready, l_read = sem("hidden_ready"), sem("hidden_read")
        y1_ready, y1_read = sem("y1_ready"), sem("y1_read")
        stacked, values_ready = sem("stacks_ready"), sem("values_ready")
        proj1_pe, attn1_dve, q1T_ready = sem("attn1_pe"), sem("attn1_dve"), sem("q1T_ready")
        s1_ready, lmax1, p1_exp = sem("scores1_ready"), sem("logits1_max"), sem("probs1_exp")
        t1_ready, t1_read, pv1_done = sem("probs1T_ready"), sem("probs1T_read"), sem("pv1_done")
        bias_ready, vz_zeroed, kz_ready = sem("bias_ready"), sem("vz_zeroed"), sem("kz_ready")
        wb_read, zeroed = sem("weight_rows_read"), sem("zeroed")
        wb_ready, stored = sem("weight_rows_ready"), sem("stored")

        block = ctx.enter_context(nc.Block())

        def turned(u):
            tt, kind = divmod(u, 5)
            return (qsT, ksT, qwT, kwT, qkT)[kind][:, :, tt * P:(tt + 1) * P]

        def turned_bank(u):
            return ps[:, u % 8].rearrange("p (g t) -> p g t", g=4)

        def turn_mid(act, i, u):
            half, q = (u // 4) % 2, u % 4
            act.wait_ge(midT_ready, i * 2 * TAU + u + 1)
            dst = midT[:, half, :, q * P:(q + 1) * P]
            act.activation(dst[:, 0], ps[:, 2 + u % 2, 0:P], ACT.Copy)
            act.activation(dst[0:I0 - P, 1], ps[0:I0 - P, 2 + u % 2, P:2 * P], ACT.Copy).then_inc(midT_done, 1)

        def store(sp):
            need = {1: 0, 2: B, 3: B + 1, 4: 2 * B + 1, 5: 2 * B + 2}[phases]
            if need:
                sp.wait_ge(x_done, need)
            sp.dma_start(out, xT[:]).then_inc(stored, 16)
            sp.wait_ge(stored, 16)

        @block.sync
        def _(sp):
            def load(dst, src, s):
                sp.dma_start(dst, src).then_inc(s, 16)

            load(condv[:], d["cond"].partition_broadcast(P), ld["cond"])
            load(wu[:], d["wu"], ld["cond"])
            load(kT[:], d["fT"], ld["cond"])
            load(xT[:], d["xT"], ld["x"])
            load(ident[:], d["ident"], ld["x"])
            for dst, n in ((wqkv, "wqkv"), (dw1, "dw1"), (qkw, "qkw"), (ddw, "ddw"), (wo0, "wo0")):
                load(dst, d[n], ld["attn0"])
            load(identb[:], d["identb"], ld["attn0"])
            load(causal[:], d["causal"], ld["attn0"])
            if phases < 2:
                sp.wait_ge(ld["attn0"], 112)
                return store(sp)
            sp.wait_ge(x_done, B)
            load(wr0, d["wr0"], ld["moe0"])
            load(iota, d["iota"].partition_broadcast(P), ld["moe0"])
            for dst, n in ((w1qkv, "w1qkv"), (wo1, "wo1"), (cosk, "cosk"), (sink, "sink"), (rmask, "rmask")):
                load(dst, d[n], ld["attn1"])

            def expert0(e, slot):
                load(wgu[:, slot], d["wgu"][bass.ds(e, 1)].rearrange("o p k n -> (o p) k n"), w_in[slot])
                load(wd[:, slot, 0], d["wd"][bass.ds(e, 1), 0:P].rearrange("o p n -> (o p) n"), w_in[slot])
                load(wd[0:I0 - P, slot, 1], d["wd"][bass.ds(e, 1), P:I0].rearrange("o p n -> (o p) n"), w_in[slot])

            if phases >= 3:
                expert0(0, 0)
                expert0(1, 1)
                with sp.Fori(1, EX0 // 2) as i:
                    for slot in range(2):
                        sp.wait_ge(down_done, 4 * i + 2 * slot - 2)
                        expert0(2 * i + slot, slot)
            if phases < 4:
                sp.wait_ge(ld["moe0"], 32)
                sp.wait_ge(ld["attn1"], 80)
                return store(sp)
            if phases >= 5:
                sp.wait_ge(x_done, 2 * B + 1)
                load(wg1, d["wg1"], ld["moe1"])
                load(bg1, d["bg1"].partition_broadcast(P), ld["moe1"])
                load(iota1, d["iota"][:, 0:E1].partition_broadcast(P), ld["moe1"])
                load(sel1, d["sel1"], ld["moe1"])
                load(b1, d["b1"], ld["moe1"])
                load(b2, d["b2"], ld["moe1"])
                load(b3, d["b3"], ld["moe1"])

                def expert1(e, slot):
                    for dst, n in ((w1e, "w1"), (w2e, "w2"), (w3e, "w3")):
                        load(dst[:, slot], d[n][bass.ds(e, 1)].rearrange("o p k n -> (o p) k n"), w1_in[slot])

                expert1(0, 0)
                expert1(1, 1)
                with sp.Fori(1, E1 // 2) as i:
                    for slot in range(2):
                        sp.wait_ge(y1_ready, 8 * i + 4 * slot - 4)
                        expert1(2 * i + slot, slot)
            store(sp)

        @block.gpsimd
        def _(pool):
            st = Steps(pool, pool_own)
            pool.memset(zerob[:], 0.0).then_inc(zeroed, 1)
            st(pool.memset(small[:, 40:42], -0.5))
            st.settle()
            st.settle()

            def sum_slice(n):
                pool.wait_ge(sums_in, n + 1)
                st(pool.tensor_tensor(den[:], den[:], backd[:], ALU.add))
                st(pool.tensor_tensor(num[:], num[:], backn[:], ALU.add))
                st.settle()
                st(pool.tensor_tensor(den[:], den[:], euk[:], ALU.add))
                st.tell(pool.tensor_tensor(num[:], num[:], euv[:], ALU.add), sums_out, n + 1)

            sum_slice(0)
            if phases < 2:
                return
            with st.loop(B, 6) as b:
                pool.wait_ge(norm_in, b + 1)
                pool.tensor_tensor(ms, ms, spread(small[:, 40:42], 1, TT * 4), ALU.pow).then_inc(norm_out, 1)
                pool.wait_ge(mix_ready, b + 1)

                def diagonals(ring, n, row, i0):
                    w = mixw[:, :, row, i0:i0 + 2, n]
                    return pool.tensor_tensor(ring[:, n % 4].rearrange("p (s i) j -> p s i j", i=2),
                                              spread(spread(ident[:], 1, 2), 1, TT),
                                              spread(w, 3, P), ALU.mult)

                for n in range(N0 + 1):
                    if n < N0:
                        if n >= 4:
                            pool.wait_ge(s_ready, b * N0 + n - 3)
                        diagonals(diag_pre, n, 1, 2).then_inc(dg_pre, 1)
                    if n >= 1:
                        if n >= 5:
                            pool.wait_ge(pv_done, b * N0 + n - 4)
                        diagonals(diag_post, n - 1, 3, 0).then_inc(dg_post, 1)
                    if n in SLICE_SUMS:
                        sum_slice(2 * b + 1 + SLICE_SUMS.index(n))
            if phases < 3:
                return
            with st.loop(7, 3) as i:
                sum_slice(i + 9)
            if phases < 4:
                return
            pool.wait_ge(x_done, B)
            pool.memset(vz, 0.0).then_inc(vz_zeroed, 1)
            with st.loop(B, 0) as b:
                pool.wait_ge(attn1_dve, b * 4 + 2)
                for n in range(N1):
                    if n >= 4:
                        pool.wait_ge(s1_ready, b * N1 + n - 3)
                    k, m = divmod(n, P // HD1)
                    pool.tensor_tensor(kz[:, n % 4], k1T[:, k], rmask[:, m:m + 1].broadcast_to([P, T]),
                                       ALU.mult).then_inc(kz_ready, 1)

        @block.scalar
        def _(act):
            st = Steps(act, act_own)
            act.wait_ge(ld["cond"], 16 * 3)
            st(act.activation(small[:, 16:24], wu[:, 0].rearrange("p i c -> p (i c)"), ACT.Exp))
            st.settle()
            act.activation(small[:, 24:32], small[:, 16:24], ACT.Exp, scale=-1.0).then_inc(c_act, 1)
            act.wait_ge(c_dve, 1)
            act.activation(small[:, 4:8], small[:, 0:4], ACT.Sigmoid).then_inc(c_act, 1)
            act.wait_ge(c_dve, 5)
            act.activation(ek[:], ek[:], ACT.Exp).then_inc(c_act, 1)

            def exp_slice(n):
                act.wait_ge(euk_in, n + 1)
                act.activation(euk[:], euk[:], ACT.Exp).then_inc(euk_out, 1)

            exp_slice(0)

            def sigmoid_batch(b):
                act.activation(sig[:], xT[:, :, bass.ds(b * T, T)], ACT.Sigmoid).then_inc(sig_ready, 1)

            if phases < 2:
                return
            act.wait_ge(ld["x"], 32)
            with st.loop(B, 0) as b:
                sigmoid_batch(b)
                for tt in range(TT):
                    act.wait_ge(projected, b * PROJ0 + 2 * tt + 2)
                    act.activation(v0[:, tt], ps[:, 1 + 2 * tt, 0:C], ACT.Copy).then_inc(evac_a, 1)
                    act.activation(dd[:, tt], ps[:, 1 + 2 * tt, C:C + 64], ACT.Tanh).then_inc(evac_a, 1)
                for h in range(2):
                    act.wait_ge(projected, b * PROJ0 + 5 + h)
                    act.activation(hid[:, 2 * h:2 * h + 2].rearrange("p c t -> p (c t)"), ps[:, 4 + h],
                                   ACT.Gelu_apprx_tanh).then_inc(evac_a, 1)
                for u in range(0, 10, 2):
                    act.wait_ge(projected, b * PROJ0 + 8 + u)
                    act.activation(turned(u), turned_bank(u), ACT.Copy).then_inc(evac_a, 1)
                act.wait_ge(projected, b * PROJ0 + 19)
                act.activation(rankq[:, 1], ps[:, 3, 0:384], ACT.Copy).then_inc(evac_a, 1)
                act.wait_ge(projected, b * PROJ0 + 21)
                act.activation(rankkT[:, 1], ps[:, 5, 0:384], ACT.Copy).then_inc(evac_a, 1)

                def exps(n):
                    s = n % 2
                    act.wait_ge(lmax, b * N0 + n + 1)
                    if n >= 2:
                        act.wait_ge(r_ready, b * N0 + n - 1)
                    if n >= 3:
                        act.wait_ge(h_done, b * N0 + n - 2)
                        act.wait_ge(t_ready, b * N0 + n - 2)
                    act.activation(prob[:, n % 3, 0:P], logit[:, s, 0:P], ACT.Exp, bias=nmax[:, s, 0:1],
                                   accum_out=rsum[:, s, 0:1])
                    act.activation(prob[:, n % 3, P:], logit[:, s, P:], ACT.Exp, bias=nmax[:, s, 1:2],
                                   accum_out=rsum[:, s, 1:2]).then_inc(p_exp, 1)

                def normalise(n):
                    act.wait_ge(r_ready, b * N0 + n + 1)
                    for tt, cols in enumerate((slice(0, P), slice(P, 384))):
                        ins = act.activation(prob[:, n % 3, cols], prob[:, n % 3, cols], ACT.Copy,
                                             scale=rinv[:, n % 2, tt:tt + 1])
                    ins.then_inc(p_norm, 1)

                def turn_out(n):
                    act.wait_ge(t_ready, b * N0 + n + 1)
                    if n >= 2:
                        act.wait_ge(pv_done, b * N0 + n - 1)
                    act.activation(probT[:, n % 2], ps[:, 2 + n % 2, 0:384], ACT.Copy).then_inc(t_read, 1)

                for k in range(N0 + 2):
                    if k < N0:
                        exps(k)
                    if k in SLICE_EXP:
                        exp_slice(b * 2 + 1 + SLICE_EXP.index(k))
                    if 1 <= k <= N0:
                        normalise(k - 1)
                    if k >= 2:
                        turn_out(k - 2)
                act.wait_ge(pv_done, b * N0 + N0)
                act.activation(mixk[:, 0:256], ps[:, 6, 0:256], ACT.Copy).then_inc(tail_act, 1)
                act.activation(mixk[:, 256:768], ps[:, 7], ACT.Copy).then_inc(tail_act, 1)
                act.activation(owT.rearrange("p (a g) t -> p a (g t)", a=2), ps[:, 4:6], ACT.Copy).then_inc(tail_act, 1)
                for i in range(2):
                    act.wait_ge(tail_pe, b * TAIL0 + 3 + i)
                    act.activation(mixkT[:, i], ps[:, 2 + i, 0:384], ACT.Copy).then_inc(tail_act, 1)
            if phases < 3:
                return
            act.wait_ge(x_done, B)
            act.activation(hT[:], xT[:], ACT.Sigmoid).then_inc(route_act, 1)
            act.wait_ge(route_dve, 2)
            act.activation(pr0, pr0, ACT.Exp).then_inc(route_act, 1)
            act.activation(comb0[:, :, E0], lg0[:, :, E0], ACT.Sigmoid).then_inc(route_act, 1)
            for turns in (7, 3):
              first = 0 if turns == 7 else 7
              with st.loop(turns, 0) as j:
                i = j + first
                for u in range(2 * TAU):
                    if turns == 7 and u == 2:
                        exp_slice(i + 9)
                    act.wait_ge(gu_ready, i * 2 * TAU + u + 1)
                    if u >= 2:
                        act.wait_ge(mid_done, i * 2 * TAU + u - 1)
                    act.activation(act0[:, u % 2], ps[:, u % 2, 0:I0], ACT.Silu).then_inc(silu_done, 1)
                    if u >= 1:
                        turn_mid(act, i, u - 1)
                turn_mid(act, i, 2 * TAU - 1)
            if phases < 4:
                return
            act.wait_ge(x_done, B + 1)
            with st.loop(B, 0) as b:
                sigmoid_batch(b)
                act.wait_ge(proj1_pe, b * 6 + 3)
                act.activation(q1T.rearrange("p a t -> p (a t)"), ps[:, 2], ACT.Copy).then_inc(q1T_ready, 1)

                def exps1(n):
                    s = n % 4
                    act.wait_ge(lmax1, b * N1 + n + 1)
                    if n >= 4:
                        act.wait_ge(t1_ready, b * N1 + n - 3)
                    act.activation(prob1[:, s, 0:P], ps[:, 2 + s, 0:P], ACT.Exp, bias=nmax1[:, s, 0:1],
                                   scale=HD1 ** -0.5, accum_out=rsum1[:, n, 0:1])
                    act.activation(prob1[:, s, P:], ps[:, 2 + s, P:384], ACT.Exp, bias=nmax1[:, s, 1:2],
                                   scale=HD1 ** -0.5, accum_out=rsum1[:, n, 1:2]).then_inc(p1_exp, 1)

                for n in range(N1):
                    exps1(n)
            if phases < 5:
                return
            act.wait_ge(x_done, 2 * B + 1)
            act.activation(hT[:], xT[:], ACT.Sigmoid).then_inc(route_act, 1)
            act.wait_ge(route_dve, 3)
            act.wait_ge(ld["moe1"], 7 * 16)
            act.activation(pr1, pr1, ACT.Exp).then_inc(route_act, 1)
            with st.loop(E1 // 2, 0) as i:
                act.wait_ge(bias_ready, i + 1)
                for slot in range(2):
                    for half in range(2):
                        for m in range(4):
                            k = slot * 16 + half * 4 + m
                            act.wait_ge(l_ready, i * 32 + k + 1)
                            act.activation(h1[:, half, m], ps[:, k % 4], ACT.Gelu,
                                           bias=biases[:, 0, slot, m:m + 1]).then_inc(l_read, 1)
                    for half in range(2):
                        for m in range(4):
                            k = slot * 16 + 8 + half * 4 + m
                            act.wait_ge(l_ready, i * 32 + k + 1)
                            act.activation(h2[:, half, m], ps[:, k % 4], ACT.Gelu,
                                           bias=biases[:, 1, slot, m:m + 1]).then_inc(l_read, 1)

        @block.vector
        def _(dve):
            st = Steps(dve, dve_own)

            cs = Steps(dve, c_dve)
            dve.wait_ge(ld["cond"], 16 * 3)
            cs(dve.tensor_reduce(small[:, 0:4], condv[:], X, ALU.add))
            dve.wait_ge(c_act, 2)
            cs(dve.tensor_scalar(small[:, 8:12], small[:, 4:8], 0.5, 0.5, ALU.mult, ALU.add))
            cs(dve.tensor_scalar(oscale[:], small[:, 4:8], 0.2, 0.8, ALU.mult, ALU.add))
            cs.settle()
            cs(dve.tensor_tensor(dec[:], spread(small[:, 24:32], 2, B), spread(small[:, 8:12], 1, 4 * CT), ALU.mult))
            cs(dve.tensor_scalar(ek[:], kT[:], 30.0, None, ALU.min))
            dve.wait_ge(c_act, 3)
            cs(dve.tensor_tensor(ekv[:], ek[:], kT[:], ALU.mult))
            for c in range(CT):
                cs(dve.memset(backn[:, c, T - 1:], 0.0))
                cs(dve.memset(backd[:, c, T - 1:], 0.0))
            cs.settle()

            def slice_steps(n, nth):
                i, b = divmod(n, B) if isinstance(n, int) else (
                    nc.s_assert_within(n >> 2, 0, 3, skip_runtime_bounds_check_because="n < 16"), n & 3)
                cols = bass.ds(b * T, T)

                def forward(out, src):
                    for c in range(CT):
                        rate = dec[:, bass.ds(i * CT + c, 1), bass.ds(b, 1)].rearrange("p a b -> p (a b)")
                        st(dve.tensor_tensor_scan(out[:, c], rate.broadcast_to([P, T]), src[:, c, cols], 0.0,
                                                  ALU.mult, ALU.add))
                    st.settle()

                def backward(back, src):
                    st(dve.tensor_scalar(euv[:], src[:, :, cols], 1.0, None, ALU.mult))
                    st.settle()
                    for c in range(CT):
                        rate = dec[:, bass.ds(i * CT + c, 1), bass.ds(b, 1)].rearrange("p a b -> p (a b)")
                        st(dve.tensor_tensor_scan(back[:, c, T - 2::-1],
                                                  euv[:, c, T - 1:0:-1],
                                                  rate.broadcast_to([P, T - 1]), 0.0, ALU.add, ALU.mult))
                    st.settle()

                def own_term():
                    dve.wait_ge(euk_out, nth + 1)
                    st.tell(dve.tensor_tensor(euv[:], euk[:], kT[:, :, cols], ALU.mult), sums_in, nth + 1)

                def tell_shifted():
                    for c in range(CT):
                        ins = dve.tensor_scalar(euk[:, c], kT[:, c, cols], wu[:, 1, bass.ds(i, 1), c], 30.0,
                                                ALU.add, ALU.min)
                    st.tell(ins, euk_in, nth + 1)

                def finish():
                    st(dve.reciprocal(den[:, 1], den[:, 1]))
                    st.settle()
                    st(dve.scalar_tensor_tensor(
                        fac[:, bass.ds(i, 1), :, cols].rearrange("p i c t -> p (i c) t"), num[:],
                        oscale[:, bass.ds(b, 1)], den[:], ALU.mult, ALU.mult))
                    st.settle()

                def floor():
                    dve.wait_ge(sums_out, nth + 1)
                    st(dve.tensor_scalar(den[:], den[:], 1e-8, None, ALU.max))
                    st.settle()
                    st(dve.reciprocal(den[:, 0], den[:, 0]))

                return [tell_shifted, lambda: (forward(num, ekv), forward(den, ek)), lambda: backward(backn, ekv),
                        lambda: backward(backd, ek), own_term, floor, finish]

            for step in slice_steps(0, 0):
                step()
            if phases < 2:
                dve.wait_ge(ld["attn0"], 112)
                return

            def condition_batch(b, which, before):
                dve.wait_ge(sig_ready, before + b + 1)
                st.tell(dve.tensor_tensor(xc[:], sig[:], fac[:, which, :, bass.ds(b * T, T)], ALU.mult),
                        xc_ready, before + b + 1)

            with st.loop(B, OWN0) as b:
                condition_batch(b, 0, 0)
                for tt in range(TT):
                    dve.wait_ge(projected, b * PROJ0 + 2 * tt + 1)
                    st(dve.tensor_scalar(qk[:, tt, 0], ps[:, 2 * tt, 0:C], HD0 ** -0.5, None, ALU.mult))
                    st.tell(dve.tensor_copy(qk[:, tt, 1], ps[:, 2 * tt, C:]), evac_d, b * EVD0 + tt + 1)
                dve.wait_ge(projected, b * PROJ0 + 7)
                flat = mixw.rearrange("p t c i m -> p (t c) i m")
                st.tell(dve.tensor_copy(mixw.rearrange("p t c i m -> p (t c i m)"), ps[:, 6]), evac_d, b * EVD0 + 3)
                st.settle()
                st(dve.tensor_tensor(sq, flat[:, :, 0:2], flat[:, :, 0:2], ALU.mult))
                st.settle()
                st(dve.tensor_reduce(ms, sq, X, ALU.add))
                st.settle()
                st.tell(dve.tensor_scalar(ms, ms, 1.0 / N0, 1e-6, ALU.mult, ALU.add), norm_in, b + 1)
                dve.wait_ge(norm_out, b + 1)
                st.tell(dve.tensor_tensor(flat[:, :, 0:2], flat[:, :, 0:2], spread(ms, 3, N0), ALU.mult),
                        mix_ready, b + 1)
                st.settle()
                dve.wait_ge(evac_a, b * EVA0 + 4)

                def heads(ap):
                    return ap.rearrange("p (n h) -> p n h", h=HD0)

                for tt in range(TT):
                    q, k = heads(qk[:, tt, 0]), heads(qk[:, tt, 1])
                    st(dve.scalar_tensor_tensor(qs[:, tt, :, 0], spread(dd[:, tt, 0:16], 2, HD0), 1.0, q,
                                                ALU.add, ALU.mult))
                    st(dve.tensor_copy(qs[:, tt, :, 1], q))
                    st(dve.tensor_copy(ks[:, tt, :, 0], k))
                    st(dve.tensor_tensor(ks[:, tt, :, 1], k, spread(dd[:, tt, 16:32], 2, HD0), ALU.mult))
                    st(dve.tensor_tensor(qw[:, tt].rearrange("p i (n h) -> p i n h", h=HD0), spread(q, 1, 2),
                                         spread(mixw[:, tt, 0, 0:2], 3, HD0), ALU.mult))
                    st.tell(dve.tensor_tensor(kw[:, tt].rearrange("p i (n h) -> p i n h", h=HD0), spread(k, 1, 2),
                                              spread(mixw[:, tt, 1, 0:2], 3, HD0), ALU.mult),
                            stacked, b * TT + tt + 1)
                for tt in range(TT):
                    v = heads(v0[:, tt])
                    st(dve.tensor_copy(vs[:, tt, :, 0], v))
                    st(dve.tensor_tensor(vs[:, tt, :, 1], v, spread(dd[:, tt, 48:64], 2, HD0), ALU.mult))
                    ins = dve.tensor_tensor(vk[:, tt].rearrange("p i (n h) -> p i n h", h=HD0), spread(v, 1, 2),
                                            spread(mixw[:, tt, 3, 2:4], 3, HD0), ALU.mult)
                    if tt:
                        st.tell(ins, values_ready, b + 1)
                    else:
                        st(ins)
                for u in range(1, 10, 2):
                    dve.wait_ge(projected, b * PROJ0 + 8 + u)
                    st.tell(dve.tensor_copy(turned(u), turned_bank(u)), evac_d, b * EVD0 + 4 + u // 2)
                dve.wait_ge(projected, b * PROJ0 + 18)
                st.tell(dve.tensor_copy(rankq[:, 0], ps[:, 2, 0:384]), evac_d, b * EVD0 + 9)
                dve.wait_ge(projected, b * PROJ0 + 20)
                st.tell(dve.tensor_copy(rankkT[:, 0], ps[:, 4, 0:384]), evac_d, b * EVD0 + 10)
                st.settle()
                dve.wait_ge(evac_a, b * EVA0 + 12)
                tiles = (slice(0, P), slice(P, 384))

                def logits(n):
                    s = n % 2
                    dve.wait_ge(s_ready, b * N0 + n + 1)
                    if n >= 2:
                        dve.wait_ge(p_exp, b * N0 + n - 1)
                    for tt in range(TT):
                        ins = dve.scalar_tensor_tensor(logit[:, s, tiles[tt]], rankq[:, 0, tiles[tt]],
                                                       mixw[:, tt, 0, 2, n:n + 1], ps[:, s, tiles[tt]],
                                                       ALU.mult, ALU.add)
                    st.tell(ins, s_read, b * N0 + n + 1)
                    st.settle()
                    for tt in range(TT):
                        ins = dve.scalar_tensor_tensor(logit[:, s, tiles[tt]], rankq[:, 1, tiles[tt]],
                                                       mixw[:, tt, 0, 3, n:n + 1], logit[:, s, tiles[tt]],
                                                       ALU.mult, ALU.add)
                    st(ins)
                    st.settle()
                    for tt in range(TT):
                        ins = dve.tensor_reduce(nmax[:, s, tt:tt + 1], logit[:, s, tiles[tt]], X, ALU.max, negate=True)
                    st.tell(ins, lmax, b * N0 + n + 1)

                def invert(n):
                    dve.wait_ge(p_exp, b * N0 + n + 1)
                    st.tell(dve.reciprocal(rinv[:, n % 2], rsum[:, n % 2]), r_ready, b * N0 + n + 1)

                def mix(n):
                    dve.wait_ge(p_norm, b * N0 + n + 1)
                    if n >= N0 - 2:
                        dve.wait_ge(h_done, b * N0 + n)
                    for i in range(2):
                        for tt in range(TT):
                            w = mixw[:, tt, 2, i, n:n + 1]
                            dst = mixq[:, i, tiles[tt]]
                            if n == 0:
                                ins = dve.tensor_scalar(dst, prob[:, n % 3, tiles[tt]], w, None, ALU.mult)
                            else:
                                ins = dve.scalar_tensor_tensor(dst, prob[:, n % 3, tiles[tt]], w, dst, ALU.mult, ALU.add)
                    st.tell(ins, h_done, b * N0 + n + 1)

                one, two = slice_steps(b * 2 + 1, b * 2 + 1), slice_steps(b * 2 + 2, b * 2 + 2)
                extra = dict(zip((0, 1, 2, 3, 4), one)) | dict(zip((9, 10, 11, 12, 13), two))
                extra[7], extra[8], extra[16], extra[17] = one[5], one[6], two[5], two[6]
                for k in range(N0 + 2):
                    if k < N0:
                        logits(k)
                    if 1 <= k <= N0:
                        invert(k - 1)
                    if k >= 2:
                        mix(k - 2)
                    if k in extra:
                        extra[k]()

                for i in range(2):
                    dve.wait_ge(tail_pe, b * TAIL0 + 1 + i)
                    st.tell(dve.tensor_copy(mixqT[:, i], ps[:, i, 0:384]), tail_dve, b * 4 + 1 + i)
                dve.wait_ge(tail_pe, b * TAIL0 + 7)
                for tt in range(TT):
                    o = heads(o_tok[:, tt])
                    own = ps[:, 4 + tt].rearrange("p (n e h) -> p e n h", e=2, h=HD0)
                    st(dve.scalar_tensor_tensor(o, spread(dd[:, tt, 32:48], 2, HD0), 1.0, own[:, 0],
                                                ALU.add, ALU.mult))
                    for i in range(2):
                        if i:
                            st.settle()
                        st(dve.tensor_tensor(heads(o_tmp[:, tt]), heads(ps[:, tt, i * C:(i + 1) * C]),
                                             spread(mixw[:, tt, 2, 2 + i], 2, HD0), ALU.mult))
                        st.settle()
                        st(dve.tensor_tensor(o_tok[:, tt], o_tok[:, tt], o_tmp[:, tt], ALU.add))
                    st.settle()
                    st(dve.tensor_tensor(o, o, own[:, 1], ALU.add))
                    st.settle()
                    ins = dve.tensor_tensor(o_tok[:, tt], o_tok[:, tt], ps[:, 2, tt * C:(tt + 1) * C], ALU.add)
                    if tt:
                        st.tell(ins, tail_dve, b * 4 + 3)
                    else:
                        st(ins)
                dve.wait_ge(tail_pe, b * TAIL0 + 8)
                st.tell(dve.tensor_copy(oT.rearrange("p a t -> p (a t)"), ps[:, 3]), tail_dve, b * 4 + 4)
                dve.wait_ge(tail_pe, b * TAIL0 + 9)
                here = xT[:, :, bass.ds(b * T, T)]
                st.tell(dve.tensor_tensor(here, here, ps[:, 4].rearrange("p (m t) -> p m t", m=CT), ALU.add),
                        x_done, b + 1)
            if phases < 3:
                return

            def condition_all(which, act_done, done):
                dve.wait_ge(route_act, act_done)
                st.tell(dve.tensor_tensor(hT[:], hT[:], fac[:, which], ALU.mult), h_ready, done)

            def softmax_rows(lg, pr, mx, told, act_done):
                n = pr.shape[2]
                st(dve.tensor_reduce(mx, lg[:, :, 0:n], X, ALU.max))
                st.settle()
                st.tell(dve.tensor_tensor(pr, lg[:, :, 0:n], spread(mx, 2, n), ALU.subtract), route_dve, told)
                dve.wait_ge(route_act, act_done)
                st(dve.tensor_reduce(mx, pr, X, ALU.add))
                st.settle()
                st(dve.reciprocal(mx, mx))
                st.settle()
                st(dve.tensor_tensor(pr, pr, spread(mx, 2, n), ALU.mult))
                st.settle()

            def choose(pr, top, idf, comb, oh, ia, kk):
                n = pr.shape[2]
                for tau in range(TAU):
                    st(dve.max(top[:, tau], pr[:, tau]))
                st.settle()
                for tau in range(TAU):
                    st(dve.max_index(idx0[:, tau], top[:, tau], pr[:, tau]))
                st.settle()
                st(dve.tensor_copy(idf, idx0[:]))
                st.settle()

            def weigh(top, idf, comb, oh, ia, kk):
                n = oh.shape[2]
                for k in range(kk):
                    st(dve.tensor_tensor(oh, spread(ia, 1, TAU), spread(idf[:, :, k], 2, n), ALU.is_equal))
                    st.settle()
                    st(dve.tensor_tensor(comb if k == 0 else oh, oh, spread(top[:, :, k], 2, n), ALU.mult))
                    st.settle()
                    if k:
                        st(dve.tensor_tensor(comb, comb, oh, ALU.add))
                        st.settle()

            condition_all(1, 1, 1)
            dve.wait_ge(ld["moe0"], 32)
            dve.wait_ge(route_pe, 1)
            st.tell(dve.tensor_copy(lg0, ps[:, 0].rearrange("p (a n) -> p a n", n=64)[:, :, 0:E0 + 1]), route_dve, 1)
            st.settle()
            softmax_rows(lg0, pr0, mx0, 2, 2)
            choose(pr0, top0, idf0, comb0, oh0, iota, K0)
            st(dve.tensor_reduce(mx0, top0[:, :, 0:K0], X, ALU.add))
            st.settle()
            st(dve.tensor_scalar(mx0, mx0, 1e-9, None, ALU.max))
            st.settle()
            st(dve.reciprocal(mx0, mx0))
            st.settle()
            st(dve.tensor_tensor(top0, top0, spread(mx0, 2, 8), ALU.mult))
            st.settle()
            weigh(top0, idf0, comb0[:, :, 0:E0], oh0, iota, K0)
            dve.wait_ge(route_act, 3)
            st(dve.tensor_copy(comb0[:, :, E0 + 1:], spread(comb0[:, :, E0], 2, SH0 - 1)))
            st.settle()
            assert EX0 // 2 == 10
            for turns in (7, 3):
              first = 0 if turns == 7 else 7
              with st.loop(turns, SLICE_OWN if turns == 7 else 0) as j:
                i = j + first
                extra = dict(zip((0, 1, 2, 3, 4, 10, 12), slice_steps(i + 9, i + 9))) if turns == 7 else {}
                for u in range(2 * TAU):
                    if u in extra:
                        extra[u]()
                    slot, tau = divmod(u, TAU)
                    dve.wait_ge(silu_done, i * 2 * TAU + u + 1)
                    if u >= 2:
                        dve.wait_ge(midT_ready, i * 2 * TAU + u - 1)
                    dve.scalar_tensor_tensor(mid0[:, u % 2], ps[:, u % 2, I0:2 * I0],
                                             comb0[:, tau, bass.ds(2 * i + slot, 1)], act0[:, u % 2],
                                             ALU.mult, ALU.mult).then_inc(mid_done, 1)
            dve.wait_ge(y_ready, 1)
            for m in range(CT):
                here = xT[:, m].rearrange("p (a t) -> p a t", a=2)
                ins = dve.tensor_tensor(here, here, ps[:, 4 + 2 * m:6 + 2 * m], ALU.add)
                if m:
                    st.tell(ins, x_done, B + 1)
            if phases < 4:
                return

            with st.loop(B, OWN1) as b:
                condition_batch(b, 2, B)
                dve.wait_ge(ld["attn1"], 80)
                for tt in range(TT):
                    dve.wait_ge(proj1_pe, b * 6 + tt + 1)
                    st(dve.tensor_copy(raw1[:, tt], ps[:, tt, 0:320]))
                    st(dve.tensor_copy(v1[:, tt], ps[:, tt, 320:384]))
                st.settle()
                dve.wait_ge(vz_zeroed, 1)
                for r in range(REP):
                    st(dve.tensor_copy(vz[:, :, :, r, r * HD1:(r + 1) * HD1],
                                       v1.rearrange("p t (j d) -> p t j d", d=HD1)))
                x0, x1 = (raw1.rearrange("p t (g d e) -> p t g d e", d=4, e=2)[:, :, :, :, e] for e in range(2))
                r0, r1 = (rot1.rearrange("p t (g d e) -> p t g d e", d=4, e=2)[:, :, :, :, e] for e in range(2))
                tmp = rtmp.rearrange("p t (g d) -> p t g d", d=4)
                for tt in range(TT):
                    c, s = spread(cosk[:, tt], 1, 40), spread(sink[:, tt], 1, 40)
                    st(dve.tensor_tensor(tmp[:, tt], x1[:, tt], s, ALU.mult))
                    st(dve.tensor_tensor(r0[:, tt], x0[:, tt], c, ALU.mult))
                    st.settle()
                    st(dve.tensor_tensor(r0[:, tt], r0[:, tt], tmp[:, tt], ALU.subtract))
                    st.settle()
                    st(dve.tensor_tensor(tmp[:, tt], x1[:, tt], c, ALU.mult))
                    st(dve.tensor_tensor(r1[:, tt], x0[:, tt], s, ALU.mult))
                    st.settle()
                    st(dve.tensor_tensor(r1[:, tt], r1[:, tt], tmp[:, tt], ALU.add))
                    st.settle()
                for tt in range(TT):
                    ins = dve.tensor_copy(krep[:, tt].rearrange("p (j r d) -> p j r d", r=REP, d=HD1),
                                          spread(rot1[:, tt, C:].rearrange("p (j d) -> p j d", d=HD1), 2, REP))
                st.tell(ins, attn1_dve, b * 4 + 1)
                dve.wait_ge(proj1_pe, b * 6 + 4)
                st.tell(dve.tensor_copy(k1T.rearrange("p a t -> p (a t)"), ps[:, 3]), attn1_dve, b * 4 + 2)

                def maxima(n):
                    s = n % 4
                    dve.wait_ge(s1_ready, b * N1 + n + 1)
                    for tt in range(TT):
                        ins = dve.tensor_reduce(nmax1[:, s, tt:tt + 1], ps[:, 2 + s, tt * P:P + 2 * tt * P], X,
                                                ALU.max, negate=True)
                    st(ins)
                    st.settle()
                    st.tell(dve.tensor_scalar(nmax1[:, s], nmax1[:, s], HD1 ** -0.5, None, ALU.mult),
                            lmax1, b * N1 + n + 1)

                def turn_out(n):
                    dve.wait_ge(t1_ready, b * N1 + n + 1)
                    if n >= 2:
                        dve.wait_ge(pv1_done, b * N1 + n - 1)
                    st.tell(dve.tensor_copy(prob1T[:, n % 2], ps[:, n % 2, 0:384]), t1_read, b * N1 + n + 1)

                for k in range(N1 + 2):
                    if k < N1:
                        maxima(k)
                    if k >= 2:
                        turn_out(k - 2)
                st(dve.reciprocal(rinv1, rsum1))
                st.settle()
                for tt in range(TT):
                    ins = dve.tensor_copy(rrep[:, tt].rearrange("p (n h) -> p n h", h=HD1),
                                          spread(rinv1[:, :, tt], 2, HD1))
                st.tell(ins, attn1_dve, b * 4 + 3)
                dve.wait_ge(proj1_pe, b * 6 + 5)
                st(dve.tensor_copy(rT.rearrange("p a t -> p (a t)"), ps[:, 7]))
                st.settle()
                dve.wait_ge(pv1_done, b * N1 + N1)
                st.tell(dve.tensor_tensor(o1T.rearrange("p a t -> p (a t)"), rT.rearrange("p a t -> p (a t)"), ps[:, 6],
                                          ALU.mult), attn1_dve, b * 4 + 4)
                dve.wait_ge(proj1_pe, b * 6 + 6)
                here = xT[:, :, bass.ds(b * T, T)]
                st.tell(dve.tensor_tensor(here, here, ps[:, 2].rearrange("p (m t) -> p m t", m=CT), ALU.add),
                        x_done, B + b + 2)
            if phases < 5:
                return

            condition_all(3, 4, 2)
            dve.wait_ge(ld["moe1"], 7 * 16)
            dve.wait_ge(route_pe, 2)
            st(dve.tensor_tensor(lg1, ps[:, 0].rearrange("p (a n) -> p a n", n=64)[:, :, 0:E1], spread(bg1, 1, TAU),
                                 ALU.add))
            st.settle()
            softmax_rows(lg1, pr1, mx1, 3, 5)
            choose(pr1, top1, idf1, comb1, oh1, iota1, K1)
            weigh(top1, idf1, comb1, oh1, iota1, K1)
            st.tell(dve.tensor_copy(oh1, comb1), route_dve, 4)
            dve.wait_ge(route_pe, 3)
            st.tell(dve.tensor_copy(combT[0:E1, :].rearrange("p (a t) -> p a t", a=2), ps[0:E1, 1:3]), route_dve, 5)
            for e in range(E1):
                for half in range(2):
                    j = 2 * e + half
                    dve.wait_ge(wb_ready, j + 1)
                    st.tell(dve.tensor_copy(weight[:, e, half * 512:(half + 1) * 512], ps[:, 4 + j % 4]),
                            wb_read, j + 1)
            st.settle()
            with st.loop(E1 // 2, OWN3) as i:
                st(dve.tensor_scalar(biases[:, 0], b1[:, bass.ds(2 * i, 2)], 1.0, None, ALU.mult))
                st.tell(dve.tensor_scalar(biases[:, 1], b2[:, bass.ds(2 * i, 2)], 1.0, None, ALU.mult),
                        bias_ready, i + 1)
                for slot in range(2):
                    for half in range(2):
                        for m in range(CT):
                            y = i * 8 + slot * 4 + half * 2 + m
                            cols = slice(half * 512, (half + 1) * 512)
                            dve.wait_ge(y1_ready, y + 1)
                            st.tell(dve.scalar_tensor_tensor(scaled[:, m], ps[:, 4 + 2 * half + m],
                                                             b3[:, bass.ds(2 * i + slot, 1), m], weight[:, bass.ds(2 * i + slot, 1), cols].rearrange("p o t -> p (o t)"),
                                                             ALU.add, ALU.mult), y1_read, y + 1)
                            st.settle()
                            st(dve.tensor_tensor(xT[:, m, cols], xT[:, m, cols], scaled[:, m], ALU.add))
                            st.settle()
            dve.tensor_copy(small[:, 0:1], xT[:, 0, 0:1]).then_inc(x_done, 1)

        @block.tensor
        def _(pe):
            if phases < 2:
                return

            def mm(o, l, r, start=True, stop=True, shared=False):
                return pe.matmul(o, l, r, start=start, stop=stop, skip_group_check=shared)

            pe.wait_ge(ld["x"], 32)
            pe.wait_ge(ld["attn0"], 112)
            with pe.Fori(0, B) as b:
                pe.wait_ge(xc_ready, b + 1)
                for tt in range(TT):
                    tok = slice(tt * P, (tt + 1) * P)
                    for o, w in ((ps[:, 2 * tt], wqkv[:, :, 0:2 * C]), (ps[:, 2 * tt + 1, 0:C], wqkv[:, :, 2 * C:]),
                                 (ps[:, 2 * tt + 1, C:C + 64], ddw)):
                        for k in range(CT):
                            ins = mm(o, xc[:, k, tok], w[:, k], k == 0, k == CT - 1)
                        if w is not ddw and w.shape[2] == C:
                            continue
                        ins.then_inc(projected, 1)
                for c in range(4):
                    for k in range(CT):
                        ins = mm(ps[:, 4 + c // 2, (c % 2) * T:(c % 2 + 1) * T], dw1[:, k, c * P:(c + 1) * P],
                                 xc[:, k], k == 0, k == CT - 1)
                    if c % 2:
                        ins.then_inc(projected, 1)
                pe.wait_ge(evac_a, b * EVA0 + 6)
                for tt in range(TT):
                    for c in range(4):
                        ins = mm(ps[:, 6, tt * 256 + c * 64:tt * 256 + (c + 1) * 64], hid[:, c, tt * P:(tt + 1) * P],
                                 qkw[:, c])
                ins.then_inc(projected, 1)
                for u in range(10):
                    tt, kind = divmod(u, 5)
                    if kind == 0:
                        pe.wait_ge(stacked, b * TT + tt + 1)
                    if u == 8:
                        pe.wait_ge(evac_a, b * EVA0 + 7)
                    if u == 9:
                        pe.wait_ge(evac_d, b * EVD0 + 4)
                    src = (qs[:, tt].rearrange("p n e h -> p (n e h)"), ks[:, tt].rearrange("p n e h -> p (n e h)"),
                           qw[:, tt].rearrange("p i c -> p (i c)"), kw[:, tt].rearrange("p i c -> p (i c)"),
                           qk[:, tt].rearrange("p i c -> p (i c)"))[kind]
                    for g in range(4):
                        ins = pe.transpose(ps[:, u % 8, g * P:(g + 1) * P], src[:, g * P:(g + 1) * P], ident[:])
                    ins.then_inc(projected, 1)
                pe.wait_ge(evac_a, b * EVA0 + 11)
                pe.wait_ge(evac_d, b * EVD0 + 8)
                for i in range(2):
                    for tt in range(TT):
                        for k in range(CT):
                            ins = mm(ps[:, 2 + i, tt * P:P + tt * 2 * P], qwT[:, 2 * i + k, tt * P:(tt + 1) * P],
                                     kTb[:, k, 0:(tt + 1) * P], k == 0, k == CT - 1)
                    ins.then_inc(projected, 1)
                for i in range(2):
                    for s in range(TT):
                        for k in range(CT):
                            ins = mm(ps[:, 4 + i, s * 256:s * 256 + (2 - s) * P], kwT[:, 2 * i + k, s * P:(s + 1) * P],
                                     qT[:, k, s * P:], k == 0, k == CT - 1)
                    ins.then_inc(projected, 1)
                pe.wait_ge(evac_a, b * EVA0 + 13)
                pe.wait_ge(evac_d, b * EVD0 + 10)

                def scores(n):
                    pe.wait_ge(dg_pre, b * N0 + n + 1)
                    if n >= 2:
                        pe.wait_ge(s_read, b * N0 + n - 1)
                    rows, g = slice(32 * (n % 4), 32 * (n % 4) + 32), n // 4
                    o = ps[:, n % 2]
                    mm(o[:, 0:P], qsT[rows, g, 0:P], ksT[rows, g, 0:P], True, False, True)
                    mm(o[:, P:384], qsT[rows, g, P:], ksT[rows, g], False, False, True)
                    for blk in (0, 2):
                        mm(o[:, blk * P:(blk + 1) * P], identb[:], causal[:], False, False, True)
                    for blk, (tt, s) in enumerate(CAUSAL):
                        for i in range(2):
                            ins = mm(o[:, blk * P:(blk + 1) * P], rankkT[:, i, blk * P:(blk + 1) * P],
                                     diag_pre[:, n % 4, 2 * s + i], False, blk == 2 and i == 1, True)
                    ins.then_inc(s_ready, 1)

                def turn(n):
                    pe.wait_ge(p_norm, b * N0 + n + 1)
                    if n >= 2:
                        pe.wait_ge(t_read, b * N0 + n - 1)
                    for blk in range(3):
                        ins = pe.transpose(ps[:, 2 + n % 2, blk * P:(blk + 1) * P],
                                           prob[:, n % 3, blk * P:(blk + 1) * P], ident[:])
                    ins.then_inc(t_ready, 1)

                def values(n):
                    pe.wait_ge(t_read, b * N0 + n + 1)
                    pe.wait_ge(dg_post, b * N0 + n + 1)
                    if n == 0:
                        pe.wait_ge(values_ready, b + 1)
                    pT = probT[:, n % 2]
                    vals = vs.rearrange("p t n e h -> p t n (e h)")
                    o = ps[32 * (n % 4):32 * (n % 4) + 32, 4 + n // 8, (n // 4 % 2) * T:(n // 4 % 2 + 1) * T]
                    mm(o, vals[:, 0, n], pT[:, 0:2 * P], True, False, True)
                    mm(o[:, P:], vals[:, 1, n], pT[:, 2 * P:], False, True, True)
                    d0 = diag_post[:, n % 4, 0:2].rearrange("p i j -> p (i j)")
                    d1 = diag_post[:, n % 4, 2:4].rearrange("p i j -> p (i j)")
                    last = n == N0 - 1
                    mm(ps[:, 6, 0:256], pT[:, 0:P], d0, n == 0, last, True)
                    mm(ps[:, 7, 0:256], pT[:, P:2 * P], d0, n == 0, last, True)
                    mm(ps[:, 7, 256:512], pT[:, 2 * P:], d1, False, last, True).then_inc(pv_done, 1)

                for k in range(N0 + 3):
                    if k < N0:
                        scores(k)
                    if 2 <= k <= N0 + 1:
                        turn(k - 2)
                    if k >= 3:
                        values(k - 3)

                pe.wait_ge(h_done, b * N0 + N0)
                pe.wait_ge(s_read, b * N0 + N0)
                for i in range(2):
                    for blk in range(3):
                        ins = pe.transpose(ps[:, i, blk * P:(blk + 1) * P], mixq[:, i, blk * P:(blk + 1) * P], ident[:])
                    ins.then_inc(tail_pe, 1)
                pe.wait_ge(tail_act, b * 5 + 2)
                for i in range(2):
                    for blk in range(3):
                        src = (0, 256, 512)[blk] + i * P
                        ins = pe.transpose(ps[:, 2 + i, blk * P:(blk + 1) * P], mixk[:, src:src + P], ident[:])
                    ins.then_inc(tail_pe, 1)
                pe.wait_ge(tail_dve, b * 4 + 2)
                for tt in range(TT):
                    for i in range(2):
                        for s in range(tt + 1):
                            blk = tt + s
                            ins = mm(ps[:, tt, i * C:(i + 1) * C], mixqT[:, i, blk * P:(blk + 1) * P], v0[:, s],
                                     s == 0, s == tt)
                    ins.then_inc(tail_pe, 1)
                pe.wait_ge(tail_act, b * 5 + 3)
                for tt in range(TT):
                    for g in range(4):
                        pe.transpose(ps[:, 4 + tt, g * P:(g + 1) * P], owT[:, g, tt * P:(tt + 1) * P], ident[:])
                pe.wait_ge(tail_act, b * 5 + 5)
                for tt in range(TT):
                    terms = [(i, s) for i in range(2) for s in range(tt + 1)]
                    for j, (i, s) in enumerate(terms):
                        blk = tt + s
                        ins = mm(ps[:, 2, tt * C:(tt + 1) * C], mixkT[:, i, blk * P:(blk + 1) * P], vk[:, s, i],
                                 j == 0, j == len(terms) - 1)
                ins.then_inc(tail_pe, 1)
                pe.wait_ge(tail_dve, b * 4 + 3)
                for k in range(CT):
                    for tt in range(TT):
                        ins = pe.transpose(ps[:, 3, (k * TT + tt) * P:(k * TT + tt + 1) * P],
                                           o_tok[:, tt, k * P:(k + 1) * P], ident[:])
                ins.then_inc(tail_pe, 1)
                pe.wait_ge(tail_dve, b * 4 + 4)
                for m in range(CT):
                    for k in range(CT):
                        ins = mm(ps[:, 4, m * T:(m + 1) * T], wo0[:, k, m * P:(m + 1) * P], oT[:, k], k == 0, k == CT - 1)
                ins.then_inc(tail_pe, 1)
            if phases < 3:
                return

            def route(w, n, h_done_, banks):
                pe.wait_ge(h_ready, h_done_)
                for tau in range(TAU):
                    for k in range(CT):
                        ins = mm(ps[:, 0, tau * 64:tau * 64 + n], hT[:, k, tau * P:(tau + 1) * P], w[:, k],
                                 k == 0, k == CT - 1)
                ins.then_inc(route_pe, 1)

            pe.wait_ge(ld["moe0"], 32)
            route(wr0, E0 + 1, 1, None)
            pe.wait_ge(route_dve, 1)
            pe.wait_ge(zeroed, 1)
            for m in range(4):
                mm(ps[:, 4 + m], zerob[:, 0:P], zerob[:], True, False, True)
            with pe.Fori(0, EX0 // 2) as i:
                for u in range(2 * TAU + 3):
                    if u < 2 * TAU:
                        slot, tau = divmod(u, TAU)
                        if tau == 0:
                            pe.wait_ge(w_in[slot], 48 * i + 48)
                        if u >= 2:
                            pe.wait_ge(mid_done, i * 2 * TAU + u - 1)
                        for k in range(CT):
                            ins = mm(ps[:, u % 2, 0:2 * I0], hT[:, k, tau * P:(tau + 1) * P], wgu[:, slot, k],
                                     k == 0, k == CT - 1)
                        ins.then_inc(gu_ready, 1)
                    if 1 <= u <= 2 * TAU:
                        v = u - 1
                        pe.wait_ge(mid_done, i * 2 * TAU + v + 1)
                        if v >= 2:
                            pe.wait_ge(midT_done, i * 2 * TAU + v - 1)
                        pe.transpose(ps[:, 2 + v % 2, 0:P], mid0[:, v % 2, 0:P], ident[:])
                        pe.transpose(ps[0:I0 - P, 2 + v % 2, P:2 * P], mid0[:, v % 2, P:I0], ident[:])\
                            .then_inc(midT_ready, 1)
                    if u in (6, 10, 14, 18):
                        n = (u - 6) // 4
                        slot, half = divmod(n, 2)
                        pe.wait_ge(midT_done, i * 2 * TAU + 4 * n + 4)
                        for m in range(CT):
                            mm(ps[:, 4 + 2 * m + half], wd[:, slot, 0, m * P:(m + 1) * P], midT[:, half, 0],
                               False, False, True)
                            ins = mm(ps[:, 4 + 2 * m + half], wd[0:I0 - P, slot, 1, m * P:(m + 1) * P],
                                     midT[0:I0 - P, half, 1], False, False, True)
                        ins.then_inc(down_done, 1)
            for m in range(4):
                ins = mm(ps[:, 4 + m], zerob[:, 0:P], zerob[:], False, True, True)
            ins.then_inc(y_ready, 1)
            if phases < 4:
                return

            pe.wait_ge(ld["attn1"], 80)
            with pe.Fori(0, B) as b:
                pe.wait_ge(xc_ready, B + b + 1)
                for tt in range(TT):
                    for k in range(CT):
                        ins = mm(ps[:, tt, 0:384], xc[:, k, tt * P:(tt + 1) * P], w1qkv[:, k], k == 0, k == CT - 1)
                    ins.then_inc(proj1_pe, 1)
                pe.wait_ge(attn1_dve, b * 4 + 1)
                for src, bank in ((rot1, 2), (krep, 3)):
                    for k in range(CT):
                        for tt in range(TT):
                            ins = pe.transpose(ps[:, bank, (k * TT + tt) * P:(k * TT + tt + 1) * P],
                                               src[:, tt, k * P:(k + 1) * P], ident[:])
                    ins.then_inc(proj1_pe, 1)
                pe.wait_ge(attn1_dve, b * 4 + 2)
                pe.wait_ge(q1T_ready, b + 1)

                def scores(n):
                    k = n // (P // HD1)
                    pe.wait_ge(kz_ready, b * N1 + n + 1)
                    if n >= 4:
                        pe.wait_ge(p1_exp, b * N1 + n - 3)
                    o = ps[:, 2 + n % 4]
                    mm(o[:, 0:P], q1T[:, k, 0:P], kz[:, n % 4, 0:P], True, False, True)
                    mm(o[:, P:384], q1T[:, k, P:], kz[:, n % 4], False, False, True)
                    mm(o[:, 0:P], identb[:], causal[:], False, False, True)
                    mm(o[:, 256:384], identb[:], causal[:], False, True, True).then_inc(s1_ready, 1)

                def turn(n):
                    pe.wait_ge(p1_exp, b * N1 + n + 1)
                    if n >= 2:
                        pe.wait_ge(t1_read, b * N1 + n - 1)
                    for blk in range(3):
                        ins = pe.transpose(ps[:, n % 2, blk * P:(blk + 1) * P],
                                           prob1[:, n % 4, blk * P:(blk + 1) * P], ident[:])
                    ins.then_inc(t1_ready, 1)

                def values(n):
                    j, r = divmod(n, REP)
                    pe.wait_ge(t1_read, b * N1 + n + 1)
                    pT, o = prob1T[:, n % 2], ps[32 * (j % 4):32 * (j % 4) + 32, 6, (j // 4) * T:(j // 4 + 1) * T]
                    mm(o, vz[:, 0, j, r], pT[:, 0:2 * P], r == 0, False, True)
                    mm(o[:, P:], vz[:, 1, j, r], pT[:, 2 * P:], False, r == REP - 1, True).then_inc(pv1_done, 1)

                for k in range(N1 + 3):
                    if k < N1:
                        scores(k)
                    if 2 <= k <= N1 + 1:
                        turn(k - 2)
                    if k >= 3:
                        values(k - 3)
                pe.wait_ge(attn1_dve, b * 4 + 3)
                for k in range(CT):
                    for tt in range(TT):
                        ins = pe.transpose(ps[:, 7, (k * TT + tt) * P:(k * TT + tt + 1) * P],
                                           rrep[:, tt, k * P:(k + 1) * P], ident[:])
                ins.then_inc(proj1_pe, 1)
                pe.wait_ge(attn1_dve, b * 4 + 4)
                for m in range(CT):
                    for k in range(CT):
                        ins = mm(ps[:, 2, m * T:(m + 1) * T], wo1[:, k, m * P:(m + 1) * P], o1T[:, k], k == 0, k == CT - 1)
                ins.then_inc(proj1_pe, 1)
            if phases < 5:
                return

            pe.wait_ge(ld["moe1"], 7 * 16)
            route(wg1, E1, 2, None)
            pe.wait_ge(route_dve, 4)
            for tau in range(TAU):
                ins = pe.transpose(ps[0:E1, 1 + tau // 4, (tau % 4) * P:(tau % 4 + 1) * P], oh1[:, tau], ident[:])
            ins.then_inc(route_pe, 1)
            pe.wait_ge(route_dve, 5)
            for e in range(E1):
                for half in range(2):
                    j = 2 * e + half
                    if j >= 4:
                        pe.wait_ge(wb_read, j - 3)
                    mm(ps[:, 4 + j % 4], sel1[0:E1, e], combT[0:E1, half * 512:(half + 1) * 512]).then_inc(wb_ready, 1)
            pe.wait_ge(wb_read, 2 * E1)
            with pe.Fori(0, E1 // 2) as i:
                for slot in range(2):
                    pe.wait_ge(w1_in[slot], 48 * i + 48)
                    if slot:
                        pe.wait_ge(y1_read, i * 8 + slot * 4)

                    def layer(k0, w, src, nk, width):
                        for half in range(2):
                            for m in range(4):
                                k = k0 + half * 4 + m
                                if k >= 4:
                                    pe.wait_ge(l_read, i * 32 + k - 3)
                                for c in range(nk):
                                    ins = mm(ps[:, k % 4], w[:, slot, c, m * P:(m + 1) * P], src(half, c),
                                             c == 0, c == nk - 1)
                                ins.then_inc(l_ready, 1)
                    layer(slot * 16, w1e, lambda half, c: hT[:, c, half * 512:(half + 1) * 512], CT, H1)
                    pe.wait_ge(l_read, i * 32 + slot * 16 + 8)
                    layer(slot * 16 + 8, w2e, lambda half, c: h1[:, half, c], 4, H1)
                    pe.wait_ge(l_read, i * 32 + slot * 16 + 16)
                    for half in range(2):
                        for m in range(CT):
                            for c in range(4):
                                ins = mm(ps[:, 4 + 2 * half + m], w3e[:, slot, c, m * P:(m + 1) * P], h2[:, half, c],
                                         c == 0, c == 3)
                            ins.then_inc(y1_ready, 1)


INPUTS = ["x", "fside_BxSxS_0", "cond_512"]


def kernel(**inp):
    from concourse import bacc
    from concourse.bass_utils import run_bass_kernel_spmd
    import ml_dtypes

    a = {k: np.asarray(v) for k, v in inp.items()}

    def tiles(w):
        return np.ascontiguousarray(w.reshape(-1, P, w.shape[-1]).transpose(1, 0, 2))

    def stack(w):
        return np.ascontiguousarray(w.reshape(w.shape[0], -1, P, w.shape[-1]).transpose(0, 2, 1, 3))

    def column(v):
        return np.ascontiguousarray(v.reshape(v.shape[0], -1, P).transpose(2, 0, 1))

    w = np.stack([a[n + "_w"] for n in ("L0_cond", "L0_cond2", "L1_cond", "L1_cond2")])
    u = np.stack([a[n + "_u"] for n in ("L0_cond", "L0_cond2", "L1_cond", "L1_cond2")])

    def cut(w):
        return w.reshape(C, SH0, I0).transpose(1, 0, 2)

    gate = np.concatenate([a["L0_ffn_w_gate"], cut(a["L0_ffn_sh_gate"])])
    up = np.concatenate([a["L0_ffn_w_up"], cut(a["L0_ffn_sh_up"])])
    down = np.concatenate([a["L0_ffn_w_down"], a["L0_ffn_sh_down"].reshape(SH0, I0, C)])
    f4 = np.float32
    freq = 10000.0 ** (-(np.arange(HD1 // 2, dtype=f4) * f4(2.0 / HD1)))
    phase = (np.arange(T, dtype=f4)[:, None] * freq.astype(f4)[None, :]).astype(f4)
    s_after_t = np.arange(P)[None, :] > np.arange(P)[:, None]
    arrays = {
        "xT": tiles(a["x"].reshape(NT, C).T), "fT": tiles(a["fside_BxSxS_0"].reshape(NT, C).T),
        "cond": a["cond_512"], "wu": np.ascontiguousarray(np.stack([column(w), column(u)], 1)),
        "ident": np.eye(P, dtype=f4), "identb": np.eye(P).astype(ml_dtypes.bfloat16),
        "causal": np.where(s_after_t, MASKED, 0.0).astype(ml_dtypes.bfloat16),
        "wqkv": tiles(a["L0_attn_w_qkv"]), "dw1": tiles(a["L0_attn_dw1"].reshape(C, 512)),
        "qkw": np.ascontiguousarray(a["L0_attn_qkw"][0].reshape(4, P, 64).transpose(1, 0, 2)),
        "ddw": tiles(a["L0_attn_dd_w"][:, 0]), "wo0": tiles(a["L0_attn_w_o"].T),
        "wr0": tiles(np.concatenate([a["L0_ffn_router_w"].T, a["L0_ffn_sh_gate_w"]], 1)),
        "iota": np.arange(E0, dtype=f4)[None],
        "wgu": stack(np.concatenate([gate, up], 2)), "wd": np.ascontiguousarray(down),
        "w1qkv": tiles(np.concatenate([a["L1_attn_wq"], a["L1_attn_wk"], a["L1_attn_wv"]], 1)),
        "wo1": tiles(a["L1_attn_wo"]),
        "cosk": tiles(np.cos(phase)), "sink": tiles(np.sin(phase)),
        "rmask": (np.arange(P)[:, None] // HD1 == np.arange(P // HD1)[None, :]).astype(f4),
        "wg1": tiles(a["L1_ffn_Wg"]), "bg1": a["L1_ffn_bg"][None],
        "sel1": np.ascontiguousarray(np.broadcast_to(np.eye(P, E1, dtype=f4)[:, :, None], (P, E1, P))),
        "b1": column(a["L1_ffn_b1"]), "b2": column(a["L1_ffn_b2"]), "b3": column(a["L1_ffn_b3"]),
        "w1": stack(a["L1_ffn_W1"]), "w2": stack(a["L1_ffn_W2"]), "w3": stack(a["L1_ffn_W3"]),
    }
    nc = bacc.Bacc("TRN2", target_bir_lowering=False, num_devices=1)
    d = {k: nc.dram_tensor("in_" + k, v.shape, mybir.dt.from_np(v.dtype), kind="ExternalInput").ap()
         for k, v in arrays.items()}
    out = nc.dram_tensor("out", (P, CT, NT), F32, kind="ExternalOutput").ap()
    build(nc, d, out)
    got = run_bass_kernel_spmd(nc, [{"in_" + k: v for k, v in arrays.items()}], core_ids=[0])
    xT = got.results[0]["out"]
    return np.ascontiguousarray(xT.transpose(1, 0, 2).reshape(C, NT).T).reshape(B, T, C)
```

```python
from contextlib import ExitStack, contextmanager

import concourse.bass as bass
from concourse import mybir
import numpy as np

F32 = mybir.dt.float32
BF16 = mybir.dt.bfloat16
F16 = mybir.dt.float16
U32 = mybir.dt.uint32
ALU = mybir.AluOpType
ACT = mybir.ActivationFunctionType
X = mybir.AxisListType.X

P = 128
B, T, C = 4, 256, 256
NT = B * T
CT = C // P
TT = T // P
BANK = 512
N0, HD0 = 16, 16
N1, J1, HD1 = 32, 8, 8
REP = N1 // J1
E0, K0, I0 = 16, 4, 176
SH0 = 704 // I0
EX0 = E0 + SH0
E1, K1, H1 = 8, 2, 512
ARENA = 31700
TAU = NT // P
UNITS = 2 * TAU
FIRST_LATE = 2 * B + 1
LATE = 4 * B - FIRST_LATE
EARLY = FIRST_LATE + 1
SLICE_OWN = 17
OWN0, OWN1, OWN3 = 78, 54, 41
PROJ0, EVA0, EVD0, TAIL0 = 21, 13, 10, 9
SLICE_EXP = (1, 10)
SLICE_SUMS = (7, 15)
TURNS = [(0, 0), (0, 1), (0, 4), (1, 0), (1, 1), (1, 4), (0, 2), (0, 3), (1, 2), (1, 3)]
CAUSAL = [(0, 0), (1, 0), (1, 1)]
MASKED = -1.0e30


class Steps:

    def __init__(self, eng, own):
        self.eng, self.own, self.n, self.term = eng, own, 0, 0
        self.last = None

    def __call__(self, ins):
        ins.then_inc(self.own, 1)
        self.n += 1
        self.last = (self.own, self.term + self.n)

    def tell(self, ins, sem, value):
        ins.then_inc(sem, 1)
        self.last = (sem, value)

    def settle(self):
        self.eng.wait_ge(*self.last)

    @contextmanager
    def loop(self, count, per):
        before = self.n
        with self.eng.Fori(0, count) as it:
            self.term, self.n = it * per + before, 0
            yield it
            assert self.n == per, f"{self.own}: {self.n} steps in a turn"
        self.term, self.n, self.last = 0, before + count * per, None


def spread(ap, axis, n):
    shape = list(ap.shape)
    return ap.unsqueeze(axis).broadcast_to(shape[:axis] + [n] + shape[axis:])


def build(nc, d, out):
    ctx = ExitStack()
    with ctx:
        def sb(name, *shape, dt=F32):
            return ctx.enter_context(nc.sbuf_tensor(name, [P, *shape], dt))

        def sem(name):
            return ctx.enter_context(nc.semaphore(name))

        xT = sb("xT", CT, NT)
        fac = sb("fac", 4, CT, NT)
        kT, ek, ekv = sb("kT", CT, NT), sb("ek", CT, NT), sb("ekv", CT, NT)
        euk, euv, num, den, backn, backd = (sb(n, CT, T) for n in ("euk", "euv", "num", "den", "backn", "backd"))
        dec = sb("dec", 4 * CT, B)
        oscale = sb("oscale", B)
        wu = sb("wu", 2, 4, CT)
        small = sb("small", 64)
        ident = sb("ident", P)
        causal = sb("causal", P, dt=BF16)
        identb = sb("identb", P, dt=BF16)
        zerob = sb("zerob", BANK, dt=BF16)
        zero32 = sb("zero32", 1)
        ident16 = sb("ident16", P, dt=F16)
        condv = sb("condv", B, 64)
        sig = sb("sig", CT, T)
        xc = sb("xc", CT, T)
        arena = sb("arena", ARENA)
        at = [0]

        def cut(*shape, dt=F32):
            n = int(np.prod(shape)) // (2 if dt == F16 else 1)
            a = arena[:, at[0]:at[0] + n]
            at[0] += n
            assert at[0] <= ARENA
            if dt != F32:
                a = a.bitcast(dt)
            if len(shape) > 1:
                names = "abcdef"[:len(shape)]
                a = a.rearrange(f"p ({' '.join(names)}) -> p {' '.join(names)}",
                                **dict(zip(names, shape)))
            return a

        at[0] = 0
        wqkv, dw1, qkw, ddw, wo0 = cut(CT, 3 * C), cut(CT, 512), cut(4, 64), cut(CT, 64), cut(CT, C)
        qk, v0 = cut(TT, 2, C), cut(TT, C)
        dd, mixw, sq, ms = cut(TT, 64), cut(TT, 4, 4, N0), cut(TT * 4, 2, N0), cut(TT * 4, 2)
        hid = cut(4, T)
        qs_at = at[0]
        qs, ks = cut(TT, N0, 2, HD0), cut(TT, N0, 2, HD0)
        owT = arena[:, qs_at:qs_at + 4 * T].rearrange("p (g t) -> p g t", g=4)
        qw, kw = cut(TT, 2, C), cut(TT, 2, C)
        vs, vk = cut(TT, N0, 2, HD0), cut(TT, 2, C)
        qsT, ksT, qkT = cut(4, T), cut(4, T), cut(2 * CT, T)
        qT, kTb = qkT[:, 0:CT], qkT[:, CT:]
        qwT, kwT = cut(2 * CT, T), cut(2 * CT, T)
        rankq, rankkT = cut(2, 384), cut(2, 384)
        diag_pre, diag_post = cut(4, TT * 2, P), cut(4, TT * 2, P)
        logit, prob, probT = cut(2, 384), cut(3, 384), cut(2, 384)
        nmax, rsum, rinv = cut(2, 2), cut(2, 2), cut(2, 2)
        mixq, mixk = cut(2, 384), cut(2 * 384)
        mixqT, mixkT = cut(2, 384), cut(2, 384)
        o_tok, o_tmp, oT = cut(TT, C), cut(TT, C), cut(CT, T)
        at[0] = 0
        hT = cut(CT, NT)
        hT_words = at[0]
        wr0 = cut(CT, E0 + 1)
        iota = cut(E0)
        lg0, pr0, mx0 = cut(TAU, E0 + 1), cut(TAU, E0), cut(TAU)
        top0, idf0, comb0, oh0 = cut(TAU, 8), cut(TAU, 8), cut(TAU, EX0), cut(TAU, E0)
        wgu, wd = cut(2, CT, 2 * I0), cut(2, 2, C)
        act0, mid0 = cut(2, I0), cut(2, I0)
        hTs0, wgus, wds = cut(2, CT, NT, dt=F16), cut(2, 2, CT, 2 * I0, dt=F16), cut(2, 2, 2, C, dt=F16)
        mids, midT = cut(4, 2, I0, dt=F16), cut(2, 2, 2, 512, dt=F16)
        w1qkv, wo1, cosk, sink, rmask = cut(CT, 384), cut(CT, C), cut(TT, 4), cut(TT, 4), cut(P // HD1)
        raw1, rot1, rtmp, v1 = cut(TT, 320), cut(TT, 320), cut(TT, 160), cut(TT, 64)
        krep, q1T, k1T, kz = cut(TT, C), cut(CT, T), cut(CT, T), cut(4, T)
        vz = cut(TT, J1, REP, 32)
        prob1, prob1T, nmax1 = cut(4, 384), cut(2, 384), cut(4, 2)
        rsum1, rinv1 = cut(N1, 2), cut(N1, 2)
        rrep, rT, o1T = cut(TT, C), cut(CT, T), cut(CT, T)
        at[0] = hT_words
        wg1, bg1, sel1 = cut(CT, E1), cut(E1), cut(2, P)
        lg1, pr1, top1, idf1, comb1 = cut(TAU, E1), cut(TAU, E1), cut(TAU, 8), cut(TAU, 8), cut(TAU, E1)
        oh1, mx1, combT, pair = cut(TAU, E1), cut(TAU), cut(NT), cut(TAU, 2)
        iota1 = cut(E1)
        b1, b2, b3, biases = cut(E1, 4), cut(E1, 4), cut(E1, 2), cut(2, 2, 4)
        weight = cut(2, NT)
        w1e, w2e, w3e = cut(CT, H1), cut(4, H1), cut(4, C)
        w1s, w2s, w3s = cut(2, 2, CT, H1, dt=F16), cut(2, 2, 4, H1, dt=F16), cut(2, 2, 4, C, dt=F16)
        hTs, h1, h2 = cut(2, CT, NT, dt=F16), cut(2, 2, 4, 512, dt=F16), cut(2, 2, 4, 512, dt=F16)
        scaled = cut(2, 512)
        hfull = arena[:, 0:CT * NT].rearrange("p (k n) -> p k n", k=4)
        idx0 = sb("idx0", TAU, 8, dt=U32)

        ps = ctx.enter_context(nc.psum_tensor("ps", [P, 8, BANK], F32))

        ld = {n: sem(f"loaded_{n}") for n in ("cond", "x", "attn0", "moe0", "attn1", "moe1")}
        dve_own, act_own, pool_own = sem("dve_own"), sem("act_own"), sem("pool_own")
        c_dve, c_act = sem("cond_dve"), sem("cond_act")
        euk_in, euk_out = sem("euk_in"), sem("euk_out")
        sums_in, sums_out = sem("cond_sums_in"), sem("cond_sums_out")
        sig_ready, xc_ready = sem("sig_ready"), sem("xc_ready")
        projected, evac_a, evac_d = sem("projected"), sem("evacuated_act"), sem("evacuated_dve")
        mix_ready, norm_in, norm_out = sem("mix_ready"), sem("norm_in"), sem("norm_out")
        s_ready, s_read = sem("scores_ready"), sem("scores_read")
        lmax, p_exp, p_norm, r_ready = sem("logits_max"), sem("probs_exp"), sem("probs_normed"), sem("rinv_ready")
        h_done = sem("mixed_queries")
        t_ready, t_read, pv_done = sem("probsT_ready"), sem("probsT_read"), sem("pv_done")
        dg_pre, dg_post = sem("diag_pre_ready"), sem("diag_post_ready")
        tail_pe, tail_dve, tail_act = sem("tail_pe"), sem("tail_dve"), sem("tail_act")
        x_done = sem("residual_done")
        h_ready, route_pe, route_dve, route_act = sem("h_ready"), sem("route_pe"), sem("route_dve"), sem("route_act")
        gu_ready, silu_done, mid_done = sem("gate_up_ready"), sem("silu_done"), sem("mid_done")
        midT_ready, midT_done = sem("midT_ready"), sem("midT_done")
        hs0_ready, w0_split, up_read = sem("h_split"), sem("expert_weights_split"), sem("up_read")
        w_in = [sem("expert_weights_0"), sem("expert_weights_1")]
        down_done = sem("down_done")
        y_ready = sem("y_ready")
        w1_in, w_split, h_split = sem("expert1_weights"), sem("expert1_weights_split"), sem("hidden_split")
        pair_ready, turned_ready, rows_ready = sem("pair_ready"), sem("pair_turned"), sem("weight_rows_copied")
        l_ready, l_read = sem("hidden_ready"), sem("hidden_read")
        y1_ready, y1_read = sem("y1_ready"), sem("y1_read")
        stacked, values_ready = sem("stacks_ready"), sem("values_ready")
        proj1_pe, attn1_dve, q1T_ready = sem("attn1_pe"), sem("attn1_dve"), sem("q1T_ready")
        s1_ready, lmax1, p1_exp = sem("scores1_ready"), sem("logits1_max"), sem("probs1_exp")
        t1_ready, t1_read, pv1_done = sem("probs1T_ready"), sem("probs1T_read"), sem("pv1_done")
        bias_ready, vz_zeroed, kz_ready = sem("bias_ready"), sem("vz_zeroed"), sem("kz_ready")
        wb_read, zeroed = sem("weight_rows_read"), sem("zeroed")
        wb_ready, stored = sem("weight_rows_ready"), sem("stored")

        block = ctx.enter_context(nc.Block())

        def turned(u):
            tt, kind = TURNS[u]
            return (qsT, ksT, qwT, kwT, qkT)[kind][:, :, tt * P:(tt + 1) * P]

        def turned_bank(u):
            return ps[:, u % 8].rearrange("p (g t) -> p g t", g=4)

        def gate_up(u):
            return ps[:, 1 if u % UNITS == UNITS - 1 else u % UNITS % 3]

        def turned_parts():
            return ps[:, 3].bitcast(F16)[:, 0:4 * P].rearrange("p (j a t) -> p j a t", j=2, a=2)

        def turn_mid(act, i, u):
            half, q = (u // 4) % 2, u % 4
            act.wait_ge(midT_ready, i * 2 * TAU + u + 1)
            dst, src = midT[:, half, :, :, q * P:(q + 1) * P], turned_parts()
            act.activation(dst[:, 0], src[:, 0], ACT.Copy)
            act.activation(dst[0:I0 - P, 1], src[0:I0 - P, 1], ACT.Copy).then_inc(midT_done, 1)

        def store(sp):
            sp.wait_ge(x_done, 2 * B + 2)
            sp.dma_start(out, xT[:]).then_inc(stored, 16)
            sp.wait_ge(stored, 16)

        @block.sync
        def _(sp):
            def load(dst, src, s):
                sp.dma_start(dst, src).then_inc(s, 16)

            load(condv[:], d["cond"].partition_broadcast(P), ld["cond"])
            load(wu[:], d["wu"], ld["cond"])
            load(kT[:], d["fT"], ld["cond"])
            load(xT[:], d["xT"], ld["x"])
            load(ident[:], d["ident"], ld["x"])
            for dst, n in ((wqkv, "wqkv"), (dw1, "dw1"), (qkw, "qkw"), (ddw, "ddw"), (wo0, "wo0")):
                load(dst, d[n], ld["attn0"])
            load(identb[:], d["identb"], ld["attn0"])
            load(ident16[:], d["ident16"], ld["attn0"])
            load(causal[:], d["causal"], ld["attn0"])
            sp.wait_ge(x_done, B)
            load(wr0, d["wr0"], ld["moe0"])
            load(iota, d["iota"].partition_broadcast(P), ld["moe0"])
            for dst, n in ((w1qkv, "w1qkv"), (wo1, "wo1"), (cosk, "cosk"), (sink, "sink"), (rmask, "rmask")):
                load(dst, d[n], ld["attn1"])

            def expert0(e, slot):
                load(wgu[:, slot], d["wgu"][bass.ds(e, 1)].rearrange("o p k n -> (o p) k n"), w_in[slot])
                load(wd[:, slot, 0], d["wd"][bass.ds(e, 1), 0:P].rearrange("o p n -> (o p) n"), w_in[slot])
                load(wd[0:I0 - P, slot, 1], d["wd"][bass.ds(e, 1), P:I0].rearrange("o p n -> (o p) n"), w_in[slot])

            expert0(0, 0)
            expert0(1, 1)
            with sp.Fori(1, EX0 // 2) as i:
                for slot in range(2):
                    sp.wait_ge(w0_split, 2 * i + slot - 1)
                    expert0(2 * i + slot, slot)
            sp.wait_ge(x_done, 2 * B + 1)
            load(wg1, d["wg1"], ld["moe1"])
            load(bg1, d["bg1"].partition_broadcast(P), ld["moe1"])
            load(iota1, d["iota"][:, 0:E1].partition_broadcast(P), ld["moe1"])
            load(sel1, d["sel1"], ld["moe1"])
            load(b1, d["b1"], ld["moe1"])
            load(b2, d["b2"], ld["moe1"])
            load(b3, d["b3"], ld["moe1"])

            def expert1(e):
                for dst, n in ((w1e, "w1"), (w2e, "w2"), (w3e, "w3")):
                    load(dst, d[n][bass.ds(e, 1)].rearrange("o p k n -> (o p) k n"), w1_in)

            expert1(0)
            with sp.Fori(1, E1) as e:
                sp.wait_ge(w_split, 3 * e)
                expert1(e)
            store(sp)

        @block.gpsimd
        def _(pool):
            st = Steps(pool, pool_own)
            pool.memset(zerob[:], 0.0).then_inc(zeroed, 1)
            pool.memset(zero32[:], 0.0)
            st(pool.memset(small[:, 40:42], -0.5))
            st.settle()
            st.settle()

            def sum_slice(n, early=False):
                pool.wait_ge(sums_in, n + 1)
                st(pool.tensor_tensor(den[:], den[:], backd[:], ALU.add))
                st(pool.tensor_tensor(num[:], num[:], backn[:], ALU.add))
                st.settle()
                if not early:
                    st(pool.tensor_tensor(den[:], den[:], euk[:], ALU.add))
                st.tell(pool.tensor_tensor(num[:], num[:], euv[:], ALU.add), sums_out, n + 1)

            sum_slice(0)
            with st.loop(B, 6) as b:
                pool.wait_ge(norm_in, b + 1)
                pool.tensor_tensor(ms, ms, spread(small[:, 40:42], 1, TT * 4), ALU.pow).then_inc(norm_out, 1)
                pool.wait_ge(mix_ready, b + 1)

                def diagonals(ring, n, row, i0):
                    w = mixw[:, :, row, i0:i0 + 2, n]
                    return pool.tensor_tensor(ring[:, n % 4].rearrange("p (s i) j -> p s i j", i=2),
                                              spread(spread(ident[:], 1, 2), 1, TT),
                                              spread(w, 3, P), ALU.mult)

                for n in range(N0 + 1):
                    if n < N0:
                        if n >= 4:
                            pool.wait_ge(s_ready, b * N0 + n - 3)
                        diagonals(diag_pre, n, 1, 2).then_inc(dg_pre, 1)
                    if n >= 1:
                        if n >= 5:
                            pool.wait_ge(pv_done, b * N0 + n - 4)
                        diagonals(diag_post, n - 1, 3, 0).then_inc(dg_post, 1)
                    if n in SLICE_SUMS:
                        sum_slice(2 * b + 1 + SLICE_SUMS.index(n))

            def split_expert0(i, slot, peeled):
                pool.wait_ge(w_in[slot], 48 * i + 48)
                if not peeled:
                    pool.wait_ge(down_done, 4 * i + 2 * slot - 2)
                pieces = ((wgu[:, slot], wgus[:, slot, 0], wgus[:, slot, 1]),
                          (wd[:, slot, 0], wds[:, slot, 0, 0], wds[:, slot, 1, 0]),
                          (wd[0:I0 - P, slot, 1], wds[0:I0 - P, slot, 0, 1], wds[0:I0 - P, slot, 1, 1]))
                for w, high, low in pieces:
                    zeros = zero32[0:w.shape[0]]
                    zeros = zeros.unsqueeze(2) if len(w.shape) == 3 else zeros
                    st(pool.tensor_tensor(high, w, zeros.broadcast_to(list(w.shape)), ALU.add))
                st.settle()
                for n, (w, high, low) in enumerate(pieces):
                    ins = pool.tensor_tensor(low, w, high, ALU.subtract)
                    if n < 2:
                        st(ins)
                    else:
                        st.tell(ins, w0_split, 2 * i + slot + 1)

            for slot in range(2):
                split_expert0(0, slot, True)
            sum_slice(FIRST_LATE, True)
            with st.loop(LATE - 1, 12) as j:
                for slot in range(2):
                    split_expert0(j + 1, slot, False)
                sum_slice(j + FIRST_LATE + 1, True)
            with st.loop(EX0 // 2 - LATE, 10) as j:
                for slot in range(2):
                    split_expert0(j + LATE, slot, False)
            pool.wait_ge(x_done, B)
            pool.memset(vz, 0.0).then_inc(vz_zeroed, 1)
            with st.loop(B, 0) as b:
                pool.wait_ge(attn1_dve, b * 4 + 2)
                for n in range(N1):
                    if n >= 4:
                        pool.wait_ge(s1_ready, b * N1 + n - 3)
                    k, m = divmod(n, P // HD1)
                    pool.tensor_tensor(kz[:, n % 4], k1T[:, k], rmask[:, m:m + 1].broadcast_to([P, T]),
                                       ALU.mult).then_inc(kz_ready, 1)

            def split_expert(i, slot, peeled):
                pool.wait_ge(w1_in, 96 * i + 48 * slot + 48)
                if not peeled:
                    pool.wait_ge(y1_ready, 8 * i + 4 * slot - 4)
                for n, (w, ws) in enumerate(((w1e, w1s), (w2e, w2s), (w3e, w3s))):
                    zeros = zero32[:].unsqueeze(2).broadcast_to(list(w.shape))
                    st(pool.tensor_tensor(ws[:, slot, 0], w, zeros, ALU.add))
                    st.settle()
                    st.tell(pool.tensor_tensor(ws[:, slot, 1], w, ws[:, slot, 0], ALU.subtract), w_split,
                            6 * i + 3 * slot + n + 1)

            for slot in range(2):
                split_expert(0, slot, True)
            with st.loop(E1 // 2 - 1, 6) as j:
                for slot in range(2):
                    split_expert(j + 1, slot, False)

        @block.scalar
        def _(act):
            st = Steps(act, act_own)
            act.wait_ge(ld["cond"], 16 * 3)
            st(act.activation(small[:, 16:24], wu[:, 0].rearrange("p i c -> p (i c)"), ACT.Exp))
            st.settle()
            act.activation(small[:, 24:32], small[:, 16:24], ACT.Exp, scale=-1.0).then_inc(c_act, 1)
            act.wait_ge(c_dve, 1)
            act.activation(small[:, 4:8], small[:, 0:4], ACT.Sigmoid).then_inc(c_act, 1)
            act.wait_ge(c_dve, 5)
            act.activation(ek[:], ek[:], ACT.Exp).then_inc(c_act, 1)

            def exp_slice(n):
                act.wait_ge(euk_in, n + 1)
                act.activation(euk[:], euk[:], ACT.Exp).then_inc(euk_out, 1)

            exp_slice(0)

            def sigmoid_batch(b):
                act.activation(sig[:], xT[:, :, bass.ds(b * T, T)], ACT.Sigmoid).then_inc(sig_ready, 1)

            act.wait_ge(ld["x"], 32)
            sigmoid_batch(0)
            with st.loop(B, 0) as b:
                for h in range(2):
                    act.wait_ge(projected, b * PROJ0 + 1 + h)
                    act.activation(hid[:, 2 * h:2 * h + 2].rearrange("p c t -> p (c t)"), ps[:, 4 + h],
                                   ACT.Gelu_apprx_tanh).then_inc(evac_a, 1)
                for tt in range(TT):
                    act.wait_ge(projected, b * PROJ0 + 4 + 3 * tt)
                    act.activation(v0[:, tt], ps[:, 1 + 2 * tt, 0:C], ACT.Copy).then_inc(evac_a, 1)
                    act.activation(dd[:, tt], ps[:, 1 + 2 * tt, C:C + 64], ACT.Tanh).then_inc(evac_a, 1)
                for u in range(0, 10, 2):
                    act.wait_ge(projected, b * PROJ0 + 8 + u)
                    act.activation(turned(u), turned_bank(u), ACT.Copy).then_inc(evac_a, 1)
                act.wait_ge(projected, b * PROJ0 + 19)
                act.activation(rankq[:, 1], ps[:, 3, 0:384], ACT.Copy).then_inc(evac_a, 1)
                act.wait_ge(projected, b * PROJ0 + 21)
                act.activation(rankkT[:, 1], ps[:, 5, 0:384], ACT.Copy).then_inc(evac_a, 1)

                def exps(n):
                    s = n % 2
                    act.wait_ge(lmax, b * N0 + n + 1)
                    if n >= 2:
                        act.wait_ge(r_ready, b * N0 + n - 1)
                    if n >= 3:
                        act.wait_ge(h_done, b * N0 + n - 2)
                        act.wait_ge(t_ready, b * N0 + n - 2)
                    act.activation(prob[:, n % 3, 0:P], logit[:, s, 0:P], ACT.Exp, bias=nmax[:, s, 0:1],
                                   accum_out=rsum[:, s, 0:1])
                    act.activation(prob[:, n % 3, P:], logit[:, s, P:], ACT.Exp, bias=nmax[:, s, 1:2],
                                   accum_out=rsum[:, s, 1:2]).then_inc(p_exp, 1)

                def normalise(n):
                    act.wait_ge(r_ready, b * N0 + n + 1)
                    for tt, cols in enumerate((slice(0, P), slice(P, 384))):
                        ins = act.activation(prob[:, n % 3, cols], prob[:, n % 3, cols], ACT.Copy,
                                             scale=rinv[:, n % 2, tt:tt + 1])
                    ins.then_inc(p_norm, 1)

                def turn_out(n):
                    act.wait_ge(t_ready, b * N0 + n + 1)
                    if n >= 2:
                        act.wait_ge(pv_done, b * N0 + n - 1)
                    act.activation(probT[:, n % 2], ps[:, 2 + n % 2, 0:384], ACT.Copy).then_inc(t_read, 1)

                for k in range(N0 + 2):
                    if k < N0:
                        exps(k)
                    if k in SLICE_EXP:
                        exp_slice(b * 2 + 1 + SLICE_EXP.index(k))
                    if 1 <= k <= N0:
                        normalise(k - 1)
                    if k >= 2:
                        turn_out(k - 2)
                sigmoid_batch((b + 1) & (B - 1))
                act.wait_ge(pv_done, b * N0 + N0)
                act.activation(mixk[:, 0:256], ps[:, 6, 0:256], ACT.Copy).then_inc(tail_act, 1)
                act.activation(mixk[:, 256:768], ps[:, 7], ACT.Copy).then_inc(tail_act, 1)
                act.activation(owT.rearrange("p (a g) t -> p a (g t)", a=2), ps[:, 4:6], ACT.Copy).then_inc(tail_act, 1)
                for i in range(2):
                    act.wait_ge(tail_pe, b * TAIL0 + 3 + i)
                    act.activation(mixkT[:, i], ps[:, 2 + i, 0:384], ACT.Copy).then_inc(tail_act, 1)
            act.wait_ge(x_done, B)
            act.activation(hT[:], xT[:], ACT.Sigmoid).then_inc(route_act, 1)
            act.wait_ge(route_dve, 2)
            act.activation(pr0, pr0, ACT.Exp).then_inc(route_act, 1)
            act.wait_ge(euk_in, EARLY)
            act.activation(fac[:, 2, :, T:], fac[:, 2, :, T:], ACT.Exp)
            act.activation(fac[:, 3], fac[:, 3], ACT.Exp).then_inc(euk_out, 1)
            act.activation(comb0[:, :, E0], lg0[:, :, E0], ACT.Sigmoid).then_inc(route_act, 1)

            def gated(i, u):
                act.wait_ge(gu_ready, i * UNITS + u + 1)
                if u >= 2:
                    act.wait_ge(up_read, i * UNITS + u - 1)
                act.activation(act0[:, u % 2], gate_up(u)[:, 0:I0], ACT.Silu).then_inc(silu_done, 1)

            gated(0, 0)
            gated(0, 1)
            with st.loop(EX0 // 2 - 1, 0) as i:
                for u in range(2, UNITS + 2):
                    gated(i, u)
                    turn_mid(act, i, u - 2)
            for u in range(2, UNITS + 2):
                if u < UNITS:
                    gated(EX0 // 2 - 1, u)
                turn_mid(act, EX0 // 2 - 1, u - 2)
            act.wait_ge(x_done, B + 1)
            sigmoid_batch(0)
            with st.loop(B, 0) as b:
                act.wait_ge(proj1_pe, b * 6 + 3)
                act.activation(q1T.rearrange("p a t -> p (a t)"), ps[:, 2], ACT.Copy).then_inc(q1T_ready, 1)

                def exps1(n):
                    s = n % 4
                    act.wait_ge(lmax1, b * N1 + n + 1)
                    if n >= 4:
                        act.wait_ge(t1_ready, b * N1 + n - 3)
                    act.activation(prob1[:, s, 0:P], ps[:, 2 + s, 0:P], ACT.Exp, bias=nmax1[:, s, 0:1],
                                   scale=HD1 ** -0.5, accum_out=rsum1[:, n, 0:1])
                    act.activation(prob1[:, s, P:], ps[:, 2 + s, P:384], ACT.Exp, bias=nmax1[:, s, 1:2],
                                   scale=HD1 ** -0.5, accum_out=rsum1[:, n, 1:2]).then_inc(p1_exp, 1)

                for n in range(N1):
                    exps1(n)
                sigmoid_batch((b + 1) & (B - 1))
            act.wait_ge(x_done, 2 * B + 1)
            act.activation(hT[:], xT[:], ACT.Sigmoid).then_inc(route_act, 1)
            act.wait_ge(route_dve, 3)
            act.wait_ge(ld["moe1"], 7 * 16)
            act.activation(pr1, pr1, ACT.Exp).then_inc(route_act, 1)
            with st.loop(E1 // 2, 0) as i:
                act.wait_ge(bias_ready, i + 1)
                for k in range(32):
                    slot, layer, m = k // 16, k // 8 % 2, k % 4
                    act.wait_ge(l_ready, i * 32 + k + 1)
                    if k >= 4:
                        act.wait_ge(h_split, i * 32 + k - 3)
                    act.activation(hfull[:, k % 4], ps[:, k % 4], ACT.Gelu,
                                   bias=biases[:, layer, slot, m:m + 1]).then_inc(l_read, 1)

        @block.vector
        def _(dve):
            st = Steps(dve, dve_own)

            cs = Steps(dve, c_dve)
            dve.wait_ge(ld["cond"], 16 * 3)
            cs(dve.tensor_reduce(small[:, 0:4], condv[:], X, ALU.add))
            dve.wait_ge(c_act, 2)
            cs(dve.tensor_scalar(small[:, 8:12], small[:, 4:8], 0.5, 0.5, ALU.mult, ALU.add))
            cs(dve.tensor_scalar(oscale[:], small[:, 4:8], 0.2, 0.8, ALU.mult, ALU.add))
            cs.settle()
            cs(dve.tensor_tensor(dec[:], spread(small[:, 24:32], 2, B), spread(small[:, 8:12], 1, 4 * CT), ALU.mult))
            cs(dve.tensor_scalar(ek[:], kT[:], 30.0, None, ALU.min))
            dve.wait_ge(c_act, 3)
            cs(dve.tensor_tensor(ekv[:], ek[:], kT[:], ALU.mult))
            for c in range(CT):
                cs(dve.memset(backn[:, c, T - 1:], 0.0))
                cs(dve.memset(backd[:, c, T - 1:], 0.0))
            cs.settle()

            def slice_steps(n, nth, early=False):
                i, b = divmod(n, B) if isinstance(n, int) else (
                    nc.s_assert_within(n >> 2, 0, 3, skip_runtime_bounds_check_because="n < 16"), n & 3)
                cols = bass.ds(b * T, T)

                done = {}

                def rate(c, n):
                    return dec[:, bass.ds(i * CT + c, 1), bass.ds(b, 1)].rearrange("p a b -> p (a b)")\
                        .broadcast_to([P, n])

                def shifted():
                    for c in range(CT):
                        ins = dve.tensor_scalar(euk[:, c], kT[:, c, cols], wu[:, 1, bass.ds(i, 1), c], 30.0,
                                                ALU.add, ALU.min)
                    st.tell(ins, euk_in, nth + 1)

                def forward(out, src):
                    for c in range(CT):
                        st(dve.tensor_tensor_scan(out[:, c], rate(c, T), src[:, c, cols], 0.0, ALU.mult, ALU.add))

                def stage(src):
                    if "scan" in done:
                        dve.wait_ge(*done["scan"])
                    st(dve.tensor_scalar(euv[:], src[:, :, cols], 1.0, None, ALU.mult))
                    done["stage"] = st.last

                def backward(back):
                    dve.wait_ge(*done["stage"])
                    for c in range(CT):
                        st(dve.tensor_tensor_scan(back[:, c, T - 2::-1], euv[:, c, T - 1:0:-1], rate(c, T - 1), 0.0,
                                                  ALU.add, ALU.mult))
                    done["scan"] = st.last

                def early_own_term():
                    mine = fac[:, bass.ds(i, 1), :, cols].rearrange("p i c t -> p (i c) t")
                    dve.wait_ge(*done["scan"])
                    st(dve.tensor_tensor(den[:], den[:], mine, ALU.add))
                    st.tell(dve.tensor_tensor(euv[:], mine, kT[:, :, cols], ALU.mult), sums_in, nth + 1)

                def own_term():
                    dve.wait_ge(*done["scan"])
                    dve.wait_ge(euk_out, nth + 1)
                    st.tell(dve.tensor_tensor(euv[:], euk[:], kT[:, :, cols], ALU.mult), sums_in, nth + 1)

                def floor():
                    dve.wait_ge(sums_out, nth + 1)
                    st(dve.tensor_scalar(den[:], den[:], 1e-8, None, ALU.max))
                    done["floor"] = st.last

                def invert(q):
                    if q == 0:
                        dve.wait_ge(*done["floor"])
                    part = den[:, q // 2, (q % 2) * P:(q % 2 + 1) * P]
                    st(dve.reciprocal(part, part))
                    done["invert"] = st.last

                def finish():
                    dve.wait_ge(*done["invert"])
                    st(dve.scalar_tensor_tensor(
                        fac[:, bass.ds(i, 1), :, cols].rearrange("p i c t -> p (i c) t"), num[:],
                        oscale[:, bass.ds(b, 1)], den[:], ALU.mult, ALU.mult))
                    st.settle()

                return [*([] if early else [shifted]), lambda: forward(num, ekv), lambda: forward(den, ek),
                        lambda: stage(ekv), lambda: backward(backn), lambda: stage(ek), lambda: backward(backd),
                        early_own_term if early else own_term, floor, *(lambda q=q: invert(q) for q in range(4)), finish]

            for step in slice_steps(0, 0):
                step()

            def condition_batch(b, which, count):
                dve.wait_ge(sig_ready, count)
                st.tell(dve.tensor_tensor(xc[:], sig[:], fac[:, which, :, bass.ds(b * T, T)], ALU.mult),
                        xc_ready, count)

            condition_batch(0, 0, 1)
            with st.loop(B, OWN0) as b:

                def scaled_qk(tt, event):
                    dve.wait_ge(projected, b * PROJ0 + 3 + 3 * tt)
                    st(dve.tensor_scalar(qk[:, tt, 0], ps[:, 2 * tt, 0:C], HD0 ** -0.5, None, ALU.mult))
                    st.tell(dve.tensor_copy(qk[:, tt, 1], ps[:, 2 * tt, C:]), evac_d, b * EVD0 + event)

                scaled_qk(0, 1)
                dve.wait_ge(projected, b * PROJ0 + 5)
                flat = mixw.rearrange("p t c i m -> p (t c) i m")
                st.tell(dve.tensor_copy(mixw.rearrange("p t c i m -> p (t c i m)"), ps[:, 6]), evac_d, b * EVD0 + 2)
                st.settle()
                st(dve.tensor_tensor(sq, flat[:, :, 0:2], flat[:, :, 0:2], ALU.mult))
                st.settle()
                st(dve.tensor_reduce(ms, sq, X, ALU.add))
                st.settle()
                st.tell(dve.tensor_scalar(ms, ms, 1.0 / N0, 1e-6, ALU.mult, ALU.add), norm_in, b + 1)
                scaled_qk(1, 3)
                st.settle()
                dve.wait_ge(evac_a, b * EVA0 + 6)

                def heads(ap):
                    return ap.rearrange("p (n h) -> p n h", h=HD0)

                for tt in range(TT):
                    q, k = heads(qk[:, tt, 0]), heads(qk[:, tt, 1])
                    st(dve.scalar_tensor_tensor(qs[:, tt, :, 0], spread(dd[:, tt, 0:16], 2, HD0), 1.0, q,
                                                ALU.add, ALU.mult))
                    st(dve.tensor_copy(qs[:, tt, :, 1], q))
                    st(dve.tensor_copy(ks[:, tt, :, 0], k))
                    st.tell(dve.tensor_tensor(ks[:, tt, :, 1], k, spread(dd[:, tt, 16:32], 2, HD0), ALU.mult),
                            stacked, b * 4 + tt + 1)
                dve.wait_ge(norm_out, b + 1)
                st.tell(dve.tensor_tensor(flat[:, :, 0:2], flat[:, :, 0:2], spread(ms, 3, N0), ALU.mult),
                        mix_ready, b + 1)
                st.settle()
                for tt in range(TT):
                    q, k = heads(qk[:, tt, 0]), heads(qk[:, tt, 1])
                    st(dve.tensor_tensor(qw[:, tt].rearrange("p i (n h) -> p i n h", h=HD0), spread(q, 1, 2),
                                         spread(mixw[:, tt, 0, 0:2], 3, HD0), ALU.mult))
                    st.tell(dve.tensor_tensor(kw[:, tt].rearrange("p i (n h) -> p i n h", h=HD0), spread(k, 1, 2),
                                              spread(mixw[:, tt, 1, 0:2], 3, HD0), ALU.mult),
                            stacked, b * 4 + tt + 3)
                for tt in range(TT):
                    v = heads(v0[:, tt])
                    st(dve.tensor_copy(vs[:, tt, :, 0], v))
                    st(dve.tensor_tensor(vs[:, tt, :, 1], v, spread(dd[:, tt, 48:64], 2, HD0), ALU.mult))
                    ins = dve.tensor_tensor(vk[:, tt].rearrange("p i (n h) -> p i n h", h=HD0), spread(v, 1, 2),
                                            spread(mixw[:, tt, 3, 2:4], 3, HD0), ALU.mult)
                    if tt:
                        st.tell(ins, values_ready, b + 1)
                    else:
                        st(ins)
                for u in range(1, 10, 2):
                    dve.wait_ge(projected, b * PROJ0 + 8 + u)
                    st.tell(dve.tensor_copy(turned(u), turned_bank(u)), evac_d, b * EVD0 + 4 + u // 2)
                dve.wait_ge(projected, b * PROJ0 + 18)
                st.tell(dve.tensor_copy(rankq[:, 0], ps[:, 2, 0:384]), evac_d, b * EVD0 + 9)
                dve.wait_ge(projected, b * PROJ0 + 20)
                st.tell(dve.tensor_copy(rankkT[:, 0], ps[:, 4, 0:384]), evac_d, b * EVD0 + 10)
                st.settle()
                dve.wait_ge(evac_a, b * EVA0 + 12)
                tiles = (slice(0, P), slice(P, 384))

                def logits(n):
                    s = n % 2
                    dve.wait_ge(s_ready, b * N0 + n + 1)
                    if n >= 2:
                        dve.wait_ge(p_exp, b * N0 + n - 1)
                    for tt in range(TT):
                        ins = dve.scalar_tensor_tensor(logit[:, s, tiles[tt]], rankq[:, 0, tiles[tt]],
                                                       mixw[:, tt, 0, 2, n:n + 1], ps[:, s, tiles[tt]],
                                                       ALU.mult, ALU.add)
                    st.tell(ins, s_read, b * N0 + n + 1)
                    st.settle()
                    for tt in range(TT):
                        ins = dve.scalar_tensor_tensor(logit[:, s, tiles[tt]], rankq[:, 1, tiles[tt]],
                                                       mixw[:, tt, 0, 3, n:n + 1], logit[:, s, tiles[tt]],
                                                       ALU.mult, ALU.add)
                    st(ins)
                    st.settle()
                    for tt in range(TT):
                        ins = dve.tensor_reduce(nmax[:, s, tt:tt + 1], logit[:, s, tiles[tt]], X, ALU.max, negate=True)
                    st.tell(ins, lmax, b * N0 + n + 1)

                def invert(n):
                    dve.wait_ge(p_exp, b * N0 + n + 1)
                    st.tell(dve.reciprocal(rinv[:, n % 2], rsum[:, n % 2]), r_ready, b * N0 + n + 1)

                def mix(n):
                    dve.wait_ge(p_norm, b * N0 + n + 1)
                    if n >= N0 - 2:
                        dve.wait_ge(h_done, b * N0 + n)
                    for i in range(2):
                        for tt in range(TT):
                            w = mixw[:, tt, 2, i, n:n + 1]
                            dst = mixq[:, i, tiles[tt]]
                            if n == 0:
                                ins = dve.tensor_scalar(dst, prob[:, n % 3, tiles[tt]], w, None, ALU.mult)
                            else:
                                ins = dve.scalar_tensor_tensor(dst, prob[:, n % 3, tiles[tt]], w, dst, ALU.mult, ALU.add)
                    st.tell(ins, h_done, b * N0 + n + 1)

                one, two = slice_steps(b * 2 + 1, b * 2 + 1), slice_steps(b * 2 + 2, b * 2 + 2)
                extra = {0: one[0:2], 1: one[2:4], 2: one[4:6], 3: one[6:7], 4: one[7:8], 7: one[8:11], 8: one[11:],
                         9: two[0:2], 10: two[2:4], 11: two[4:6], 12: two[6:7], 13: two[7:8], 16: two[8:11],
                         17: two[11:]}
                for k in range(N0 + 2):
                    if k < N0:
                        logits(k)
                    if 1 <= k <= N0:
                        invert(k - 1)
                    if k >= 2:
                        mix(k - 2)
                    for step in extra.get(k, []):
                        step()

                condition_batch((b + 1) & (B - 1), 0, b + 2)
                for i in range(2):
                    dve.wait_ge(tail_pe, b * TAIL0 + 1 + i)
                    st.tell(dve.tensor_copy(mixqT[:, i], ps[:, i, 0:384]), tail_dve, b * 4 + 1 + i)
                dve.wait_ge(tail_pe, b * TAIL0 + 6)
                own = [ps[:, 4 + tt].rearrange("p (n e h) -> p e n h", e=2, h=HD0) for tt in range(TT)]
                for tt in range(TT):
                    st(dve.scalar_tensor_tensor(heads(o_tok[:, tt]), spread(dd[:, tt, 32:48], 2, HD0), 1.0,
                                                own[tt][:, 0], ALU.add, ALU.mult))
                for i in range(2):
                    for tt in range(TT):
                        st(dve.tensor_tensor(heads(o_tmp[:, tt]), heads(ps[:, tt, i * C:(i + 1) * C]),
                                             spread(mixw[:, tt, 2, 2 + i], 2, HD0), ALU.mult))
                    st.settle()
                    for tt in range(TT):
                        st(dve.tensor_tensor(o_tok[:, tt], o_tok[:, tt], o_tmp[:, tt], ALU.add))
                    st.settle()
                for tt in range(TT):
                    st(dve.tensor_tensor(heads(o_tok[:, tt]), heads(o_tok[:, tt]), own[tt][:, 1], ALU.add))
                st.settle()
                dve.wait_ge(tail_pe, b * TAIL0 + 7)
                for tt in range(TT):
                    ins = dve.tensor_tensor(o_tok[:, tt], o_tok[:, tt], ps[:, 2, tt * C:(tt + 1) * C], ALU.add)
                    if tt:
                        st.tell(ins, tail_dve, b * 4 + 3)
                    else:
                        st(ins)
                dve.wait_ge(tail_pe, b * TAIL0 + 8)
                st.tell(dve.tensor_copy(oT.rearrange("p a t -> p (a t)"), ps[:, 3]), tail_dve, b * 4 + 4)
                dve.wait_ge(tail_pe, b * TAIL0 + 9)
                here = xT[:, :, bass.ds(b * T, T)]
                st.tell(dve.tensor_tensor(here, here, ps[:, 7].rearrange("p (m t) -> p m t", m=CT), ALU.add),
                        x_done, b + 1)

            def condition_all(which, act_done, done):
                dve.wait_ge(route_act, act_done)
                st.tell(dve.tensor_tensor(hT[:], hT[:], fac[:, which], ALU.mult), h_ready, done)

            def softmax_rows(lg, pr, mx, told, act_done):
                n = pr.shape[2]
                st(dve.tensor_reduce(mx, lg[:, :, 0:n], X, ALU.max))
                st.settle()
                st.tell(dve.tensor_tensor(pr, lg[:, :, 0:n], spread(mx, 2, n), ALU.subtract), route_dve, told)
                dve.wait_ge(route_act, act_done)
                st(dve.tensor_reduce(mx, pr, X, ALU.add))
                st.settle()
                st(dve.reciprocal(mx, mx))
                st.settle()
                st(dve.tensor_tensor(pr, pr, spread(mx, 2, n), ALU.mult))
                st.settle()

            def choose(pr, top, idf):
                for tau in range(TAU):
                    st(dve.max(top[:, tau], pr[:, tau]))
                st.settle()
                for tau in range(TAU):
                    st(dve.max_index(idx0[:, tau], top[:, tau], pr[:, tau]))
                st.settle()
                st(dve.tensor_copy(idf, idx0[:]))
                st.settle()

            def weigh(top, idf, comb, oh, ia, kk):
                n = oh.shape[2]
                for k in range(kk):
                    st(dve.tensor_tensor(oh, spread(ia, 1, TAU), spread(idf[:, :, k], 2, n), ALU.is_equal))
                    st.settle()
                    st(dve.tensor_tensor(comb if k == 0 else oh, oh, spread(top[:, :, k], 2, n), ALU.mult))
                    st.settle()
                    if k:
                        st(dve.tensor_tensor(comb, comb, oh, ALU.add))
                        st.settle()

            for i, cols in ((2, slice(T, NT)), (3, slice(0, NT))):
                for c in range(CT):
                    ins = dve.tensor_scalar(fac[:, i, c, cols], kT[:, c, cols], wu[:, 1, i, c:c + 1], 30.0,
                                            ALU.add, ALU.min)
            st.tell(ins, euk_in, EARLY)
            condition_all(1, 1, 1)
            st.settle()
            st(dve.tensor_copy(hTs0[:, 0], hT[:]))
            st.settle()
            st.tell(dve.tensor_tensor(hTs0[:, 1], hT[:], hTs0[:, 0], ALU.subtract), hs0_ready, 1)
            dve.wait_ge(ld["moe0"], 32)
            dve.wait_ge(route_pe, 1)
            st.tell(dve.tensor_copy(lg0, ps[:, 0].rearrange("p (a n) -> p a n", n=64)[:, :, 0:E0 + 1]), route_dve, 1)
            st.settle()
            softmax_rows(lg0, pr0, mx0, 2, 2)
            choose(pr0, top0, idf0)
            st(dve.tensor_reduce(mx0, top0[:, :, 0:K0], X, ALU.add))
            st.settle()
            st(dve.tensor_scalar(mx0, mx0, 1e-9, None, ALU.max))
            st.settle()
            st(dve.reciprocal(mx0, mx0))
            st.settle()
            st(dve.tensor_tensor(top0, top0, spread(mx0, 2, 8), ALU.mult))
            st.settle()
            weigh(top0, idf0, comb0[:, :, 0:E0], oh0, iota, K0)
            dve.wait_ge(route_act, 3)
            st(dve.tensor_copy(comb0[:, :, E0 + 1:], spread(comb0[:, :, E0], 2, SH0 - 1)))
            st.settle()
            dve.wait_ge(euk_out, EARLY)

            def gated_unit(i, u):
                slot, tau = divmod(u, TAU)
                unit = i * UNITS + u + 1
                dve.wait_ge(silu_done, unit)
                st.tell(dve.scalar_tensor_tensor(mid0[:, u % 2], gate_up(u)[:, I0:2 * I0],
                                                 comb0[:, tau, bass.ds(2 * i + slot, 1)], act0[:, u % 2],
                                                 ALU.mult, ALU.mult), up_read, unit)
                if u >= 4:
                    dve.wait_ge(midT_ready, unit - 4)
                st.settle()
                st(dve.tensor_copy(mids[:, u % 4, 0], mid0[:, u % 2]))
                st.settle()
                st.tell(dve.tensor_tensor(mids[:, u % 4, 1], mid0[:, u % 2], mids[:, u % 4, 0], ALU.subtract),
                        mid_done, unit)

            with st.loop(LATE, UNITS + SLICE_OWN) as i:
                steps = slice_steps(i + FIRST_LATE, i + FIRST_LATE, early=True)
                extra = dict(zip((0, 1, 2, 3, 4, 5, 6, 9, 10, 11, 12, 13, 14), steps))
                for u in range(UNITS):
                    if u in extra:
                        extra[u]()
                    gated_unit(i, u)
            with st.loop(EX0 // 2 - LATE, UNITS) as j:
                for u in range(UNITS):
                    gated_unit(j + LATE, u)
            dve.wait_ge(y_ready, 1)
            for m in range(CT):
                here = xT[:, m].rearrange("p (a t) -> p a t", a=2)
                ins = dve.tensor_tensor(here, here, ps[:, 4 + 2 * m:6 + 2 * m], ALU.add)
                if m:
                    st.tell(ins, x_done, B + 1)

            condition_batch(0, 2, B + 2)
            dve.wait_ge(ld["attn1"], 80)
            with st.loop(B, OWN1) as b:
                for tt in range(TT):
                    dve.wait_ge(proj1_pe, b * 6 + tt + 1)
                    st(dve.tensor_copy(raw1[:, tt], ps[:, tt, 0:320]))
                    st(dve.tensor_copy(v1[:, tt], ps[:, tt, 320:384]))
                st.settle()
                dve.wait_ge(vz_zeroed, 1)
                for r in range(REP):
                    st(dve.tensor_copy(vz[:, :, :, r, r * HD1:(r + 1) * HD1],
                                       v1.rearrange("p t (j d) -> p t j d", d=HD1)))
                x0, x1 = (raw1.rearrange("p t (g d e) -> p t g d e", d=4, e=2)[:, :, :, :, e] for e in range(2))
                r0, r1 = (rot1.rearrange("p t (g d e) -> p t g d e", d=4, e=2)[:, :, :, :, e] for e in range(2))
                tmp = rtmp.rearrange("p t (g d) -> p t g d", d=4)
                for tt in range(TT):
                    c, s = spread(cosk[:, tt], 1, 40), spread(sink[:, tt], 1, 40)
                    st(dve.tensor_tensor(tmp[:, tt], x1[:, tt], s, ALU.mult))
                    st(dve.tensor_tensor(r0[:, tt], x0[:, tt], c, ALU.mult))
                    st.settle()
                    st(dve.tensor_tensor(r0[:, tt], r0[:, tt], tmp[:, tt], ALU.subtract))
                    st.settle()
                    st(dve.tensor_tensor(tmp[:, tt], x1[:, tt], c, ALU.mult))
                    st(dve.tensor_tensor(r1[:, tt], x0[:, tt], s, ALU.mult))
                    st.settle()
                    st(dve.tensor_tensor(r1[:, tt], r1[:, tt], tmp[:, tt], ALU.add))
                    st.settle()
                for tt in range(TT):
                    ins = dve.tensor_copy(krep[:, tt].rearrange("p (j r d) -> p j r d", r=REP, d=HD1),
                                          spread(rot1[:, tt, C:].rearrange("p (j d) -> p j d", d=HD1), 2, REP))
                st.tell(ins, attn1_dve, b * 4 + 1)
                dve.wait_ge(proj1_pe, b * 6 + 4)
                st.tell(dve.tensor_copy(k1T.rearrange("p a t -> p (a t)"), ps[:, 3]), attn1_dve, b * 4 + 2)

                def maxima(n):
                    s = n % 4
                    dve.wait_ge(s1_ready, b * N1 + n + 1)
                    for tt in range(TT):
                        ins = dve.tensor_reduce(nmax1[:, s, tt:tt + 1], ps[:, 2 + s, tt * P:P + 2 * tt * P], X,
                                                ALU.max, negate=True)
                    st(ins)
                    st.settle()
                    st.tell(dve.tensor_scalar(nmax1[:, s], nmax1[:, s], HD1 ** -0.5, None, ALU.mult),
                            lmax1, b * N1 + n + 1)

                def turn_out(n):
                    dve.wait_ge(t1_ready, b * N1 + n + 1)
                    if n >= 2:
                        dve.wait_ge(pv1_done, b * N1 + n - 1)
                    st.tell(dve.tensor_copy(prob1T[:, n % 2], ps[:, n % 2, 0:384]), t1_read, b * N1 + n + 1)

                for k in range(N1 + 2):
                    if k < N1:
                        maxima(k)
                    if k >= 2:
                        turn_out(k - 2)
                condition_batch((b + 1) & (B - 1), 2, B + b + 3)
                st(dve.reciprocal(rinv1, rsum1))
                st.settle()
                for tt in range(TT):
                    ins = dve.tensor_copy(rrep[:, tt].rearrange("p (n h) -> p n h", h=HD1),
                                          spread(rinv1[:, :, tt], 2, HD1))
                st.tell(ins, attn1_dve, b * 4 + 3)
                dve.wait_ge(proj1_pe, b * 6 + 5)
                st(dve.tensor_copy(rT.rearrange("p a t -> p (a t)"), ps[:, 7]))
                st.settle()
                dve.wait_ge(pv1_done, b * N1 + N1)
                st.tell(dve.tensor_tensor(o1T.rearrange("p a t -> p (a t)"), rT.rearrange("p a t -> p (a t)"), ps[:, 6],
                                          ALU.mult), attn1_dve, b * 4 + 4)
                dve.wait_ge(proj1_pe, b * 6 + 6)
                here = xT[:, :, bass.ds(b * T, T)]
                st.tell(dve.tensor_tensor(here, here, ps[:, 2].rearrange("p (m t) -> p m t", m=CT), ALU.add),
                        x_done, B + b + 2)

            condition_all(3, 4, 2)
            st.settle()
            st(dve.tensor_copy(hTs[:, 0], hT[:]))
            st.settle()
            st.tell(dve.tensor_tensor(hTs[:, 1], hT[:], hTs[:, 0], ALU.subtract), h_ready, 3)
            dve.wait_ge(ld["moe1"], 7 * 16)
            dve.wait_ge(route_pe, 2)
            st(dve.tensor_tensor(lg1, ps[:, 0].rearrange("p (a n) -> p a n", n=64)[:, :, 0:E1], spread(bg1, 1, TAU),
                                 ALU.add))
            st.settle()
            softmax_rows(lg1, pr1, mx1, 3, 5)
            choose(pr1, top1, idf1)
            weigh(top1, idf1, comb1, oh1, iota1, K1)
            with st.loop(E1 // 2, OWN3) as i:
                st(dve.tensor_scalar(biases[:, 0], b1[:, bass.ds(2 * i, 2)], 1.0, None, ALU.mult))
                st.tell(dve.tensor_scalar(biases[:, 1], b2[:, bass.ds(2 * i, 2)], 1.0, None, ALU.mult),
                        bias_ready, i + 1)
                st.tell(dve.tensor_scalar(pair, comb1[:, :, bass.ds(2 * i, 2)], 1.0, None, ALU.mult), pair_ready, i + 1)

                def split_hidden(k):
                    layer, half, m = k // 8 % 2, k // 4 % 2, k % 4
                    dst = (h1, h2)[layer][:, half]
                    dve.wait_ge(l_read, i * 32 + k + 1)
                    st(dve.tensor_copy(dst[:, 0, m], hfull[:, k % 4]))
                    st.settle()
                    st.tell(dve.tensor_tensor(dst[:, 1, m], hfull[:, k % 4], dst[:, 0, m], ALU.subtract),
                            h_split, i * 32 + k + 1)

                for slot in range(2):
                    for k in range(slot * 16, slot * 16 + 16):
                        split_hidden(k)
                        if k == 7:
                            dve.wait_ge(turned_ready, i + 1)
                            st.tell(dve.tensor_copy(combT[0:2, :].rearrange("p (a t) -> p a t", a=2), ps[0:2, 4:6]),
                                    rows_ready, i + 1)
                        if k == 11:
                            dve.wait_ge(wb_ready, i + 1)
                            st.tell(dve.tensor_copy(weight.rearrange("p e (a t) -> p (e a) t", a=2), ps[:, 4:8]),
                                    wb_read, i + 1)
                    for half in range(2):
                        for m in range(CT):
                            y = i * 8 + slot * 4 + half * 2 + m
                            cols = slice(half * 512, (half + 1) * 512)
                            dve.wait_ge(y1_ready, y + 1)
                            st.tell(dve.scalar_tensor_tensor(scaled[:, m], ps[:, 4 + 2 * half + m],
                                                             b3[:, bass.ds(2 * i + slot, 1), m],
                                                             weight[:, slot, cols], ALU.add, ALU.mult), y1_read, y + 1)
                            st.settle()
                            st(dve.tensor_tensor(xT[:, m, cols], xT[:, m, cols], scaled[:, m], ALU.add))
                            st.settle()
            dve.tensor_copy(small[:, 0:1], xT[:, 0, 0:1]).then_inc(x_done, 1)

        @block.tensor
        def _(pe):

            def mm(o, l, r, start=True, stop=True, shared=False):
                return pe.matmul(o, l, r, start=start, stop=stop, skip_group_check=shared)

            pe.wait_ge(ld["x"], 32)
            pe.wait_ge(ld["attn0"], 128)
            with pe.Fori(0, B) as b:
                pe.wait_ge(xc_ready, b + 1)
                for c in range(4):
                    for k in range(CT):
                        ins = mm(ps[:, 4 + c // 2, (c % 2) * T:(c % 2 + 1) * T], dw1[:, k, c * P:(c + 1) * P],
                                 xc[:, k], k == 0, k == CT - 1)
                    if c % 2:
                        ins.then_inc(projected, 1)
                for tt in range(TT):
                    tok = slice(tt * P, (tt + 1) * P)
                    for o, w in ((ps[:, 2 * tt], wqkv[:, :, 0:2 * C]), (ps[:, 2 * tt + 1, 0:C], wqkv[:, :, 2 * C:]),
                                 (ps[:, 2 * tt + 1, C:C + 64], ddw)):
                        for k in range(CT):
                            ins = mm(o, xc[:, k, tok], w[:, k], k == 0, k == CT - 1)
                        if w is not ddw and w.shape[2] == C:
                            continue
                        ins.then_inc(projected, 1)
                    if tt == 0:
                        pe.wait_ge(evac_a, b * EVA0 + 2)
                        for t2 in range(TT):
                            for c in range(4):
                                ins = mm(ps[:, 6, t2 * 256 + c * 64:t2 * 256 + (c + 1) * 64],
                                         hid[:, c, t2 * P:(t2 + 1) * P], qkw[:, c])
                        ins.then_inc(projected, 1)
                for u in range(10):
                    tt, kind = TURNS[u]
                    if u in (0, 3, 6, 8):
                        pe.wait_ge(stacked, b * 4 + 1 + (0, 3, 6, 8).index(u))
                    if u == 8:
                        pe.wait_ge(evac_a, b * EVA0 + 7)
                    if u == 9:
                        pe.wait_ge(evac_d, b * EVD0 + 4)
                    src = (qs[:, tt].rearrange("p n e h -> p (n e h)"), ks[:, tt].rearrange("p n e h -> p (n e h)"),
                           qw[:, tt].rearrange("p i c -> p (i c)"), kw[:, tt].rearrange("p i c -> p (i c)"),
                           qk[:, tt].rearrange("p i c -> p (i c)"))[kind]
                    for g in range(4):
                        ins = pe.transpose(ps[:, u % 8, g * P:(g + 1) * P], src[:, g * P:(g + 1) * P], ident[:])
                    ins.then_inc(projected, 1)
                pe.wait_ge(evac_a, b * EVA0 + 11)
                pe.wait_ge(evac_d, b * EVD0 + 8)
                for i in range(2):
                    for tt in range(TT):
                        for k in range(CT):
                            ins = mm(ps[:, 2 + i, tt * P:P + tt * 2 * P], qwT[:, 2 * i + k, tt * P:(tt + 1) * P],
                                     kTb[:, k, 0:(tt + 1) * P], k == 0, k == CT - 1)
                    ins.then_inc(projected, 1)
                for i in range(2):
                    for s in range(TT):
                        for k in range(CT):
                            ins = mm(ps[:, 4 + i, s * 256:s * 256 + (2 - s) * P], kwT[:, 2 * i + k, s * P:(s + 1) * P],
                                     qT[:, k, s * P:], k == 0, k == CT - 1)
                    ins.then_inc(projected, 1)
                pe.wait_ge(evac_a, b * EVA0 + 13)
                pe.wait_ge(evac_d, b * EVD0 + 10)

                def scores(n):
                    pe.wait_ge(dg_pre, b * N0 + n + 1)
                    if n >= 2:
                        pe.wait_ge(s_read, b * N0 + n - 1)
                    rows, g = slice(32 * (n % 4), 32 * (n % 4) + 32), n // 4
                    o = ps[:, n % 2]
                    mm(o[:, 0:P], qsT[rows, g, 0:P], ksT[rows, g, 0:P], True, False, True)
                    mm(o[:, P:384], qsT[rows, g, P:], ksT[rows, g], False, False, True)
                    for blk in (0, 2):
                        mm(o[:, blk * P:(blk + 1) * P], identb[:], causal[:], False, False, True)
                    for blk, (tt, s) in enumerate(CAUSAL):
                        for i in range(2):
                            ins = mm(o[:, blk * P:(blk + 1) * P], rankkT[:, i, blk * P:(blk + 1) * P],
                                     diag_pre[:, n % 4, 2 * s + i], False, blk == 2 and i == 1, True)
                    ins.then_inc(s_ready, 1)

                def turn(n):
                    pe.wait_ge(p_norm, b * N0 + n + 1)
                    if n >= 2:
                        pe.wait_ge(t_read, b * N0 + n - 1)
                    for blk in range(3):
                        ins = pe.transpose(ps[:, 2 + n % 2, blk * P:(blk + 1) * P],
                                           prob[:, n % 3, blk * P:(blk + 1) * P], ident[:])
                    ins.then_inc(t_ready, 1)

                def values(n):
                    pe.wait_ge(t_read, b * N0 + n + 1)
                    pe.wait_ge(dg_post, b * N0 + n + 1)
                    if n == 0:
                        pe.wait_ge(values_ready, b + 1)
                    pT = probT[:, n % 2]
                    vals = vs.rearrange("p t n e h -> p t n (e h)")
                    o = ps[32 * (n % 4):32 * (n % 4) + 32, 4 + n // 8, (n // 4 % 2) * T:(n // 4 % 2 + 1) * T]
                    mm(o, vals[:, 0, n], pT[:, 0:2 * P], True, False, True)
                    mm(o[:, P:], vals[:, 1, n], pT[:, 2 * P:], False, True, True)
                    d0 = diag_post[:, n % 4, 0:2].rearrange("p i j -> p (i j)")
                    d1 = diag_post[:, n % 4, 2:4].rearrange("p i j -> p (i j)")
                    last = n == N0 - 1
                    mm(ps[:, 6, 0:256], pT[:, 0:P], d0, n == 0, last, True)
                    mm(ps[:, 7, 0:256], pT[:, P:2 * P], d0, n == 0, last, True)
                    mm(ps[:, 7, 256:512], pT[:, 2 * P:], d1, False, last, True).then_inc(pv_done, 1)

                for k in range(N0 + 3):
                    if k < N0:
                        scores(k)
                    if 2 <= k <= N0 + 1:
                        turn(k - 2)
                    if k >= 3:
                        values(k - 3)

                pe.wait_ge(h_done, b * N0 + N0)
                pe.wait_ge(s_read, b * N0 + N0)
                for i in range(2):
                    for blk in range(3):
                        ins = pe.transpose(ps[:, i, blk * P:(blk + 1) * P], mixq[:, i, blk * P:(blk + 1) * P], ident[:])
                    ins.then_inc(tail_pe, 1)
                pe.wait_ge(tail_act, b * 5 + 2)
                for i in range(2):
                    for blk in range(3):
                        src = (0, 256, 512)[blk] + i * P
                        ins = pe.transpose(ps[:, 2 + i, blk * P:(blk + 1) * P], mixk[:, src:src + P], ident[:])
                    ins.then_inc(tail_pe, 1)
                pe.wait_ge(tail_act, b * 5 + 3)
                for tt in range(TT):
                    for g in range(4):
                        pe.transpose(ps[:, 4 + tt, g * P:(g + 1) * P], owT[:, g, tt * P:(tt + 1) * P], ident[:])
                pe.wait_ge(tail_dve, b * 4 + 2)
                for tt in range(TT):
                    for i in range(2):
                        for s in range(tt + 1):
                            blk = tt + s
                            ins = mm(ps[:, tt, i * C:(i + 1) * C], mixqT[:, i, blk * P:(blk + 1) * P], v0[:, s],
                                     s == 0, s == tt)
                    ins.then_inc(tail_pe, 1)
                pe.wait_ge(tail_act, b * 5 + 5)
                for tt in range(TT):
                    terms = [(i, s) for i in range(2) for s in range(tt + 1)]
                    for j, (i, s) in enumerate(terms):
                        blk = tt + s
                        ins = mm(ps[:, 2, tt * C:(tt + 1) * C], mixkT[:, i, blk * P:(blk + 1) * P], vk[:, s, i],
                                 j == 0, j == len(terms) - 1)
                ins.then_inc(tail_pe, 1)
                pe.wait_ge(tail_dve, b * 4 + 3)
                for k in range(CT):
                    for tt in range(TT):
                        ins = pe.transpose(ps[:, 3, (k * TT + tt) * P:(k * TT + tt + 1) * P],
                                           o_tok[:, tt, k * P:(k + 1) * P], ident[:])
                ins.then_inc(tail_pe, 1)
                pe.wait_ge(tail_dve, b * 4 + 4)
                for m in range(CT):
                    for k in range(CT):
                        ins = mm(ps[:, 7, m * T:(m + 1) * T], wo0[:, k, m * P:(m + 1) * P], oT[:, k], k == 0, k == CT - 1)
                ins.then_inc(tail_pe, 1)

            def route(w, n, conditioned):
                pe.wait_ge(h_ready, conditioned)
                for tau in range(TAU):
                    for k in range(CT):
                        ins = mm(ps[:, 0, tau * 64:tau * 64 + n], hT[:, k, tau * P:(tau + 1) * P], w[:, k],
                                 k == 0, k == CT - 1)
                ins.then_inc(route_pe, 1)

            pe.wait_ge(ld["moe0"], 32)
            route(wr0, E0 + 1, 1)
            pe.wait_ge(route_dve, 1)
            pe.wait_ge(hs0_ready, 1)
            pe.wait_ge(zeroed, 1)
            for m in range(4):
                mm(ps[:, 4 + m], zerob[:, 0:P], zerob[:], True, False, True)
            def step(i, u, last=False):
                if u < UNITS or not last:
                    slot, tau = divmod(u % UNITS, TAU)
                    if tau == 0:
                        pe.wait_ge(w0_split, 2 * i + u // TAU + 1)
                    before = {UNITS - 1: UNITS - 3, UNITS: None, UNITS + 1: UNITS - 1, UNITS + 2: None}\
                        .get(u, u - 3 if u >= 3 else None)
                    if before is not None:
                        pe.wait_ge(up_read, i * UNITS + before + 1)
                    for k in range(CT):
                        for a, b in ((0, 0), (0, 1), (1, 0)):
                            ins = mm(gate_up(u)[:, 0:2 * I0], hTs0[:, a, k, tau * P:(tau + 1) * P],
                                     wgus[:, slot, b, k], k + a + b == 0, k == CT - 1 and a == 1)
                    ins.then_inc(gu_ready, 1)
                v = u - 2
                if 0 <= v and (v < UNITS or not last):
                    pe.wait_ge(mid_done, i * UNITS + v + 1)
                    if v >= 1:
                        pe.wait_ge(midT_done, i * UNITS + v)
                    for part in range(2):
                        pe.transpose(turned_parts()[:, 0, part], mids[:, v % 4, part, 0:P], ident16[:])
                        ins = pe.transpose(turned_parts()[0:I0 - P, 1, part], mids[:, v % 4, part, P:I0], ident16[:])
                    ins.then_inc(midT_ready, 1)
                if u in (7, 11, 15, 19):
                    n = (u - 7) // 4
                    slot, half = divmod(n, 2)
                    pe.wait_ge(midT_done, i * UNITS + 4 * n + 4)
                    for m in range(CT):
                        for j, rows in enumerate((slice(0, P), slice(0, I0 - P))):
                            for a, b in ((0, 0), (0, 1), (1, 0)):
                                ins = mm(ps[:, 4 + 2 * m + half], wds[rows, slot, a, j, m * P:(m + 1) * P],
                                         midT[rows, half, j, b], False, False, True)
                    ins.then_inc(down_done, 1)

            for u in range(4):
                step(0, u)
            with pe.Fori(0, EX0 // 2 - 1) as i:
                for u in range(4, UNITS + 4):
                    step(i, u)
            for u in range(4, UNITS + 4):
                step(EX0 // 2 - 1, u, last=True)
            for m in range(4):
                ins = mm(ps[:, 4 + m], zerob[:, 0:P], zerob[:], False, True, True)
            ins.then_inc(y_ready, 1)

            pe.wait_ge(ld["attn1"], 80)
            with pe.Fori(0, B) as b:
                pe.wait_ge(xc_ready, B + b + 2)
                for tt in range(TT):
                    for k in range(CT):
                        ins = mm(ps[:, tt, 0:384], xc[:, k, tt * P:(tt + 1) * P], w1qkv[:, k], k == 0, k == CT - 1)
                    ins.then_inc(proj1_pe, 1)
                pe.wait_ge(attn1_dve, b * 4 + 1)
                for src, bank in ((rot1, 2), (krep, 3)):
                    for k in range(CT):
                        for tt in range(TT):
                            ins = pe.transpose(ps[:, bank, (k * TT + tt) * P:(k * TT + tt + 1) * P],
                                               src[:, tt, k * P:(k + 1) * P], ident[:])
                    ins.then_inc(proj1_pe, 1)
                pe.wait_ge(attn1_dve, b * 4 + 2)
                pe.wait_ge(q1T_ready, b + 1)

                def scores(n):
                    k = n // (P // HD1)
                    pe.wait_ge(kz_ready, b * N1 + n + 1)
                    if n >= 4:
                        pe.wait_ge(p1_exp, b * N1 + n - 3)
                    o = ps[:, 2 + n % 4]
                    mm(o[:, 0:P], q1T[:, k, 0:P], kz[:, n % 4, 0:P], True, False, True)
                    mm(o[:, P:384], q1T[:, k, P:], kz[:, n % 4], False, False, True)
                    mm(o[:, 0:P], identb[:], causal[:], False, False, True)
                    mm(o[:, 256:384], identb[:], causal[:], False, True, True).then_inc(s1_ready, 1)

                def turn(n):
                    pe.wait_ge(p1_exp, b * N1 + n + 1)
                    if n >= 2:
                        pe.wait_ge(t1_read, b * N1 + n - 1)
                    for blk in range(3):
                        ins = pe.transpose(ps[:, n % 2, blk * P:(blk + 1) * P],
                                           prob1[:, n % 4, blk * P:(blk + 1) * P], ident[:])
                    ins.then_inc(t1_ready, 1)

                def values(n):
                    j, r = divmod(n, REP)
                    pe.wait_ge(t1_read, b * N1 + n + 1)
                    pT, o = prob1T[:, n % 2], ps[32 * (j % 4):32 * (j % 4) + 32, 6, (j // 4) * T:(j // 4 + 1) * T]
                    mm(o, vz[:, 0, j, r], pT[:, 0:2 * P], r == 0, False, True)
                    mm(o[:, P:], vz[:, 1, j, r], pT[:, 2 * P:], False, r == REP - 1, True).then_inc(pv1_done, 1)

                for k in range(N1 + 3):
                    if k < N1:
                        scores(k)
                    if 2 <= k <= N1 + 1:
                        turn(k - 2)
                    if k >= 3:
                        values(k - 3)
                pe.wait_ge(attn1_dve, b * 4 + 3)
                for k in range(CT):
                    for tt in range(TT):
                        ins = pe.transpose(ps[:, 7, (k * TT + tt) * P:(k * TT + tt + 1) * P],
                                           rrep[:, tt, k * P:(k + 1) * P], ident[:])
                ins.then_inc(proj1_pe, 1)
                pe.wait_ge(attn1_dve, b * 4 + 4)
                for m in range(CT):
                    for k in range(CT):
                        ins = mm(ps[:, 2, m * T:(m + 1) * T], wo1[:, k, m * P:(m + 1) * P], o1T[:, k], k == 0, k == CT - 1)
                ins.then_inc(proj1_pe, 1)

            pe.wait_ge(ld["moe1"], 7 * 16)
            route(wg1, E1, 2)
            pe.wait_ge(h_ready, 3)
            pe.wait_ge(route_dve, 3)
            with pe.Fori(0, E1 // 2) as i:
                def layer(k0, w, src, nk, between=None):
                    for half in range(2):
                        for m in range(4):
                            k = k0 + half * 4 + m
                            if k >= 4:
                                pe.wait_ge(l_read, i * 32 + k - 3)
                            for c in range(nk):
                                for a, b in ((0, 0), (0, 1), (1, 0)):
                                    ins = mm(ps[:, k % 4], w[:, a, c, m * P:(m + 1) * P], src(half, b, c),
                                             c + a + b == 0, c == nk - 1 and a == 1)
                            ins.then_inc(l_ready, 1)
                        if half == 0 and between:
                            between()

                def rows():
                    pe.wait_ge(rows_ready, i + 1)
                    for r in range(2):
                        for half in range(2):
                            ins = mm(ps[:, 4 + 2 * r + half], sel1[0:2, r], combT[0:2, half * 512:(half + 1) * 512])
                    ins.then_inc(wb_ready, 1)

                for slot in range(2):
                    pe.wait_ge(w_split, 6 * i + 3 * slot + 1)
                    layer(slot * 16, w1s[:, slot], lambda half, b, c: hTs[:, b, c, half * 512:(half + 1) * 512], CT)
                    if slot == 0:
                        pe.wait_ge(pair_ready, i + 1)
                        for tau in range(TAU):
                            ins = pe.transpose(ps[0:2, 4 + tau // 4, (tau % 4) * P:(tau % 4 + 1) * P], pair[:, tau],
                                               ident[:])
                        ins.then_inc(turned_ready, 1)
                    pe.wait_ge(w_split, 6 * i + 3 * slot + 2)
                    pe.wait_ge(h_split, i * 32 + slot * 16 + 4)

                    def second_half():
                        if slot == 0:
                            rows()
                        pe.wait_ge(h_split, i * 32 + slot * 16 + 8)
                    layer(slot * 16 + 8, w2s[:, slot], lambda half, b, c: h1[:, half, b, c], 4, second_half)
                    pe.wait_ge(w_split, 6 * i + 3 * slot + 3)
                    if slot:
                        pe.wait_ge(y1_read, i * 8 + slot * 4)
                    else:
                        pe.wait_ge(wb_read, i + 1)
                    for half in range(2):
                        pe.wait_ge(h_split, i * 32 + slot * 16 + 12 + 4 * half)
                        for m in range(CT):
                            for c in range(4):
                                for a, b in ((0, 0), (0, 1), (1, 0)):
                                    ins = mm(ps[:, 4 + 2 * half + m], w3s[:, slot, a, c, m * P:(m + 1) * P],
                                             h2[:, half, b, c], c + a + b == 0, c == 3 and a == 1)
                            ins.then_inc(y1_ready, 1)


def kernel(**inp):
    from concourse import bacc
    from concourse.bass_utils import run_bass_kernel_spmd
    import ml_dtypes

    a = {k: np.asarray(v) for k, v in inp.items()}

    def tiles(w):
        return np.ascontiguousarray(w.reshape(-1, P, w.shape[-1]).transpose(1, 0, 2))

    def stack(w):
        return np.ascontiguousarray(w.reshape(w.shape[0], -1, P, w.shape[-1]).transpose(0, 2, 1, 3))

    def column(v):
        return np.ascontiguousarray(v.reshape(v.shape[0], -1, P).transpose(2, 0, 1))

    w = np.stack([a[n + "_w"] for n in ("L0_cond", "L0_cond2", "L1_cond", "L1_cond2")])
    u = np.stack([a[n + "_u"] for n in ("L0_cond", "L0_cond2", "L1_cond", "L1_cond2")])

    def cut(w):
        return w.reshape(C, SH0, I0).transpose(1, 0, 2)

    gate = np.concatenate([a["L0_ffn_w_gate"], cut(a["L0_ffn_sh_gate"])])
    up = np.concatenate([a["L0_ffn_w_up"], cut(a["L0_ffn_sh_up"])])
    down = np.concatenate([a["L0_ffn_w_down"], a["L0_ffn_sh_down"].reshape(SH0, I0, C)])
    f4 = np.float32
    freq = 10000.0 ** (-(np.arange(HD1 // 2, dtype=f4) * f4(2.0 / HD1)))
    phase = (np.arange(T, dtype=f4)[:, None] * freq.astype(f4)[None, :]).astype(f4)
    s_after_t = np.arange(P)[None, :] > np.arange(P)[:, None]
    arrays = {
        "xT": tiles(a["x"].reshape(NT, C).T), "fT": tiles(a["fside_BxSxS_0"].reshape(NT, C).T),
        "cond": a["cond_512"], "wu": np.ascontiguousarray(np.stack([column(w), column(u)], 1)),
        "ident": np.eye(P, dtype=f4), "identb": np.eye(P).astype(ml_dtypes.bfloat16),
        "ident16": np.eye(P, dtype=np.float16),
        "causal": np.where(s_after_t, MASKED, 0.0).astype(ml_dtypes.bfloat16),
        "wqkv": tiles(a["L0_attn_w_qkv"]), "dw1": tiles(a["L0_attn_dw1"].reshape(C, 512)),
        "qkw": np.ascontiguousarray(a["L0_attn_qkw"][0].reshape(4, P, 64).transpose(1, 0, 2)),
        "ddw": tiles(a["L0_attn_dd_w"][:, 0]), "wo0": tiles(a["L0_attn_w_o"].T),
        "wr0": tiles(np.concatenate([a["L0_ffn_router_w"].T, a["L0_ffn_sh_gate_w"]], 1)),
        "iota": np.arange(E0, dtype=f4)[None],
        "wgu": stack(np.concatenate([gate, up], 2)), "wd": np.ascontiguousarray(down),
        "w1qkv": tiles(np.concatenate([a["L1_attn_wq"], a["L1_attn_wk"], a["L1_attn_wv"]], 1)),
        "wo1": tiles(a["L1_attn_wo"]),
        "cosk": tiles(np.cos(phase)), "sink": tiles(np.sin(phase)),
        "rmask": (np.arange(P)[:, None] // HD1 == np.arange(P // HD1)[None, :]).astype(f4),
        "wg1": tiles(a["L1_ffn_Wg"]), "bg1": a["L1_ffn_bg"][None],
        "sel1": np.ascontiguousarray(np.broadcast_to(np.eye(P, 2, dtype=f4)[:, :, None], (P, 2, P))),
        "b1": column(a["L1_ffn_b1"]), "b2": column(a["L1_ffn_b2"]), "b3": column(a["L1_ffn_b3"]),
        "w1": stack(a["L1_ffn_W1"]), "w2": stack(a["L1_ffn_W2"]), "w3": stack(a["L1_ffn_W3"]),
    }
    nc = bacc.Bacc("TRN2", target_bir_lowering=False, num_devices=1)
    d = {k: nc.dram_tensor("in_" + k, v.shape, mybir.dt.from_np(v.dtype), kind="ExternalInput").ap()
         for k, v in arrays.items()}
    out = nc.dram_tensor("out", (P, CT, NT), F32, kind="ExternalOutput").ap()
    build(nc, d, out)
    got = run_bass_kernel_spmd(nc, [{"in_" + k: v for k, v in arrays.items()}], core_ids=[0])
    xT = got.results[0]["out"]
    return np.ascontiguousarray(xT.transpose(1, 0, 2).reshape(C, NT).T).reshape(B, T, C)
```
